# Optimizing a Trainium2 kernel written in Bass

```python
import numpy as np
import jax
import jax.numpy as jnp

def _softmax(x, axis=-1):
    return jax.nn.softmax(x, axis=axis)

def _gelu(x):
    return jax.nn.gelu(x, approximate=True)

def _silu(x):
    return jax.nn.silu(x)

def _sigmoid(x):
    return jax.nn.sigmoid(x)

def _layernorm(x, axis=-1, eps=1e-05):
    m = jnp.mean(x, axis=axis, keepdims=True)
    v = jnp.var(x, axis=axis, keepdims=True)
    return (x - m) / jnp.sqrt(v + eps)

def _scatter_add(tgt, idx, src, axis=0):
    return tgt.at[idx].add(src)

def _segment_sum(src, seg, n):
    return jax.ops.segment_sum(src, seg, n)
kernel_name = 'mk_seq_postln_d1_jaxref_r4_318cc2'

def setup_inputs(seed: int=0):
    np.random.seed(seed)
    _w = jnp.asarray

    def _L0_attn_setup():
        import jax, jax.numpy as jnp
        import numpy as np
        key = jax.random.key(seed)
        ks = jax.random.split(key, 5)
        B, S, D = (1, 1024, 512)
        H, Dh = (16, 128)
        scale = 1.0 / np.sqrt(D).astype(np.float32)
        return {'x': jax.random.normal(ks[0], (B, S, D), dtype=jnp.float32), 'W_K': jax.random.normal(ks[1], (H, Dh, D), dtype=jnp.float32) * scale, 'W_Q': jax.random.normal(ks[2], (H, Dh, D), dtype=jnp.float32) * scale, 'W_V': jax.random.normal(ks[3], (H, Dh, D), dtype=jnp.float32) * scale, 'W_O': jax.random.normal(ks[4], (D, H * Dh), dtype=jnp.float32) * scale}
    _L0_attn_in = _L0_attn_setup()

    def _L0_ffn_setup():
        import jax, jax.numpy as jnp
        import numpy as np
        B, T = (1, 128)
        DIM = 512
        MOE_INTER = 352
        N_EXPERTS = 64
        TOPK = 6
        N_SHARED = 2
        SHARED_INTER = N_SHARED * MOE_INTER
        CAPACITY = 128
        ROUTE_SCALE = 1.0
        key = jax.random.key(seed)
        ks = jax.random.split(key, 8)

        def w(k, shape, fan_in):
            return jax.random.normal(k, shape, jnp.float32) * fan_in ** (-0.5)
        return {'x': jax.random.normal(ks[0], (B, T, DIM), jnp.float32), 'gate_w': w(ks[1], (N_EXPERTS, DIM), DIM), 'w1': w(ks[2], (N_EXPERTS, MOE_INTER, DIM), DIM), 'w2': w(ks[3], (N_EXPERTS, DIM, MOE_INTER), MOE_INTER), 'w3': w(ks[4], (N_EXPERTS, MOE_INTER, DIM), DIM), 'sw1': w(ks[5], (SHARED_INTER, DIM), DIM), 'sw2': w(ks[6], (DIM, SHARED_INTER), SHARED_INTER), 'sw3': w(ks[7], (SHARED_INTER, DIM), DIM)}
    _L0_ffn_in = _L0_ffn_setup()
    _d = {'L0_attn_x': _L0_attn_in['x'], 'L0_attn_W_K': _L0_attn_in['W_K'], 'L0_attn_W_Q': _L0_attn_in['W_Q'], 'L0_attn_W_V': _L0_attn_in['W_V'], 'L0_attn_W_O': _L0_attn_in['W_O'], 'L0_ffn_gate_w': _L0_ffn_in['gate_w'], 'L0_ffn_w1': _L0_ffn_in['w1'], 'L0_ffn_w2': _L0_ffn_in['w2'], 'L0_ffn_w3': _L0_ffn_in['w3'], 'L0_ffn_sw1': _L0_ffn_in['sw1'], 'L0_ffn_sw2': _L0_ffn_in['sw2'], 'L0_ffn_sw3': _L0_ffn_in['sw3']}
    _x0 = _d['L0_attn_x']
    _d['L0_attn_x'] = jax.random.normal(jax.random.fold_in(jax.random.key(seed), 1), (1, 2048, 512), dtype=_x0.dtype)
    del _x0
    return _d

def reference(L0_attn_x, L0_attn_W_K, L0_attn_W_Q, L0_attn_W_V, L0_attn_W_O, L0_ffn_gate_w, L0_ffn_w1, L0_ffn_w2, L0_ffn_w3, L0_ffn_sw1, L0_ffn_sw2, L0_ffn_sw3):

    def _L0_attn_ref(x, W_K, W_Q, W_V, W_O):
        import jax, jax.numpy as jnp
        import numpy as np
        b, pos, d_model = x.shape
        d_head = W_K.shape[1]
        k = jnp.einsum('ihd,bpd->biph', W_K, x)
        q = jnp.einsum('ihd,bpd->biph', W_Q, x)
        v = jnp.einsum('ihd,bpd->biph', W_V, x)
        scores = jnp.einsum('biph,biqh->biqp', k, q)
        mask = jnp.tril(jnp.ones((pos, pos), dtype=x.dtype))
        masked = scores * mask - jnp.float32(10000000000.0) * (1.0 - mask)
        attn = jax.nn.softmax(masked / jnp.sqrt(jnp.float32(d_head)), axis=-1)
        z = jnp.einsum('biqp,biph->biqh', attn, v)
        z_flat = jnp.transpose(z, (0, 2, 1, 3)).reshape(b, pos, -1)
        out = jnp.einsum('df,bqf->bqd', W_O, z_flat)
        return out

    def _L0_ffn_ref(x, gate_w, w1, w2, w3, sw1, sw2, sw3):
        import jax, jax.numpy as jnp
        import numpy as np
        B, T = (1, 128)
        DIM = 512
        MOE_INTER = 352
        N_EXPERTS = 64
        TOPK = 6
        N_SHARED = 2
        SHARED_INTER = N_SHARED * MOE_INTER
        CAPACITY = 128
        ROUTE_SCALE = 1.0
        Bb, Tt, D = x.shape
        xf = x.reshape(-1, D)
        N = xf.shape[0]
        logits = xf @ gate_w.T
        scores = jax.nn.softmax(logits, axis=-1)
        gate_vals, idx = jax.lax.top_k(scores, TOPK)
        gate_vals = gate_vals * ROUTE_SCALE
        E = gate_w.shape[0]
        fe = idx.reshape(-1)
        ft = jnp.repeat(jnp.arange(N), TOPK)
        onehot = (fe[:, None] == jnp.arange(E)[None, :]).astype(jnp.int32)
        pos = jnp.take_along_axis(jnp.cumsum(onehot, axis=0) - 1, fe[:, None], axis=1)[:, 0]
        keep = pos < CAPACITY
        buf = jnp.full((E, CAPACITY), N, dtype=jnp.int32)
        buf = buf.at[fe, pos].set(ft.astype(jnp.int32), mode='drop')
        xpad = jnp.concatenate([xf, jnp.zeros((1, D), xf.dtype)], axis=0)
        xe = xpad[buf]
        h = jax.nn.silu(jnp.einsum('ecd,eid->eci', xe, w1)) * jnp.einsum('ecd,eid->eci', xe, w3)
        ye = jnp.einsum('eci,edi->ecd', h, w2)
        pc = jnp.minimum(pos, CAPACITY - 1)
        op = ye[fe, pc] * keep[:, None].astype(ye.dtype)
        routed = (op * gate_vals.reshape(-1)[:, None]).reshape(N, TOPK, D).sum(axis=1)
        z = jax.nn.silu(xf @ sw1.T) * (xf @ sw3.T) @ sw2.T
        return (routed + z).reshape(Bb, Tt, D)
    x = L0_attn_x
    x = _layernorm(x + _L0_attn_ref(x, L0_attn_W_K, L0_attn_W_Q, L0_attn_W_V, L0_attn_W_O), axis=-1)
    x = _layernorm(x + _L0_ffn_ref(x, L0_ffn_gate_w, L0_ffn_w1, L0_ffn_w2, L0_ffn_w3, L0_ffn_sw1, L0_ffn_sw2, L0_ffn_sw3), axis=-1)
    return x

_drawn_inputs = setup_inputs


def setup_inputs(seed=0):
    import zlib

    import numpy as np

    out = dict(_drawn_inputs(seed))
    spreads = {}
    factors = {}
    for name, (base, spread) in spreads.items():
        noise = np.random.default_rng([zlib.crc32(name.encode()), seed]).standard_normal(out[name].shape)
        drawn = base * np.exp(spread * noise) if base else spread * noise
        out[name] = jnp.asarray(drawn.astype(out[name].dtype))
    for name, factor in factors.items():
        out[name] = (out[name] * factor).astype(out[name].dtype)
    return out
```

```python
from contextlib import ExitStack

import numpy as np

import concourse.bass as bass
from concourse import mybir

P = 128
F32 = mybir.dt.float32
F32R = mybir.dt.float32r
BF16 = mybir.dt.bfloat16
I32 = mybir.dt.int32
U32 = mybir.dt.uint32
ALU = mybir.AluOpType
ACT = mybir.ActivationFunctionType
AX_X = mybir.AxisListType.X

SEQ, DM, HEADS, DH = 2048, 512, 16, 128
EXPERTS, INTER, TOPK, CAPACITY = 64, 352, 6, 128
SHARED_PARTS = 2
EPS = 1e-5
MASKED = -1.0e10
LOG_LEAST = -87.3365

DT = DM // P
CHUNK = 512
CHUNKS = SEQ // CHUNK
RPC = CHUNK // P
TILES = SEQ // P
PAIRS = HEADS // 2
SCALE = float(1.0 / np.sqrt(np.float32(DH)))
INTER_TILES = [(0, 128), (128, 128), (256, 96)]
SLOTS = EXPERTS * CAPACITY

PASSES = ((0, 0), (0, 1), (1, 0))


def after(i, per, k):
    return i * per + (per + k)


def wait_apart(eng, waited, sem, value):
    eng.wait_ge(sem, value)
    eng.sem_inc(waited, 1)


def split_x(nc, xT, x_parts):
    with ExitStack() as ctx:
        raw = ctx.enter_context(nc.sbuf_tensor("x_raw", [P, CHUNKS, DT * CHUNK], F32))
        hi = ctx.enter_context(nc.sbuf_tensor("x_split_hi", [P, CHUNKS, DT * CHUNK], F32R))
        lo = ctx.enter_context(nc.sbuf_tensor("x_split_lo", [P, CHUNKS, DT * CHUNK], F32R))
        loaded = [ctx.enter_context(nc.semaphore(f"x_loaded{c}")) for c in range(CHUNKS)]
        hi_made = ctx.enter_context(nc.semaphore("x_hi_made"))
        lo_made = ctx.enter_context(nc.semaphore("x_lo_made"))
        stored = ctx.enter_context(nc.semaphore("x_parts_stored"))
        block = ctx.enter_context(nc.Block())

        @block.sync
        def _(sp):
            for c in range(CHUNKS):
                sp.dma_start(raw[:, c], xT[c]).then_inc(loaded[c], 16)
            for c in range(CHUNKS):
                sp.wait_ge(hi_made, c + 1)
                sp.dma_start(x_parts[c, 0], hi[:, c].bitcast(F32)).then_inc(stored, 16)
                sp.wait_ge(lo_made, c + 1)
                sp.dma_start(x_parts[c, 1], lo[:, c].bitcast(F32)).then_inc(stored, 16)
            sp.wait_ge(stored, 16 * 2 * CHUNKS)

        @block.scalar
        def _(act):
            for c in range(CHUNKS):
                act.wait_ge(loaded[c], 16)
                nc.scalar.activation(hi[:, c], raw[:, c], ACT.Copy).then_inc(hi_made, 1)

        @block.vector
        def _(dve):
            for c in range(CHUNKS):
                dve.wait_ge(loaded[c], 16)
                dve.wait_ge(hi_made, c + 1)
                nc.vector.tensor_tensor(lo[:, c], raw[:, c], hi[:, c].bitcast(F32),
                                        ALU.subtract).then_inc(lo_made, 1)


def attention_plan():
    units = [(h, c) for c in range(CHUNKS) for h in range(2)]
    plan = []
    AHEAD = 2

    def tiles_of(u):
        h, c = units[u]
        n = RPC * (c + 1)
        steps = [("turn", h, c, j) for j in range(min(AHEAD, n))]
        for j in range(n):
            if j + AHEAD < n:
                steps.append(("turn", h, c, j + AHEAD))
            steps.append(("pv", h, c, j))
        return steps

    for u in range(len(units) + 1):
        if u < len(units):
            h, c = units[u]
            if h == 0:
                plan.append(("proj", c))
        behind = tiles_of(u - 1) if u else []
        rows = [("row", *units[u], r) for r in range(RPC)] if u < len(units) else []
        per = -(-len(behind) // RPC)
        for r in range(RPC):
            if rows:
                plan.append(rows[r])
            if u and r == 1:
                plan.append(("norm", *units[u - 1]))
            plan += behind[r * per:(r + 1) * per]
        if u:
            plan.append(("out", *units[u - 1]))
    return plan


def attention(nc, x_parts, w_qkv, z_dram, gathered_x):
    plan = attention_plan()
    BANKS = 4
    TURNS = 3

    jobs = []
    for step in plan:
        if step[0] == "proj":
            c = step[1]
            jobs += [("q", c, 0), ("k", c, 0), ("q", c, 1), ("k", c, 1), ("v", c, 0), ("v", c, 1)]
        if step[0] == "row":
            _, h, c, r = step
            jobs += [("s", h, c, r, kc) for kc in range(c + 1)]
        if step[0] == "norm":
            jobs.append(step)
    assert len(jobs) % BANKS == 0
    job_at = {job: n for n, job in enumerate(jobs)}
    turn_at = {s: n for n, s in enumerate(s for s in plan if s[0] == "turn")}
    pv_at = {("turn", *s[1:]): n for n, s in enumerate(s for s in plan if s[0] == "pv")}
    unit_at = {s[1:]: n for n, s in enumerate(s for s in plan if s[0] == "norm")}
    turns = list(turn_at)
    n_jobs, n_turns, n_units = len(jobs), len(turns), len(unit_at)
    scores_jobs = [j for j in jobs if j[0] == "s"]
    proj_jobs = [j for j in jobs if j[0] in "qkv"]
    exp_at = {j: n for n, j in enumerate(scores_jobs)}
    proj_at = {j: n for n, j in enumerate(proj_jobs)}
    rows = [s[1:] for s in plan if s[0] == "row"]
    row_at = {s: n for n, s in enumerate(rows)}
    n_exp, n_proj, n_rows = len(scores_jobs), len(proj_jobs), len(rows)

    def widths(c, r, kc):
        used = CHUNK if kc < c else (r + 1) * P
        return used, max(used, 2 * P)

    with ExitStack() as ctx:
        def sb(name, shape, dt):
            return ctx.enter_context(nc.sbuf_tensor(name, shape, dt))

        def ps(name, shape, dt=F32):
            return ctx.enter_context(nc.psum_tensor(name, shape, dt))

        def sem(name):
            return ctx.enter_context(nc.semaphore(name))

        x_sb = sb("x_sb", [P, 2, DT, CHUNK], F32R)
        w_raw = sb("w_raw", [P, 2, 6 * DH], F32)
        w_sb = [sb(f"w_{n}", [P, DT, 6 * DH], F32R) for n in ("hi", "lo")]
        q_sb = [sb(f"q_{n}", [P, 2, CHUNK], F32R) for n in ("hi", "lo")]
        k_sb = [sb(f"k_{n}", [P, 2, SEQ], F32R) for n in ("hi", "lo")]
        v_sb = [sb(f"v_{n}", [P, TILES, 2 * DH], F32R) for n in ("hi", "lo")]
        probs = sb("probs", [P, 2, RPC, SEQ], F32)
        pT_sb = [sb(f"pT_{n}", [P, TURNS, CHUNK], F32R) for n in ("hi", "lo")]
        diag = [sb(f"diag_{n}", [P, RPC, P], F32R) for n in ("hi", "lo")]
        spread_sb = sb("spread_sb", [P, CHUNK], F32)
        z_sb = sb("z_sb", [P, 2, CHUNK], F32)
        ident = sb("ident", [P, P], F32)
        ident_bf = sb("ident_bf", [P, P], BF16)
        causal_bf = sb("causal_bf", [P, P], BF16)
        ones = sb("ones", [P, P], F32R)
        zeros = sb("zeros", [P, P], F32)
        max_part = sb("max_part", [P, 2, CHUNKS], F32)
        row_max = sb("row_max", [P, 2], F32)
        neg_max = sb("neg_max", [P, 2], F32)
        sums = sb("sums", [P, 2, RPC, CHUNKS], F32)
        total = sb("total", [P, 2, RPC], F32)
        inv = sb("inv", [P, 2, RPC], F32)

        bank = ps("bank", [P, BANKS, CHUNK])
        turned = ps("turned", [P, TURNS, CHUNK])
        z_ps = ps("z_ps", [P, CHUNK])

        const_step = sem("const_step")
        pool_const = sem("pool_const")
        act_const = sem("act_const")
        dve_const = sem("dve_const")
        x_in = sem("x_in")
        w_in = [sem(f"w_in{n}") for n in range(2)]
        w_hi_made = sem("w_hi_made")
        w_split = sem("w_split")
        job_ready = sem("job_ready")
        proj_hi = sem("proj_hi")
        proj_lo = sem("proj_lo")
        part_done = sem("part_done")
        max_done = sem("max_done")
        bias_done = sem("bias_done")
        exp_done = sem("exp_done")
        turn_ready = sem("turn_ready")
        turn_hi = sem("turn_hi")
        turn_lo = sem("turn_lo")
        pv_done = sem("pv_done")
        sum_step = sem("sum_step")
        diag_done = sem("diag_done")
        spread_done = sem("spread_done")
        z_done = sem("z_done")
        z_out = [sem(f"z_out{n}") for n in range(2)]
        zero_out = sem("zero_out")
        block = ctx.enter_context(nc.Block())

        def ring_back(n):
            if n >= TURNS:
                return TURNS
            last = max(m for m in range(n_turns) if m % TURNS == n)
            return n + n_turns - last

        def proj_dst(part, job):
            kind, c, m = job
            if kind == "q":
                return q_sb[part][:, m, :]
            if kind == "k":
                return k_sb[part][:, m, c * CHUNK:(c + 1) * CHUNK]
            t = c * RPC + 2 * m
            return v_sb[part][:, t:t + 2, :].rearrange("p t n -> p (t n)")

        @block.gpsimd
        def _(pool):
            nc.gpsimd.memset(zeros[:], 0.0).then_inc(pool_const, 1)
            nc.gpsimd.memset(ident[:], 0.0).then_inc(const_step, 1)
            nc.gpsimd.memset(causal_bf[:], 0.0).then_inc(const_step, 1)
            pool.wait_ge(const_step, 2)
            nc.gpsimd.affine_select(out=ident[:], in_=ident[:], compare_op=ALU.not_equal, fill=1.0,
                                    base=0, pattern=[[-1, P]], channel_multiplier=1).then_inc(pool_const, 1)
            nc.gpsimd.affine_select(out=causal_bf[:], in_=causal_bf[:], compare_op=ALU.is_ge, fill=MASKED,
                                    base=0, pattern=[[-1, P]], channel_multiplier=1).then_inc(pool_const, 1)

        @block.sync
        def _(sp):
            sp.wait_ge(pool_const, 3)
            zero_src = zeros[:, :].rearrange("p (a n) -> p a n", a=1).to_broadcast([P, DM // P, P])
            for dt in range(2):
                sp.dma_start(w_raw[:, dt], w_qkv[0, dt]).then_inc(w_in[dt % 2], 16)
            for dt in range(2, DT):
                sp.wait_ge(w_split, dt - 1)
                sp.dma_start(w_raw[:, dt % 2], w_qkv[0, dt]).then_inc(w_in[dt % 2], 16)
            def load_x(c):
                sp.dma_start(x_sb[:, 0].bitcast(F32), x_parts[c, 0].rearrange("p (t n) -> p t n", t=DT)).then_inc(x_in, 16)
                sp.dma_start(x_sb[:, 1].bitcast(F32), x_parts[c, 1].rearrange("p (t n) -> p t n", t=DT)).then_inc(x_in, 16)

            load_x(0)
            for n in range(2):
                sp.sem_inc(z_out[n], 8 * n_units)
            with sp.Fori(0, PAIRS) as i:
                for step in plan:
                    if step[0] == "proj":
                        c = step[1]
                        sp.wait_ge(job_ready, after(i, n_jobs, job_at["v", c, 1] + 1))
                        load_x((c + 1) % CHUNKS)
                        for n in range(EXPERTS // PAIRS // CHUNKS):
                            e = i * (EXPERTS // PAIRS) + (c * (EXPERTS // PAIRS // CHUNKS) + n)
                            sp.dma_start(gathered_x[bass.ds(e, 1)].rearrange("a p (t n) -> (a p) t n", n=P),
                                         zero_src).then_inc(zero_out, 16)
                    if step[0] == "out":
                        h, c = step[1:]
                        u = unit_at[h, c]
                        sp.wait_ge(z_done, after(i, n_units, u + 1))
                        sp.dma_start(z_dram[bass.ds(i * 2 + h, 1), :, c * CHUNK:(c + 1) * CHUNK]
                                     .rearrange("a p n -> (a p) n"), z_sb[:, u % 2]).then_inc(z_out[u % 2], 16)
                    if step in (("row", 0, CHUNKS - 1, 0), ("row", 0, CHUNKS - 1, 1)):
                        for dt in (2 * step[3], 2 * step[3] + 1):
                            sp.wait_ge(w_split, i * DT + (DT + dt - 1))
                            sp.dma_start(w_raw[:, dt % 2], w_qkv[bass.ds((i + 1) % PAIRS, 1), dt]
                                         .rearrange("a p n -> (a p) n")).then_inc(w_in[dt % 2], 16)
            sp.wait_ge(x_in, 32 * (CHUNKS * PAIRS + 1))
            sp.wait_ge(zero_out, 16 * EXPERTS)
            for n in range(2):
                sp.wait_ge(z_out[n], 8 * n_units * (PAIRS + 1))

        @block.scalar
        def _(act):
            act.wait_ge(pool_const, 3)
            nc.scalar.activation(ident_bf[:], ident[:], ACT.Copy).then_inc(act_const, 1)

            def split_w(base):
                for dt in range(DT):
                    act.wait_ge(w_in[dt % 2], base * (16 // 2) + (16 * (dt // 2) + 16))
                    nc.scalar.activation(w_sb[0][:, dt], w_raw[:, dt % 2], ACT.Copy).then_inc(w_hi_made, 1)

            split_w(0)
            act.sem_inc(exp_done, n_exp)
            act.sem_inc(spread_done, n_units)
            with act.Fori(0, PAIRS) as i:
                def project(c):
                    for job in [j for j in proj_jobs if j[1] == c]:
                        act.wait_ge(job_ready, after(i, n_jobs, job_at[job] + 1))
                        src = bank[:, job_at[job] % BANKS]
                        nc.scalar.activation(proj_dst(0, job), src, ACT.Copy).then_inc(proj_hi, 1)

                def exps(h, c, r):
                    row = row_at[h, c, r]
                    act.wait_ge(bias_done, i * n_rows + (row + 1))
                    u = unit_at[h, c]
                    act.wait_ge(diag_done, after(i, n_units, u - 1))
                    for kc in range(c + 1):
                        used, _ = widths(c, r, kc)
                        job = ("s", h, c, r, kc)
                        nc.scalar.activation(probs[:, u % 2, r, kc * CHUNK:kc * CHUNK + used],
                                             bank[:, job_at[job] % BANKS, 0:used], ACT.Exp,
                                             bias=neg_max[:, row % 2:row % 2 + 1], scale=SCALE,
                                             accum_out=sums[:, u % 2, r, kc:kc + 1]).then_inc(exp_done, 1)

                def turn(s):
                    n = turn_at[s]
                    lo_col = max(0, s[3] - RPC * s[2]) * P
                    act.wait_ge(turn_ready, i * n_turns + (n + 1))
                    act.wait_ge(pv_done, after(i, n_turns, n - ring_back(n) + 1))
                    nc.scalar.activation(pT_sb[0][:, n % TURNS, lo_col:], turned[:, n % TURNS, lo_col:],
                                         ACT.Copy).then_inc(turn_hi, 1)

                late = None
                for step in plan:
                    if step[0] == "proj":
                        if late:
                            exps(*late)
                            late = None
                        project(step[1])
                    if step[0] == "row":
                        if late:
                            exps(*late)
                        late = step[1:]
                    if step[0] == "turn":
                        turn(step)
                        if late:
                            exps(*late)
                            late = None
                    if step[0] == "norm":
                        if late:
                            exps(*late)
                            late = None
                        act.wait_ge(job_ready, after(i, n_jobs, job_at[step] + 1))
                        act.wait_ge(z_done, after(i, n_units, unit_at[step[1:]]))
                        nc.scalar.activation(spread_sb[:], bank[:, job_at[step] % BANKS],
                                             ACT.Copy).then_inc(spread_done, 1)
                    if step[0] == "row" and step[1:] == (0, CHUNKS - 1, 0):
                        exps(*late)
                        late = None
                        act.wait_ge(job_ready, after(i, n_jobs, job_at["v", CHUNKS - 1, 1] + 1))
                        split_w(i * DT + DT)
                if late:
                    exps(*late)

        @block.vector
        def _(dve):
            nc.vector.memset(spread_sb[:], 1.0).then_inc(dve_const, 1)
            dve.wait_ge(dve_const, 1)
            nc.vector.tensor_copy(ones[:], spread_sb[:, 0:P]).then_inc(dve_const, 1)
            dve.sem_inc(proj_lo, n_proj)
            dve.sem_inc(turn_lo, n_turns)
            dve.sem_inc(diag_done, n_units)
            dve.sem_inc(z_done, n_units)

            def split_w(base):
                for dt in range(DT):
                    dve.wait_ge(w_hi_made, base + (dt + 1))
                    nc.vector.tensor_tensor(w_sb[1][:, dt], w_raw[:, dt % 2], w_sb[0][:, dt].bitcast(F32),
                                            ALU.subtract).then_inc(w_split, 1)

            split_w(0)
            dve.wait_ge(pool_const, 3)
            with dve.Fori(0, PAIRS) as i:
                def project(c):
                    for job in [j for j in proj_jobs if j[1] == c]:
                        dve.wait_ge(proj_hi, i * n_proj + (proj_at[job] + 1))
                        nc.vector.tensor_tensor(proj_dst(1, job), bank[:, job_at[job] % BANKS],
                                                proj_dst(0, job).bitcast(F32), ALU.subtract).then_inc(proj_lo, 1)

                def maxima(h, c, r):
                    row = row_at[h, c, r]
                    first = exp_at["s", h, c, r, 0]
                    if row >= 2:
                        h2, c2, r2 = rows[row - 2]
                        dve.wait_ge(exp_done, after(i, n_exp, exp_at["s", h2, c2, r2, c2] + 1))
                    else:
                        dve.wait_ge(exp_done, after(i, n_exp, 0))
                    for kc in range(c + 1):
                        job = ("s", h, c, r, kc)
                        used, _ = widths(c, r, kc)
                        dve.wait_ge(job_ready, after(i, n_jobs, job_at[job] + 1))
                        dst = max_part[:, row % 2, kc:kc + 1]
                        nc.vector.reduce_max(dst, bank[:, job_at[job] % BANKS, 0:used],
                                             axis=AX_X).then_inc(part_done, 1)
                    dve.wait_ge(part_done, i * n_exp + (first + c + 1))
                    nc.vector.reduce_max(row_max[:, row % 2:row % 2 + 1], max_part[:, row % 2, 0:c + 1],
                                         axis=AX_X).then_inc(max_done, 1)
                    dve.wait_ge(max_done, i * n_rows + (row + 1))
                    nc.vector.tensor_scalar(neg_max[:, row % 2:row % 2 + 1], row_max[:, row % 2:row % 2 + 1],
                                            -SCALE, None, ALU.mult).then_inc(bias_done, 1)

                def inverse(h, c):
                    u = unit_at[h, c]
                    dve.wait_ge(exp_done, after(i, n_exp, exp_at["s", h, c, RPC - 1, c] + 1))
                    nc.vector.reduce_sum(total[:, u % 2], sums[:, u % 2, :, 0:c + 1], axis=AX_X).then_inc(sum_step, 1)
                    dve.wait_ge(sum_step, i * (3 * n_units) + (3 * u + 1))
                    nc.vector.reciprocal(inv[:, u % 2], total[:, u % 2]).then_inc(sum_step, 1)
                    dve.wait_ge(sum_step, i * (3 * n_units) + (3 * u + 2))
                    dve.wait_ge(spread_done, after(i, n_units, u))
                    for r in range(RPC):
                        mark = nc.vector.tensor_scalar(diag[0][:, r], ident[:], inv[:, u % 2, r:r + 1], None,
                                                       ALU.mult)
                    mark.then_inc(sum_step, 1)
                    dve.wait_ge(sum_step, i * (3 * n_units) + (3 * u + 3))
                    for r in range(RPC):
                        mark = nc.vector.scalar_tensor_tensor(diag[1][:, r], ident[:], inv[:, u % 2, r:r + 1],
                                                              diag[0][:, r].bitcast(F32), ALU.mult, ALU.subtract)
                    mark.then_inc(diag_done, 1)

                for step in plan:
                    if step[0] == "proj":
                        project(step[1])
                    if step[0] == "row":
                        maxima(*step[1:])
                    if step[0] == "turn":
                        n = turn_at[step]
                        lo_col = max(0, step[3] - RPC * step[2]) * P
                        dve.wait_ge(turn_hi, i * n_turns + (n + 1))
                        nc.vector.tensor_tensor(pT_sb[1][:, n % TURNS, lo_col:], turned[:, n % TURNS, lo_col:],
                                                pT_sb[0][:, n % TURNS, lo_col:].bitcast(F32),
                                                ALU.subtract).then_inc(turn_lo, 1)
                    if step[0] == "norm":
                        inverse(*step[1:])
                    if step[0] == "out":
                        u = unit_at[step[1:]]
                        last = pv_at["turn", *step[1:], RPC * (step[2] + 1) - 1]
                        dve.wait_ge(pv_done, after(i, n_turns, last + 1))
                        dve.wait_ge(spread_done, after(i, n_units, u + 1))
                        dve.wait_ge(z_out[u % 2], i * (8 * n_units) + (8 * n_units + 16 * (u // 2)))
                        nc.vector.tensor_tensor(z_sb[:, u % 2], z_ps[:], spread_sb[:], ALU.mult).then_inc(z_done, 1)
                    if step[0] == "row" and step[1:] == (0, CHUNKS - 1, 0):
                        split_w(i * DT + DT)

        @block.tensor
        def _(pe):
            pe.sem_inc(job_ready, n_jobs)
            pe.sem_inc(pv_done, n_turns)
            pe.wait_ge(pool_const, 3)
            pe.wait_ge(act_const, 1)
            pe.wait_ge(dve_const, 2)
            pe.wait_ge(w_split, DT)
            with pe.Fori(0, PAIRS) as i:
                def take(n):
                    m = n - BANKS
                    old = jobs[m]
                    back = 0 if m >= 0 else 1
                    if old[0] == "s":
                        pe.wait_ge(exp_done, after(i, n_exp, exp_at[old] + 1 - back * n_exp))
                    elif old[0] == "norm":
                        pe.wait_ge(spread_done, after(i, n_units, unit_at[old[1:]] + 1 - back * n_units))
                    else:
                        pe.wait_ge(proj_lo, after(i, n_proj, proj_at[old] + 1 - back * n_proj))
                    return bank[:, n % BANKS]

                def project(c):
                    pe.wait_ge(x_in, i * (32 * CHUNKS) + (32 * c + 32))
                    if c == 0:
                        pe.wait_ge(w_split, i * DT + DT)
                    for h in range(2):
                        for kind in range(2):
                            job = ("qk"[kind], c, h)
                            dst = take(job_at[job])
                            cols = slice((2 * h + kind) * DH, (2 * h + kind + 1) * DH)
                            for dt in range(DT):
                                for a, b in PASSES:
                                    mark = nc.tensor.matmul(dst, w_sb[a][:, dt, cols], x_sb[:, b, dt, :],
                                                            start=(dt == 0 and (a, b) == PASSES[0]),
                                                            stop=(dt == DT - 1 and (a, b) == PASSES[-1]))
                            mark.then_inc(job_ready, 1)
                    for half in range(2):
                        dst = take(job_at["v", c, half])
                        for t in range(2):
                            rows_ = slice((2 * half + t) * P, (2 * half + t + 1) * P)
                            for dt in range(DT):
                                for a, b in PASSES:
                                    mark = nc.tensor.matmul(dst[:, t * 2 * DH:(t + 1) * 2 * DH],
                                                            x_sb[:, a, dt, rows_], w_sb[b][:, dt, 4 * DH:],
                                                            start=(dt == 0 and (a, b) == PASSES[0]),
                                                            stop=(dt == DT - 1 and (a, b) == PASSES[-1]))
                        mark.then_inc(job_ready, 1)

                def scores(h, c, r):
                    if r == 0:
                        pe.wait_ge(proj_lo, after(i, n_proj, proj_at["k", c, h] + 1))
                    for kc in range(c + 1):
                        n = job_at["s", h, c, r, kc]
                        dst = take(n)
                        used, width = widths(c, r, kc)
                        for a, b in PASSES:
                            mark = nc.tensor.matmul(dst[:, 0:width], q_sb[a][:, h, r * P:(r + 1) * P],
                                                    k_sb[b][:, h, kc * CHUNK:kc * CHUNK + width],
                                                    start=(a, b) == PASSES[0], stop=(a, b) == PASSES[-1])
                            if kc == c and (a, b) == PASSES[0]:
                                nc.tensor.matmul(dst[:, r * P:(r + 1) * P], ident_bf[:], causal_bf[:],
                                                 start=False, stop=False, skip_group_check=True)
                        mark.then_inc(job_ready, 1)

                def turn(s):
                    _, h, c, j = s
                    n, u = turn_at[s], unit_at[h, c]
                    first = max(0, j - RPC * c)
                    if j == 0:
                        pe.wait_ge(exp_done, after(i, n_exp, exp_at["s", h, c, RPC - 1, c] + 1))
                    pe.wait_ge(turn_lo, after(i, n_turns, n - ring_back(n) + 1))
                    for r in range(first, RPC):
                        mark = nc.tensor.transpose(turned[:, n % TURNS, r * P:(r + 1) * P],
                                                   probs[:, u % 2, r, j * P:(j + 1) * P], ident[:])
                    mark.then_inc(turn_ready, 1)

                def value(s):
                    _, h, c, j = s
                    n = turn_at["turn", h, c, j]
                    first = max(0, j - RPC * c)
                    if j == 0:
                        pe.wait_ge(z_done, after(i, n_units, unit_at[h, c]))
                        pe.wait_ge(proj_lo, after(i, n_proj, proj_at["v", c, 1] + 1))
                    pe.wait_ge(turn_lo, after(i, n_turns, n + 1))
                    for a, b in PASSES:
                        mark = nc.tensor.matmul(z_ps[:, first * P:], v_sb[a][:, j, h * DH:(h + 1) * DH],
                                                pT_sb[b][:, n % TURNS, first * P:],
                                                start=(j == 0 and (a, b) == PASSES[0]),
                                                stop=(j == RPC * (c + 1) - 1 and (a, b) == PASSES[-1]),
                                                skip_group_check=True)
                    mark.then_inc(pv_done, 1)

                for step in plan:
                    if step[0] == "proj":
                        project(step[1])
                    if step[0] == "row":
                        scores(*step[1:])
                    if step[0] == "turn":
                        turn(step)
                    if step[0] == "pv":
                        value(step)
                    if step[0] == "norm":
                        dst = take(job_at[step])
                        pe.wait_ge(diag_done, after(i, n_units, unit_at[step[1:]] + 1))
                        for part in range(2):
                            mark = nc.tensor.matmul(dst, ones[:], diag[part][:].rearrange("p r n -> p (r n)"),
                                                    start=part == 0, stop=part == 1)
                        mark.then_inc(job_ready, 1)


def project_and_route(nc, z_dram, w_o, gate_w, x_rows, x1_dram, x1T_parts, gathered_x, routes):
    slot_of, gate_of = routes
    BIG = 1 << 20

    with ExitStack() as ctx:
        def sb(name, shape, dt=F32):
            return ctx.enter_context(nc.sbuf_tensor(name, shape, dt))

        def ps(name, shape, dt=F32):
            return ctx.enter_context(nc.psum_tensor(name, shape, dt))

        def sem(name):
            return ctx.enter_context(nc.semaphore(name))

        NB = 2
        wo_raw = sb("wo_raw", [P, 2, DM])
        wo = [sb(f"wo_{n}", [P, HEADS, DM], F32R) for n in ("hi", "lo")]
        gw = sb("gw", [P, DT, EXPERTS])
        z_raw = sb("z_raw", [P, NB, HEADS, P])
        z = [sb(f"z_{n}", [P, NB, HEADS, P], F32R) for n in ("hi", "lo")]
        xr = sb("xr", [P, NB, DM])
        y = sb("y", [P, NB, DM])
        x1 = sb("x1", [P, NB, DM])
        x1T = sb("x1T", [P, NB, DT, P])
        xT_part = [sb(f"x1T_{n}", [P, NB, DT, P], F32R) for n in ("hi", "lo")]
        stats = sb("stats", [P, 6])
        mv = sb("mv", [P, 2])
        small = sb("small", [P, 16])
        eps = sb("eps", [P, 1])
        lg = sb("lg", [P, EXPERTS])
        lg_c = sb("lg_c", [P, EXPERTS])
        ex = sb("ex", [P, EXPERTS])
        top = sb("top", [P, 8])
        top_e = sb("top_e", [P, 8])
        gate = sb("gate", [P, TOPK])
        idx = sb("idx", [P, 8], U32)
        idx_f = sb("idx_f", [P, 8])
        pick = sb("pick", [P, TOPK, EXPERTS])
        pick_pos = sb("pick_pos", [P, TOPK, EXPERTS])
        chosen = sb("chosen", [P, EXPERTS])
        chosen_bf = sb("chosen_bf", [P, EXPERTS], BF16)
        count = sb("count", [P, EXPERTS])
        pos_all = sb("pos_all", [P, EXPERTS])
        slot = sb("slot", [P, NB, TOPK], U32)
        pos = sb("pos", [P, TOPK])
        full = sb("full", [P, TOPK])
        room = sb("room", [P, TOPK])
        place = sb("place", [P, TOPK])
        place2 = sb("place2", [P, TOPK])
        iota_i = sb("iota_i", [P, EXPERTS], I32)
        iota_f = sb("iota_f", [P, EXPERTS])
        ident = sb("ident3", [P, P])
        before_bf = sb("before_bf", [P, P], BF16)
        ones_bf = sb("ones_bf", [P, P], BF16)

        o_ps = ps("o_ps", [P, 2, DM])
        t_ps = ps("t_ps", [P, DT * P])
        l_ps = ps("l_ps", [P, EXPERTS])
        c_ps = ps("c_ps", [P, 2, EXPERTS])

        credits = sem("credits")
        waited = sem("waited3")
        pool_step = sem("pool_step")
        pool_const = sem("pool_const3")
        dve_const = sem("dve_const3")
        wo_in = [sem(f"wo_in{n}") for n in range(2)]
        wo_hi = sem("wo_hi")
        wo_split = sem("wo_split")
        gw_in = sem("gw_in")
        z_in = [sem(f"z_in{n}") for n in range(NB)]
        x_in = [sem(f"xr_in{n}") for n in range(NB)]
        z_hi = sem("z_hi")
        z_lo = sem("z_lo")
        out_ready = sem("out_ready")
        out_read = sem("out_read")
        rooted = sem("rooted")
        x1_ready = sem("x1_ready")
        x1_stored = [sem(f"x1_stored{n}") for n in range(NB)]
        t_ready = sem("t_ready")
        t_read = sem("t_read")
        t_hi = sem("t_hi")
        t_split = sem("t_split")
        t_stored = [sem(f"t_stored{n}") for n in range(NB)]
        l_ready = sem("l_ready")
        l_read = sem("l_read")
        exp_ready = sem("exp_ready")
        chosen_ready = sem("chosen_ready")
        c_ready = sem("c_ready")
        c_read = sem("c_read")
        placed = sem("placed")
        moved = sem("moved")
        rows_left = sem("rows_left")
        chain = sem("chain3")
        block = ctx.enter_context(nc.Block())
        STEPS = 27

        @block.gpsimd
        def _(pool):
            nc.gpsimd.memset(ident[:], 0.0).then_inc(pool_step, 1)
            nc.gpsimd.memset(before_bf[:], 1.0).then_inc(pool_step, 1)
            nc.gpsimd.iota(iota_i[:], pattern=[[1, EXPERTS]], base=0, channel_multiplier=0).then_inc(pool_const, 1)
            pool.wait_ge(pool_step, 2)
            nc.gpsimd.affine_select(out=ident[:], in_=ident[:], compare_op=ALU.not_equal, fill=1.0,
                                    base=0, pattern=[[-1, P]], channel_multiplier=1).then_inc(pool_const, 1)
            nc.gpsimd.affine_select(out=before_bf[:], in_=before_bf[:], compare_op=ALU.is_gt, fill=0.0,
                                    base=0, pattern=[[1, P]], channel_multiplier=-1).then_inc(pool_const, 1)
            flat = gathered_x.rearrange("e c d -> (e c) d")
            last_slot = nc.gpsimd.to_reg(SLOTS - 1)
            pool.sem_inc(rows_left, NB)
            with pool.Fori(0, TILES // NB) as i:
                for b in range(NB):
                    wait_apart(pool, waited, placed, after(i, NB, b + 1))
                    for k in range(TOPK):
                        nc.gpsimd.indirect_dma_start(
                            flat, bass.IndirectOffsetOnAxis(ap=slot[:, b, k:k + 1], axis=0), x1[:, b], None,
                            bounds_check=last_slot, oob_is_err=False).then_inc(moved, 16)
                    pool.wait_ge(moved, (i * NB + (b + 1)) * (16 * TOPK))
                    pool.sem_inc(rows_left, 1)

        @block.sync
        def _(sp):
            sp.dma_start(gw[:], gate_w).then_inc(gw_in, 16)
            for h in range(HEADS):
                if h >= 2:
                    sp.wait_ge(wo_split, h - 1)
                sp.dma_start(wo_raw[:, h % 2], w_o[:, h]).then_inc(wo_in[h % 2], 16)

            def load(i, b):
                t = i * NB + b
                sp.dma_start(z_raw[:, b], z_dram[:, :, bass.ds(t * P, P)].rearrange("h p n -> p h n")
                             ).then_inc(z_in[b], 16)
                sp.dma_start(xr[:, b], x_rows[bass.ds(t * P, P)]).then_inc(x_in[b], 16)

            def tiles(i, last):
                for b in range(NB):
                    t = i * NB + b
                    sp.wait_ge(x1_ready, after(i, NB, b + 1))
                    sp.dma_start(x1_dram[bass.ds(t * P, P)], x1[:, b]).then_inc(x1_stored[b], 16)
                    sp.wait_ge(t_split, after(i, NB, b + 1))
                    for part in range(2):
                        sp.dma_start(x1T_parts[bass.ds(t, 1), part].rearrange("a p n -> (a p) n"),
                                     xT_part[part][:, b].rearrange("p t n -> p (t n)").bitcast(F32)
                                     ).then_inc(t_stored[b], 16)
                    if not last:
                        sp.wait_ge(z_lo, after(i, NB, b + 1))
                        sp.wait_ge(out_read, after(i, NB, b + 1))
                        load(i + 1, b)

            load(0, 0)
            load(0, 1)
            for b in range(NB):
                sp.sem_inc(x1_stored[b], 16)
                sp.sem_inc(t_stored[b], 32)
            with sp.Fori(0, TILES // NB - 1) as i:
                tiles(i, False)
            tiles(TILES // NB - 1, True)
            for b in range(NB):
                sp.wait_ge(x1_stored[b], 16 * TILES // NB + 16)
                sp.wait_ge(t_stored[b], 32 * TILES // NB + 32)

        @block.scalar
        def _(act):
            for h in range(HEADS):
                act.wait_ge(wo_in[h % 2], 16 * (h // 2) + 16)
                nc.scalar.activation(wo[0][:, h], wo_raw[:, h % 2], ACT.Copy).then_inc(wo_hi, 1)

            def split(i, b):
                act.wait_ge(z_in[b], i * 16 + 16)
                act.wait_ge(out_ready, after(i, NB, b - 1))
                nc.scalar.activation(z[0][:, b], z_raw[:, b], ACT.Copy).then_inc(z_hi, 1)

            def tiles(i, last):
                for b in range(NB):
                    if b + 1 < NB:
                        split(i, b + 1)
                    elif not last:
                        split(i + 1, 0)
                    act.wait_ge(chain, i * (NB * STEPS) + (b * STEPS + 3))
                    nc.scalar.activation(small[:, 0:1], mv[:, 1:2], ACT.Sqrt, bias=eps[:]).then_inc(rooted, 1)
                    act.wait_ge(t_ready, i * NB + (b + 1))
                    act.wait_ge(l_ready, after(i, NB, b - 1))
                    nc.scalar.activation(x1T[:, b].rearrange("p t n -> p (t n)"), t_ps[:], ACT.Copy
                                         ).then_inc(t_read, 1)
                    act.wait_ge(t_stored[b], after(i, 32, 0))
                    nc.scalar.activation(xT_part[0][:, b].rearrange("p t n -> p (t n)"), t_ps[:], ACT.Copy
                                         ).then_inc(t_hi, 1)
                    act.wait_ge(l_read, after(i, NB, b + 1))
                    nc.scalar.activation(ex[:], lg_c[:], ACT.Exp, accum_out=small[:, 4:5]).then_inc(exp_ready, 1)

            act.wait_ge(credits, 1)
            split(0, 0)
            with act.Fori(0, TILES // NB - 1) as i:
                tiles(i, False)
            tiles(TILES // NB - 1, True)

        @block.tensor
        def _(pe):
            pe.wait_ge(wo_split, HEADS)
            pe.wait_ge(pool_const, 3)
            pe.wait_ge(dve_const, 3)
            pe.wait_ge(gw_in, 16)
            pe.sem_inc(out_ready, NB)
            pe.sem_inc(l_ready, NB)
            pe.sem_inc(credits, 1)

            def project(i, b):
                pe.wait_ge(z_lo, after(i, NB, b + 1))
                pe.wait_ge(out_read, after(i, NB, b - 1))
                for h in range(HEADS):
                    for m, n in PASSES:
                        mark = nc.tensor.matmul(o_ps[:, b], z[m][:, b, h], wo[n][:, h],
                                                start=h == 0 and (m, n) == PASSES[0],
                                                stop=h == HEADS - 1 and (m, n) == PASSES[-1])
                mark.then_inc(out_ready, 1)

            def tiles(i, last):
                for b in range(NB):
                    if b + 1 < NB:
                        project(i, b + 1)
                    elif not last:
                        project(i + 1, 0)
                    pe.wait_ge(x1_ready, after(i, NB, b + 1))
                    pe.wait_ge(t_split, after(i, NB, b))
                    for d in range(DT):
                        mark = nc.tensor.transpose(t_ps[:, d * P:(d + 1) * P], x1[:, b, d * P:(d + 1) * P], ident[:])
                    mark.then_inc(t_ready, 1)
                    pe.wait_ge(t_read, i * NB + (b + 1))
                    pe.wait_ge(l_read, after(i, NB, b))
                    for d in range(DT):
                        mark = nc.tensor.matmul(l_ps[:], x1T[:, b, d], gw[:, d], start=d == 0, stop=d == DT - 1)
                    mark.then_inc(l_ready, 1)
                    pe.wait_ge(chosen_ready, i * NB + (b + 1))
                    pe.wait_ge(c_read, after(i, NB, b))
                    nc.tensor.matmul(c_ps[:, 0], before_bf[:], chosen_bf[:], start=True, stop=True)
                    nc.tensor.matmul(c_ps[:, 1], ones_bf[:], chosen_bf[:], start=True, stop=True).then_inc(c_ready, 1)

            project(0, 0)
            with pe.Fori(0, TILES // NB - 1) as i:
                tiles(i, False)
            tiles(TILES // NB - 1, True)

        @block.vector
        def _(dve):
            done = [0, 0]

            def step(ins, waited=None):
                done[0] += 1
                ins.then_inc(chain, 1)
                if waited:
                    wait_apart(dve, waited, chain, done[1] * (NB * STEPS) + done[0])
                else:
                    dve.wait_ge(chain, done[1] * (NB * STEPS) + done[0])

            nc.vector.memset(eps[:], EPS).then_inc(dve_const, 1)
            nc.vector.memset(ones_bf[:], 1.0).then_inc(dve_const, 1)
            nc.vector.memset(count[:], 0.0).then_inc(dve_const, 1)
            dve.wait_ge(dve_const, 3)
            for h in range(HEADS):
                dve.wait_ge(wo_hi, h + 1)
                nc.vector.tensor_tensor(wo[1][:, h], wo_raw[:, h % 2], wo[0][:, h].bitcast(F32),
                                        ALU.subtract).then_inc(wo_split, 1)
            dve.wait_ge(pool_const, 3)
            nc.vector.tensor_copy(iota_f[:], iota_i[:]).then_inc(dve_const, 1)

            for free in (z_lo, out_read, x1_ready, t_split, l_read, c_read, placed):
                dve.sem_inc(free, NB)

            def split(i, b):
                dve.wait_ge(z_hi, i * NB + (b + 1))
                nc.vector.tensor_tensor(z[1][:, b], z_raw[:, b], z[0][:, b].bitcast(F32),
                                        ALU.subtract).then_inc(z_lo, 1)

            def tile(i, b, last):
                t = i * NB + b
                if b + 1 < NB:
                    split(i, b + 1)
                elif not last:
                    split(i + 1, 0)
                dve.wait_ge(out_ready, after(i, NB, b + 1))
                dve.wait_ge(x_in[b], i * 16 + 16)
                nc.vector.tensor_tensor(y[:, b], o_ps[:, b], xr[:, b], ALU.add).then_inc(out_read, 1)
                dve.wait_ge(out_read, after(i, NB, b + 1))
                step(nc.vector.bn_stats(stats[:], y[:, b]), waited)
                step(nc.vector.bn_aggr(mv[:], stats[:]))
                step(nc.vector.tensor_scalar(small[:, 1:2], mv[:, 1:2], EPS, None, ALU.add))
                dve.wait_ge(rooted, i * NB + (b + 1))
                step(nc.vector.reciprocal(small[:, 2:3], small[:, 0:1]))
                newton(nc, step, small)
                dve.wait_ge(x1_stored[b], after(i, 16, 0))
                dve.wait_ge(rows_left, after(i, NB, b - 1))
                nc.vector.tensor_scalar(x1[:, b], y[:, b], mv[:, 0:1], small[:, 2:3], ALU.subtract,
                                        ALU.mult).then_inc(x1_ready, 1)
                dve.wait_ge(t_hi, i * NB + (b + 1))
                dve.wait_ge(t_stored[b], after(i, 32, 0))
                nc.vector.tensor_tensor(xT_part[1][:, b].rearrange("p t n -> p (t n)"), t_ps[:],
                                        xT_part[0][:, b].rearrange("p t n -> p (t n)").bitcast(F32),
                                        ALU.subtract).then_inc(t_split, 1)
                dve.wait_ge(l_ready, after(i, NB, b + 1))
                step(nc.vector.reduce_max(small[:, 3:4], l_ps[:], axis=AX_X))
                nc.vector.tensor_scalar(lg_c[:], l_ps[:], small[:, 3:4], LOG_LEAST, ALU.subtract,
                                        ALU.max).then_inc(l_read, 1)
                wait_apart(dve, waited, l_read, after(i, NB, b + 1))
                step(nc.vector.max(top[:], lg_c[:]), waited)
                step(nc.vector.max_index(idx[:], top[:], lg_c[:]))
                step(nc.vector.tensor_copy(idx_f[:], idx[:]))
                step(nc.vector.tensor_tensor(
                    pick[:], iota_f[:].rearrange("p (k e) -> p k e", k=1).to_broadcast([P, TOPK, EXPERTS]),
                    idx_f[:, 0:TOPK].rearrange("p (k e) -> p k e", e=1).to_broadcast([P, TOPK, EXPERTS]),
                    ALU.is_equal))
                step(nc.vector.reduce_sum(chosen[:], pick[:].rearrange("p k e -> p e k"), axis=AX_X))
                nc.vector.tensor_copy(chosen_bf[:], chosen[:]).then_inc(chosen_ready, 1)
                dve.wait_ge(exp_ready, i * NB + (b + 1))
                step(nc.vector.tensor_tensor(pick_pos[:], pick[:], ex[:].rearrange("p (k e) -> p k e", k=1)
                                             .to_broadcast([P, TOPK, EXPERTS]), ALU.mult))
                step(nc.vector.reduce_sum(top_e[:, 0:TOPK], pick_pos[:], axis=AX_X))
                step(nc.vector.reciprocal(small[:, 5:6], small[:, 4:5]))
                step(nc.vector.tensor_scalar(gate[:], top_e[:, 0:TOPK], small[:, 5:6], None, ALU.mult))
                dve.wait_ge(c_ready, i * NB + (b + 1))
                step(nc.vector.tensor_tensor(pos_all[:], c_ps[:, 0], count[:], ALU.add))
                nc.vector.tensor_tensor(count[:], c_ps[:, 1], count[:], ALU.add).then_inc(c_read, 1)
                dve.wait_ge(c_read, after(i, NB, b + 1))
                step(nc.vector.tensor_tensor(pick_pos[:], pick[:], pos_all[:].rearrange("p (k e) -> p k e", k=1)
                                             .to_broadcast([P, TOPK, EXPERTS]), ALU.mult))
                step(nc.vector.reduce_sum(pos[:], pick_pos[:], axis=AX_X))
                step(nc.vector.tensor_scalar(full[:], pos[:], float(CAPACITY), float(BIG), ALU.is_ge, ALU.mult))
                step(nc.vector.tensor_scalar(room[:], pos[:], float(CAPACITY), None, ALU.is_lt))
                step(nc.vector.scalar_tensor_tensor(place[:], idx_f[:, 0:TOPK], float(CAPACITY), pos[:],
                                                    ALU.mult, ALU.add))
                step(nc.vector.tensor_tensor(gate_of[:, bass.ds(t, 1)].rearrange("p a k -> p (a k)"), gate[:], room[:], ALU.mult))
                step(nc.vector.tensor_tensor(slot_of[:, bass.ds(t, 1)].rearrange("p a k -> p (a k)"), place[:], full[:],
                                             ALU.add))
                nc.vector.tensor_tensor(slot[:, b], place[:], full[:], ALU.add).then_inc(placed, 1)
                assert done[0] == STEPS * (b + 1), done

            def tiles(i, last):
                done[:] = [0, i]
                for b in range(NB):
                    tile(i, b, last)

            dve.wait_ge(dve_const, 4)
            split(0, 0)
            with dve.Fori(0, TILES // NB - 1) as i:
                tiles(i, False)
            tiles(TILES // NB - 1, True)


def newton(nc, step, s):
    step(nc.vector.tensor_tensor(s[:, 6:7], s[:, 2:3], s[:, 2:3], ALU.mult))
    step(nc.vector.scalar_tensor_tensor(s[:, 7:8], s[:, 6:7], -0.5, s[:, 1:2], ALU.mult, ALU.mult))
    step(nc.vector.tensor_scalar(s[:, 8:9], s[:, 7:8], 1.5, None, ALU.add))
    step(nc.vector.tensor_tensor(s[:, 9:10], s[:, 8:9], s[:, 2:3], ALU.mult))
    step(nc.vector.tensor_copy(s[:, 2:3], s[:, 9:10]))


def experts(nc, gathered_x, x1T_parts, w13, w2, s13, s2, y_dram, shared_dram):
    with ExitStack() as ctx:
        def sb(name, shape, dt=F32):
            return ctx.enter_context(nc.sbuf_tensor(name, shape, dt))

        def ps(name, shape, dt=F32):
            return ctx.enter_context(nc.psum_tensor(name, shape, dt))

        def sem(name):
            return ctx.enter_context(nc.semaphore(name))

        BODIES = 8
        NE = EXPERTS // BODIES
        NS = TILES * SHARED_PARTS // BODIES
        UNITS = [("s", u // 3) if u % 3 == 2 else ("e", 2 * (u // 3) + u % 3) for u in range(NE + NS)]
        NU = len(UNITS)
        unit_of = {unit: u for u, unit in enumerate(UNITS)}
        PIECES = [(2 * INTER, P)] * DT + [(DM, rows) for _, rows in INTER_TILES]
        NP = len(PIECES)
        IT = len(INTER_TILES)

        raw = [sb(f"w_raw{p}", [P, cols]) for p, (cols, _) in enumerate(PIECES)]
        up_w = [sb(f"up_{n}", [P, 2, DT, 2 * INTER], F32R) for n in ("hi", "lo")]
        down_w = [sb(f"down_{n}", [P, 2, IT, DM], F32R) for n in ("hi", "lo")]
        s_up = [sb(f"s_up_{n}", [P, SHARED_PARTS, DT, 2 * INTER], F32R) for n in ("hi", "lo")]
        s_down = [sb(f"s_down_{n}", [P, SHARED_PARTS, IT, DM], F32R) for n in ("hi", "lo")]
        rows_in = sb("rows_in", [P, 2, DM])
        eT = [sb(f"eT_{n}", [P, 2, DT * P], F32R) for n in ("hi", "lo")]
        sT = sb("sT", [P, 2, 2, DT * P], F32R)
        act_sb = sb("act_sb", [P, 2, INTER])
        h_sb = sb("h_sb", [P, 2, INTER])
        hT = [sb(f"hT_{n}", [P, 2, IT * P], F32R) for n in ("hi", "lo")]
        y_sb = sb("y_sb", [P, 2, DM])
        ys_sb = sb("ys_sb", [P, 2, DM])
        ident = sb("ident4", [P, P])

        t_ps = ps("t4_ps", [P, 2, CHUNK])
        h_ps = ps("h_ps", [P, 2, 2, CHUNK])
        y_ps = ps("y_ps", [P, DM])
        ys_ps = ps("ys_ps", [P, DM])

        tjobs = []
        for u in range(NU):
            tjobs.append(("h", (u - 1) % NU))
            if u == 0 and UNITS[0][0] == "e":
                tjobs.append(("x", 0))
            if u + 1 < NU and UNITS[u + 1][0] == "e":
                tjobs.append(("x", u + 1))
        assert len(tjobs) % 2 == 0 and NU % 2 == 0 and NE % 2 == 0
        NT = len(tjobs)
        t_at = {job: n for n, job in enumerate(tjobs)}

        pool_step = sem("pool_step4")
        pool_const = sem("pool_const4")
        s_in = [sem(f"s_in{p}") for p in range(NP)]
        s_hi = sem("s_hi")
        s_lo = sem("s_lo")
        raw_in = [sem(f"raw_in{p}") for p in range(NP)]
        w_hi = sem("w_hi")
        w_lo = sem("w_lo")
        rows_loaded = [sem(f"rows_loaded{n}") for n in range(2)]
        sT_loaded = [sem(f"sT_loaded{n}") for n in range(2)]
        t_ready = sem("t4_ready")
        t_hi = sem("t4_hi")
        t_lo = sem("t4_lo")
        up_ready = sem("up_ready")
        silu_ready = sem("silu_ready")
        h_ready = sem("h_ready")
        down_ready = sem("down_ready")
        y_read = sem("y_read")
        ys_read = sem("ys_read")
        y_stored = [sem(f"y_stored{n}") for n in range(2)]
        ys_stored = [sem(f"ys_stored{n}") for n in range(2)]
        block = ctx.enter_context(nc.Block())

        def job_before(n):
            return n == 0

        def dst_of(part, n, p, up, down):
            cols, rows = PIECES[p]
            return up[part][:, n, p, :] if p < DT else down[part][0:rows, n, p - DT, :]

        @block.gpsimd
        def _(pool):
            nc.gpsimd.memset(ident[:], 0.0).then_inc(pool_step, 1)
            pool.wait_ge(pool_step, 1)
            nc.gpsimd.affine_select(out=ident[:], in_=ident[:], compare_op=ALU.not_equal, fill=1.0,
                                    base=0, pattern=[[-1, P]], channel_multiplier=1).then_inc(pool_const, 1)

        @block.sync
        def _(sp):
            def weights(up_src, down_src, p):
                cols, rows = PIECES[p]
                if p < DT:
                    return up_src[:, :, p, :].rearrange("a p n -> (a p) n")
                first = INTER_TILES[p - DT][0]
                return down_src[:, first:first + rows, :].rearrange("a p n -> (a p) n")

            for half in range(SHARED_PARTS):
                for p, (cols, rows) in enumerate(PIECES):
                    if half:
                        sp.wait_ge(s_lo, p + 1)
                    sp.dma_start(raw[p][0:rows], weights(s13[half:half + 1], s2[half:half + 1], p)).then_inc(s_in[p], 16)
            with sp.Fori(0, BODIES) as i:
                for u, (kind, n) in enumerate(UNITS):
                    if kind == "e":
                        e = i * NE + n
                        back = t_at["x", unit_of["e", (n - 2) % NE]] - (NT if n < 2 else 0)
                        sp.wait_ge(t_ready, after(i, NT, back + 1))
                        sp.dma_start(rows_in[:, n % 2], gathered_x[bass.ds(e, 1)].rearrange("a p n -> (a p) n")
                                     ).then_inc(rows_loaded[n % 2], 16)
                        for p, (cols, rows) in enumerate(PIECES):
                            sp.wait_ge(w_lo, after(i, NP * NE, NP * (n - 1) + p + 1))
                            if n == 0:
                                sp.wait_ge(s_lo, NP * SHARED_PARTS)
                            sp.dma_start(raw[p][0:rows], weights(w13[bass.ds(e, 1)], w2[bass.ds(e, 1)], p)
                                         ).then_inc(raw_in[p], 16)
                    elif n % 2 == 0:
                        s = n // 2
                        back = unit_of["s", (2 * s - 3) % NS] - (NU if s < 2 else 0)
                        sp.wait_ge(up_ready, after(i, NU, back + 1))
                        for part in range(2):
                            sp.dma_start(sT[:, s % 2, part].bitcast(F32),
                                         x1T_parts[bass.ds(i * (NS // 2) + s, 1), part].rearrange("a p n -> (a p) n")
                                         ).then_inc(sT_loaded[s % 2], 16)

        @block.scalar
        def _(act):
            for half in range(SHARED_PARTS):
                for p, (cols, rows) in enumerate(PIECES):
                    act.wait_ge(s_in[p], 16 * half + 16)
                    nc.scalar.activation(dst_of(0, half, p, s_up, s_down), raw[p][0:rows], ACT.Copy).then_inc(s_hi, 1)
            act.sem_inc(y_read, NE)
            act.sem_inc(ys_read, NS // 2)
            for n in range(2):
                act.sem_inc(y_stored[n], 16 * NE // 2)
                act.sem_inc(ys_stored[n], 16 * NS // 4)

            def split_weights(i, n):
                back = unit_of["e", (n - 2) % NE] - (NU if n < 2 else 0)
                act.wait_ge(down_ready, after(i, NU, back + 1))
                for p, (cols, rows) in enumerate(PIECES):
                    act.wait_ge(raw_in[p], i * (16 * NE) + (16 * n + 16))
                    nc.scalar.activation(dst_of(0, n % 2, p, up_w, down_w), raw[p][0:rows], ACT.Copy).then_inc(w_hi, 1)

            def turned(i, job):
                n = t_at[job]
                act.wait_ge(t_ready, after(i, NT, n + 1))
                u = job[1]
                if job[0] == "x":
                    e = UNITS[u][1]
                    back = unit_of["e", (e - 2) % NE] - (NU if e < 2 else 0)
                    act.wait_ge(up_ready, after(i, NU, back + 1))
                    nc.scalar.activation(eT[0][:, e % 2], t_ps[:, n % 2], ACT.Copy).then_inc(t_hi, 1)
                else:
                    v = (u - 2) - (NU if job_before(n) else 0)
                    act.wait_ge(down_ready, after(i, NU, v + 1))
                    nc.scalar.activation(hT[0][:, u % 2, 0:2 * P], t_ps[:, n % 2, 0:2 * P], ACT.Copy)
                    nc.scalar.activation(hT[0][0:96, u % 2, 2 * P:3 * P], t_ps[0:96, n % 2, 2 * P:3 * P],
                                         ACT.Copy).then_inc(t_hi, 1)

            def result(i, u, wrapped):
                kind, n = UNITS[u]
                if kind == "s" and n % 2 == 0:
                    return
                act.wait_ge(down_ready, after(i, NU, u + 1 - (NU if wrapped else 0)))
                if kind == "e":
                    per = 16 * NE // 2
                    act.wait_ge(y_stored[n % 2], after(i, per, 16 * (n // 2) - (per if wrapped else 0)))
                    nc.scalar.activation(y_sb[:, n % 2], y_ps[:], ACT.Copy).then_inc(y_read, 1)
                    act.wait_ge(y_read, after(i, NE, n + 1 - (NE if wrapped else 0)))
                    e = i * NE + (n - (NE if wrapped else 0))
                    act.dma_start(y_dram[bass.ds(e, 1)].rearrange("a p n -> (a p) n"), y_sb[:, n % 2]
                                  ).then_inc(y_stored[n % 2], 16)
                else:
                    s = n // 2
                    per = 16 * NS // 4
                    act.wait_ge(ys_stored[s % 2], after(i, per, 16 * (s // 2) - (per if wrapped else 0)))
                    nc.scalar.activation(ys_sb[:, s % 2], ys_ps[:], ACT.Copy).then_inc(ys_read, 1)
                    act.wait_ge(ys_read, after(i, NS // 2, s + 1 - (NS // 2 if wrapped else 0)))
                    t = i * (NS // 2) + (s - (NS // 2 if wrapped else 0))
                    act.dma_start(shared_dram[bass.ds(t * P, P)], ys_sb[:, s % 2]).then_inc(ys_stored[s % 2], 16)

            def body(i, first):
                for u, (kind, n) in enumerate(UNITS):
                    if not (first and u == 0):
                        turned(i, ("h", (u - 1) % NU))
                    if u == 0 and kind == "e":
                        turned(i, ("x", 0))
                    if kind == "e":
                        split_weights(i, n)
                    if u + 1 < NU and UNITS[u + 1][0] == "e":
                        turned(i, ("x", u + 1))
                    act.wait_ge(up_ready, after(i, NU, u + 1))
                    act.wait_ge(h_ready, after(i, NU, u - 1))
                    nc.scalar.activation(act_sb[:, u % 2], h_ps[:, u % 2, 0, 0:INTER], ACT.Silu).then_inc(silu_ready, 1)
                    if not (first and u == 0):
                        result(i, (u - 1) % NU, u == 0)

            body(0, True)
            with act.Fori(1, BODIES) as i:
                body(i, False)
            turned(BODIES, ("h", NU - 1))
            result(BODIES, NU - 1, True)
            for n in range(2):
                act.wait_ge(y_stored[n], (16 * NE // 2) * (BODIES + 1))
                act.wait_ge(ys_stored[n], (16 * NS // 4) * (BODIES + 1))

        @block.vector
        def _(dve):
            for half in range(SHARED_PARTS):
                for p, (cols, rows) in enumerate(PIECES):
                    dve.wait_ge(s_hi, NP * half + p + 1)
                    nc.vector.tensor_tensor(dst_of(1, half, p, s_up, s_down), raw[p][0:rows],
                                            dst_of(0, half, p, s_up, s_down).bitcast(F32),
                                            ALU.subtract).then_inc(s_lo, 1)
            dve.sem_inc(w_lo, NP * NE)
            dve.sem_inc(t_lo, NT)
            dve.sem_inc(h_ready, NU)

            def split_weights(i, n):
                for p, (cols, rows) in enumerate(PIECES):
                    dve.wait_ge(w_hi, i * (NP * NE) + (NP * n + p + 1))
                    nc.vector.tensor_tensor(dst_of(1, n % 2, p, up_w, down_w), raw[p][0:rows],
                                            dst_of(0, n % 2, p, up_w, down_w).bitcast(F32),
                                            ALU.subtract).then_inc(w_lo, 1)

            def turned(i, job):
                n = t_at[job]
                dve.wait_ge(t_hi, i * NT + n)
                u = job[1]
                if job[0] == "x":
                    e = UNITS[u][1]
                    nc.vector.tensor_tensor(eT[1][:, e % 2], t_ps[:, n % 2], eT[0][:, e % 2].bitcast(F32),
                                            ALU.subtract).then_inc(t_lo, 1)
                else:
                    nc.vector.tensor_tensor(hT[1][:, u % 2, 0:2 * P], t_ps[:, n % 2, 0:2 * P],
                                            hT[0][:, u % 2, 0:2 * P].bitcast(F32), ALU.subtract)
                    nc.vector.tensor_tensor(hT[1][0:96, u % 2, 2 * P:3 * P], t_ps[0:96, n % 2, 2 * P:3 * P],
                                            hT[0][0:96, u % 2, 2 * P:3 * P].bitcast(F32),
                                            ALU.subtract).then_inc(t_lo, 1)

            def body(i, first):
                for u, (kind, n) in enumerate(UNITS):
                    if not (first and u == 0):
                        turned(i, ("h", (u - 1) % NU))
                    if u == 0 and kind == "e":
                        turned(i, ("x", 0))
                    if kind == "e":
                        split_weights(i, n)
                    if u + 1 < NU and UNITS[u + 1][0] == "e":
                        turned(i, ("x", u + 1))
                    dve.wait_ge(silu_ready, i * NU + (u + 1))
                    job = t_at["h", (u - 2) % NU]
                    if u >= 2:
                        dve.wait_ge(t_ready, after(i, NT, job + 1))
                    elif u == 1:
                        dve.wait_ge(t_ready, after(i, NT, 1))
                    else:
                        dve.wait_ge(t_ready, after(i, NT, t_at["h", NU - 2] + 1 - NT))
                    nc.vector.tensor_tensor(h_sb[:, u % 2], act_sb[:, u % 2], h_ps[:, u % 2, 1, 0:INTER],
                                            ALU.mult).then_inc(h_ready, 1)

            body(0, True)
            with dve.Fori(1, BODIES) as i:
                body(i, False)
            turned(BODIES, ("h", NU - 1))

        @block.tensor
        def _(pe):
            pe.sem_inc(t_ready, NT + 1)
            pe.sem_inc(up_ready, NU)
            pe.sem_inc(down_ready, NU)
            pe.wait_ge(pool_const, 1)
            pe.wait_ge(s_lo, NP * SHARED_PARTS)

            def turn(i, job):
                n = t_at[job]
                pe.wait_ge(t_lo, after(i, NT, n - 2))
                u = job[1]
                if job[0] == "x":
                    e = UNITS[u][1]
                    pe.wait_ge(rows_loaded[e % 2], i * (16 * NE // 2) + (16 * (e // 2) + 16))
                    for d in range(DT):
                        mark = nc.tensor.transpose(t_ps[:, n % 2, d * P:(d + 1) * P],
                                                   rows_in[:, e % 2, d * P:(d + 1) * P], ident[:])
                else:
                    pe.wait_ge(h_ready, after(i, NU, u + 1 - (NU if job_before(n) else 0)))
                    for k, (first, rows) in enumerate(INTER_TILES):
                        mark = nc.tensor.transpose(t_ps[0:rows, n % 2, k * P:(k + 1) * P],
                                                   h_sb[:, u % 2, first:first + rows], ident[:])
                mark.then_inc(t_ready, 1)

            def up(i, u):
                kind, n = UNITS[u]
                pe.wait_ge(h_ready, after(i, NU, u - 1))
                if kind == "e":
                    pe.wait_ge(t_lo, after(i, NT, t_at["x", u]))
                    pe.wait_ge(w_lo, after(i, NP * NE, NP * n + DT))
                    lhs = [eT[m][:, n % 2] for m in range(2)]
                    rhs = [up_w[m][:, n % 2] for m in range(2)]
                else:
                    s = n // 2
                    pe.wait_ge(sT_loaded[s % 2], i * (32 * NS // 4) + (32 * (s // 2) + 32))
                    lhs = [sT[:, s % 2, m] for m in range(2)]
                    rhs = [s_up[m][:, n % 2] for m in range(2)]
                for k in range(2):
                    for d in range(DT):
                        for a, b in PASSES:
                            mark = nc.tensor.matmul(h_ps[:, u % 2, k, 0:INTER], lhs[a][:, d * P:(d + 1) * P],
                                                    rhs[b][:, d, k * INTER:(k + 1) * INTER],
                                                    start=d == 0 and (a, b) == PASSES[0],
                                                    stop=d == DT - 1 and (a, b) == PASSES[-1])
                mark.then_inc(up_ready, 1)

            def down(i, u, wrapped):
                kind, n = UNITS[u]
                back = NU if wrapped else 0
                pe.wait_ge(t_lo, after(i, NT, t_at["h", u]))
                if kind == "e":
                    pe.wait_ge(y_read, after(i, NE, n - (NE if wrapped else 0)))
                    pe.wait_ge(w_lo, after(i, NP * NE, NP * (n + 1) - (NP * NE if wrapped else 0)))
                    dst, rhs, opens, closes = y_ps, [down_w[m][:, n % 2] for m in range(2)], True, True
                else:
                    s = n // 2
                    pe.wait_ge(ys_read, after(i, NS // 2, s - (NS // 2 if wrapped else 0)))
                    dst, rhs, opens, closes = ys_ps, [s_down[m][:, n % 2] for m in range(2)], n % 2 == 0, n % 2 == 1
                for k, (first, rows) in enumerate(INTER_TILES):
                    for a, b in PASSES:
                        mark = nc.tensor.matmul(dst[:], hT[a][0:rows, u % 2, k * P:(k + 1) * P],
                                                rhs[b][0:rows, k],
                                                start=opens and k == 0 and (a, b) == PASSES[0],
                                                stop=closes and k == IT - 1 and (a, b) == PASSES[-1])
                mark.then_inc(down_ready, 1)

            def body(i, first):
                for u, (kind, n) in enumerate(UNITS):
                    if not (first and u == 0):
                        turn(i, ("h", (u - 1) % NU))
                    if u == 0 and kind == "e":
                        turn(i, ("x", 0))
                    up(i, u)
                    if u + 1 < NU and UNITS[u + 1][0] == "e":
                        turn(i, ("x", u + 1))
                    if not (first and u == 0):
                        down(i, (u - 1) % NU, u == 0)

            body(0, True)
            with pe.Fori(1, BODIES) as i:
                body(i, False)
            turn(BODIES, ("h", NU - 1))
            down(BODIES, NU - 1, True)


def combine(nc, y_dram, shared_dram, x1_dram, out_rows, routes):
    slot_of, gate_of = routes
    with ExitStack() as ctx:
        def sb(name, shape, dt=F32):
            return ctx.enter_context(nc.sbuf_tensor(name, shape, dt))

        def sem(name):
            return ctx.enter_context(nc.semaphore(name))

        NB = 2
        STEPS = TOPK + 10
        rows = sb("rows", [P, NB, TOPK, DM])
        shared = sb("shared", [P, NB, DM])
        x1 = sb("x1c", [P, NB, DM])
        acc = sb("acc", [P, 2, DM])
        y = sb("yc", [P, NB, DM])
        slot = sb("slotc", [P, NB, TOPK], U32)
        gate = sb("gatec", [P, NB, TOPK])
        stats = sb("statsc", [P, 6])
        mv = sb("mvc", [P, 2])
        small = sb("smallc", [P, 16])
        eps = sb("epsc", [P, 1])

        waited = sem("waited5")
        cleared = sem("cleared")
        slots_ready = sem("slots_ready")
        gathered = [sem(f"gathered{n}") for n in range(NB)]
        loaded = [sem(f"loaded{n}") for n in range(NB)]
        summed = sem("summed")
        chain = sem("chain5")
        rooted = sem("rooted5")
        y_ready = sem("y_ready")
        stored = [sem(f"stored{n}") for n in range(NB)]
        block = ctx.enter_context(nc.Block())

        @block.gpsimd
        def _(pool):
            flat = y_dram.rearrange("e c d -> (e c) d")
            last_slot = nc.gpsimd.to_reg(SLOTS - 1)
            pool.wait_ge(cleared, 1)
            with pool.Fori(0, TILES // NB) as i:
                for b in range(NB):
                    pool.wait_ge(summed, after(i, NB, b - 1))
                    wait_apart(pool, waited, slots_ready, i * NB + (b + 1))
                    for k in range(TOPK):
                        nc.gpsimd.indirect_dma_start(
                            rows[:, b, k], None, flat, bass.IndirectOffsetOnAxis(ap=slot[:, b, k:k + 1], axis=0),
                            bounds_check=last_slot, oob_is_err=False).then_inc(gathered[b], 16)

        @block.sync
        def _(sp):
            with sp.Fori(0, TILES // NB) as i:
                for b in range(NB):
                    t = i * NB + b
                    sp.wait_ge(summed, after(i, NB, b - 1))
                    sp.dma_start(shared[:, b], shared_dram[bass.ds(t * P, P)]).then_inc(loaded[b], 16)
                    sp.dma_start(x1[:, b], x1_dram[bass.ds(t * P, P)]).then_inc(loaded[b], 16)

        @block.scalar
        def _(act):
            for b in range(NB):
                act.sem_inc(stored[b], 16)
            with act.Fori(0, TILES // NB) as i:
                for b in range(NB):
                    t = i * NB + b
                    act.wait_ge(chain, i * (NB * STEPS) + (b * STEPS + TOPK + 4))
                    nc.scalar.activation(small[:, 0:1], mv[:, 1:2], ACT.Sqrt, bias=eps[:]).then_inc(rooted, 1)
                    act.wait_ge(y_ready, i * NB + (b + 1))
                    act.dma_start(out_rows[bass.ds(t * P, P)], y[:, b]).then_inc(stored[b], 16)
            for b in range(NB):
                act.wait_ge(stored[b], 16 * TILES // NB + 16)

        @block.vector
        def _(dve):
            done = [0, 0]

            def step(ins, waited=None):
                done[0] += 1
                ins.then_inc(chain, 1)
                if waited:
                    wait_apart(dve, waited, chain, done[1] * (NB * STEPS) + done[0])
                else:
                    dve.wait_ge(chain, done[1] * (NB * STEPS) + done[0])

            nc.vector.memset(eps[:], EPS)
            nc.vector.memset(rows[:], 0.0).then_inc(cleared, 1)
            dve.sem_inc(summed, NB)
            dve.wait_ge(cleared, 1)

            def places(i, b):
                nc.vector.tensor_copy(gate[:, b], gate_of[:, bass.ds(i * NB + b, 1)].rearrange("p a k -> p (a k)"))
                nc.vector.tensor_copy(slot[:, b], slot_of[:, bass.ds(i * NB + b, 1)].rearrange("p a k -> p (a k)")
                                      ).then_inc(slots_ready, 1)

            def body(i, last):
                done[:] = [0, i]
                for b in range(NB):
                    dve.wait_ge(slots_ready, i * NB + (b + 1))
                    dve.wait_ge(loaded[b], i * 32 + 32)
                    step(nc.vector.tensor_tensor(acc[:, 1], shared[:, b], x1[:, b], ALU.add))
                    dve.wait_ge(gathered[b], i * (16 * TOPK) + 16 * TOPK)
                    for k in range(TOPK):
                        ins = nc.vector.scalar_tensor_tensor(acc[:, k % 2], rows[:, b, k], gate[:, b, k:k + 1],
                                                             acc[:, (k + 1) % 2], ALU.mult, ALU.add)
                        step(ins)
                    a = acc[:, (TOPK - 1) % 2]
                    nc.vector.bn_stats(stats[:], a).then_inc(summed, 1)
                    if not last:
                        places(i + 1, b)
                    wait_apart(dve, waited, summed, after(i, NB, b + 1))
                    step(nc.vector.bn_aggr(mv[:], stats[:]))
                    step(nc.vector.tensor_scalar(small[:, 1:2], mv[:, 1:2], EPS, None, ALU.add))
                    step(nc.vector.tensor_copy(small[:, 10:11], small[:, 1:2]))
                    dve.wait_ge(rooted, i * NB + (b + 1))
                    step(nc.vector.reciprocal(small[:, 2:3], small[:, 0:1]))
                    newton(nc, step, small)
                    dve.wait_ge(stored[b], after(i, 16, 0))
                    nc.vector.tensor_scalar(y[:, b], a, mv[:, 0:1], small[:, 2:3], ALU.subtract,
                                            ALU.mult).then_inc(y_ready, 1)
                    dve.wait_ge(y_ready, i * NB + (b + 1))
                    assert done[0] == STEPS * (b + 1), done

            places(0, 0)
            places(0, 1)
            with dve.Fori(0, TILES // NB - 1) as i:
                body(i, False)
            body(TILES // NB - 1, True)


def post_ln_layer(nc, xT, x_rows, w_qkv, w_o, gate_w, w13, w2, s13, s2, out):
    def dram(name, shape):
        return nc.dram_tensor(name, shape, F32, kind="Internal").ap()

    x_parts = dram("x_parts", [CHUNKS, 2, P, DT * CHUNK])
    z_dram = dram("z_dram", [HEADS, P, SEQ])
    gathered_x = dram("gathered_x", [EXPERTS, CAPACITY, DM])
    x1_dram = dram("x1_dram", [SEQ, DM])
    x1T_parts = dram("x1T_parts", [TILES, 2, P, DT * P])
    y_dram = dram("y_dram", [EXPERTS, CAPACITY, DM])
    shared_dram = dram("shared_dram", [SEQ, DM])
    with (
        nc.sbuf_tensor("slot_of", [P, TILES, TOPK], U32) as slot_of,
        nc.sbuf_tensor("gate_of", [P, TILES, TOPK], F32) as gate_of,
    ):
        split_x(nc, xT, x_parts)
        attention(nc, x_parts, w_qkv, z_dram, gathered_x)
        project_and_route(nc, z_dram, w_o, gate_w, x_rows, x1_dram, x1T_parts, gathered_x, (slot_of, gate_of))
        experts(nc, gathered_x, x1T_parts, w13, w2, s13, s2, y_dram, shared_dram)
        combine(nc, y_dram, shared_dram, x1_dram, out, (slot_of, gate_of))


def lay_out(name, a, np):
    a = {k: np.asarray(v) for k, v in a.items()}
    if name == "x_rows":
        return a["L0_attn_x"].reshape(SEQ, DM)
    if name == "xT":
        return a["L0_attn_x"].reshape(CHUNKS, CHUNK, DT, P).transpose(0, 3, 2, 1).reshape(CHUNKS, P, DT * CHUNK)
    if name == "w_qkv":
        qk = np.stack([a["L0_attn_W_Q"], a["L0_attn_W_K"]], 1).reshape(PAIRS, 4 * DH, DM)
        v = a["L0_attn_W_V"].reshape(PAIRS, 2 * DH, DM)
        return np.concatenate([qk, v], 1).transpose(0, 2, 1).reshape(PAIRS, DT, P, 6 * DH)
    if name == "w_o":
        return a["L0_attn_W_O"].reshape(DM, HEADS, DH).transpose(2, 1, 0)
    if name == "gate_w":
        return a["L0_ffn_gate_w"].reshape(EXPERTS, DT, P).transpose(2, 1, 0)
    if name == "w13":
        w = np.concatenate([a["L0_ffn_w1"], a["L0_ffn_w3"]], 1)
        return w.reshape(EXPERTS, 2 * INTER, DT, P).transpose(0, 3, 2, 1)
    if name == "w2":
        return a["L0_ffn_w2"].transpose(0, 2, 1)
    if name == "s13":
        w = np.concatenate([a[n].reshape(SHARED_PARTS, INTER, DM) for n in ("L0_ffn_sw1", "L0_ffn_sw3")], 1)
        return w.reshape(SHARED_PARTS, 2 * INTER, DT, P).transpose(0, 3, 2, 1)
    if name == "s2":
        return a["L0_ffn_sw2"].T.reshape(SHARED_PARTS, INTER, DM)


def kernel(**inputs):
    import numpy as _np
    import concourse.bacc as _bacc
    from concourse import mybir as _mybir
    from concourse.bass_utils import run_bass_kernel_spmd as _run

    nc = _bacc.Bacc("TRN2", target_bir_lowering=False, num_devices=1)
    arrays, args = {}, []
    for name in ("xT", "x_rows", "w_qkv", "w_o", "gate_w", "w13", "w2", "s13", "s2"):
        a = _np.ascontiguousarray(lay_out(name, inputs, _np))
        arrays[f"in_{name}"] = a
        args.append(nc.dram_tensor(f"in_{name}", a.shape, _mybir.dt.from_np(a.dtype), kind="ExternalInput").ap())
    out = nc.dram_tensor("out", (SEQ, DM), F32, kind="ExternalOutput").ap()
    post_ln_layer(nc, *args, out)
    r = _run(nc, [arrays], core_ids=[0])
    return r.results[0]["out"].reshape(1, SEQ, DM)
```

```python
from contextlib import ExitStack

import numpy as np

import concourse.bass as bass
from concourse import mybir

P = 128
F32 = mybir.dt.float32
F32R = mybir.dt.float32r
BF16 = mybir.dt.bfloat16
I32 = mybir.dt.int32
U32 = mybir.dt.uint32
ALU = mybir.AluOpType
ACT = mybir.ActivationFunctionType
AX_X = mybir.AxisListType.X

SEQ, DM, HEADS, DH = 2048, 512, 16, 128
EXPERTS, INTER, TOPK, CAPACITY = 64, 352, 6, 128
SHARED_PARTS = 2
EPS = 1e-5
MASKED = -1.0e10
LOG_LEAST = -87.3365

DT = DM // P
CHUNK = 512
CHUNKS = SEQ // CHUNK
RPC = CHUNK // P
TILES = SEQ // P
PAIRS = HEADS // 2
SCALE = float(1.0 / np.sqrt(np.float32(DH)))
INTER_TILES = [(0, 128), (128, 128), (256, 96)]
SLOTS = EXPERTS * CAPACITY

PASSES = ((0, 0), (0, 1), (1, 0))


def after(i, per, k):
    return i * per + (per + k)


def wait_apart(eng, waited, sem, value):
    eng.wait_ge(sem, value)
    eng.sem_inc(waited, 1)


def split_x(nc, xT, x_parts):
    with ExitStack() as ctx:
        raw = ctx.enter_context(nc.sbuf_tensor("x_raw", [P, CHUNKS, DT * CHUNK], F32))
        hi = ctx.enter_context(nc.sbuf_tensor("x_split_hi", [P, CHUNKS, DT * CHUNK], F32R))
        lo = ctx.enter_context(nc.sbuf_tensor("x_split_lo", [P, CHUNKS, DT * CHUNK], F32R))
        loaded = [ctx.enter_context(nc.semaphore(f"x_loaded{c}")) for c in range(CHUNKS)]
        hi_made = ctx.enter_context(nc.semaphore("x_hi_made"))
        lo_made = ctx.enter_context(nc.semaphore("x_lo_made"))
        stored = ctx.enter_context(nc.semaphore("x_parts_stored"))
        block = ctx.enter_context(nc.Block())

        @block.sync
        def _(sp):
            for c in range(CHUNKS):
                sp.dma_start(raw[:, c], xT[c]).then_inc(loaded[c], 16)
            for c in range(CHUNKS):
                sp.wait_ge(hi_made, c + 1)
                sp.dma_start(x_parts[c, 0], hi[:, c].bitcast(F32)).then_inc(stored, 16)
                sp.wait_ge(lo_made, c + 1)
                sp.dma_start(x_parts[c, 1], lo[:, c].bitcast(F32)).then_inc(stored, 16)
            sp.wait_ge(stored, 16 * 2 * CHUNKS)

        @block.scalar
        def _(act):
            for c in range(CHUNKS):
                act.wait_ge(loaded[c], 16)
                nc.scalar.activation(hi[:, c], raw[:, c], ACT.Copy).then_inc(hi_made, 1)

        @block.vector
        def _(dve):
            for c in range(CHUNKS):
                dve.wait_ge(loaded[c], 16)
                dve.wait_ge(hi_made, c + 1)
                nc.vector.tensor_tensor(lo[:, c], raw[:, c], hi[:, c].bitcast(F32),
                                        ALU.subtract).then_inc(lo_made, 1)


def attention_plan():
    units = [(h, c) for c in range(CHUNKS) for h in range(2)]
    plan = []
    AHEAD = 2

    def tiles_of(u):
        h, c = units[u]
        n = RPC * (c + 1)
        steps = [("turn", h, c, j) for j in range(min(AHEAD, n))]
        for j in range(n):
            if j + AHEAD < n:
                steps.append(("turn", h, c, j + AHEAD))
            steps.append(("pv", h, c, j))
        return steps

    def between(u, r):
        if u == len(units):
            return [], [[], [("q", 0, 0)], [("k", 0, 0)], [("q", 0, 1), ("k", 0, 1)]][r]
        h, c = units[u]
        if h == 1:
            if c + 1 == CHUNKS:
                return [], []
            return [[], [], [], [("q", c + 1, 0)]][r], [[], [], [("k", c + 1, 0)], []][r]
        if c == 0:
            return [], [[("v", 0, 0)], [("v", 0, 1)], [], []][r]
        return [], [[("k", c, 1)], [("q", c, 1)], [("v", c, 0)], [("v", c, 1)]][r]

    for u in range(len(units) + 1):
        behind = tiles_of(u - 1) if u else []
        per = -(-len(behind) // RPC)
        norm_at = RPC - 1 if u < len(units) else 1
        for r in range(RPC):
            first, last = between(u, r)
            if u < len(units):
                plan.append(("row", *units[u], r))
            if u and r == norm_at:
                plan.append(("norm", *units[u - 1]))
            plan += [("job", *job) for job in first]
            plan += behind[r * per:(r + 1) * per]
            if u and r == 0:
                plan.append(("inverse", *units[u - 1]))
            plan += [("job", *job) for job in last]
        if u:
            plan.append(("out", *units[u - 1]))
    return plan, units


def attention(nc, x_parts, w_qkv, z_dram, gathered_x):
    plan, units = attention_plan()
    BANKS = 4
    TURNS = 3

    jobs = []
    for step in plan:
        if step[0] == "job":
            jobs.append(step[1:])
        if step[0] == "row":
            _, h, c, r = step
            jobs += [("s", h, c, r, kc) for kc in range(c + 1)]
        if step[0] == "norm":
            jobs.append(step)
    early = [("q", 0, 0), ("k", 0, 0), ("q", 0, 1), ("k", 0, 1)]
    assert len(jobs) % BANKS == 0 and jobs[-len(early):] == early
    job_at = {job: n for n, job in enumerate(jobs)}
    turn_at = {s: n for n, s in enumerate(s for s in plan if s[0] == "turn")}
    pv_at = {("turn", *s[1:]): n for n, s in enumerate(s for s in plan if s[0] == "pv")}
    unit_at = {unit: n for n, unit in enumerate(units)}
    turns = list(turn_at)
    n_jobs, n_turns, n_units = len(jobs), len(turns), len(unit_at)
    scores_jobs = [j for j in jobs if j[0] == "s"]
    proj_jobs = [j for j in jobs if j[0] in "qkv"]
    exp_at = {j: n for n, j in enumerate(scores_jobs)}
    proj_at = {j: n for n, j in enumerate(proj_jobs)}
    rows = [s[1:] for s in plan if s[0] == "row"]
    row_at = {s: n for n, s in enumerate(rows)}
    n_exp, n_proj, n_rows = len(scores_jobs), len(proj_jobs), len(rows)

    w_load_steps = [("row", 0, 1, 0), ("row", 0, 2, 0), ("row", 1, CHUNKS - 1, 1), ("row", 1, CHUNKS - 1, 2)]
    w_split_steps = [("row", 1, CHUNKS - 1, r) for r in range(RPC)]

    def widths(c, r, kc):
        used = CHUNK if kc < c else (r + 1) * P
        return used, max(used, 2 * P)

    with ExitStack() as ctx:
        def sb(name, shape, dt):
            return ctx.enter_context(nc.sbuf_tensor(name, shape, dt))

        def ps(name, shape, dt=F32):
            return ctx.enter_context(nc.psum_tensor(name, shape, dt))

        def sem(name):
            return ctx.enter_context(nc.semaphore(name))

        x_sb = sb("x_sb", [P, 2, DT, CHUNK], F32R)
        w_raw = sb("w_raw", [P, 2, 6 * DH], F32)
        w_sb = [sb(f"w_{n}", [P, DT, 6 * DH], F32R) for n in ("hi", "lo")]
        q_sb = [sb(f"q_{n}", [P, 2, CHUNK], F32R) for n in ("hi", "lo")]
        k_sb = [sb(f"k_{n}", [P, 2, SEQ], F32R) for n in ("hi", "lo")]
        v_sb = [sb(f"v_{n}", [P, TILES, 2 * DH], F32R) for n in ("hi", "lo")]
        probs = sb("probs", [P, 2, RPC, SEQ], F32)
        pT_sb = [sb(f"pT_{n}", [P, TURNS, CHUNK], F32R) for n in ("hi", "lo")]
        diag = [sb(f"diag_{n}", [P, RPC, P], F32R) for n in ("hi", "lo")]
        spread_sb = sb("spread_sb", [P, CHUNK], F32)
        z_sb = sb("z_sb", [P, 2, CHUNK], F32)
        ident = sb("ident", [P, P], F32)
        ident_bf = sb("ident_bf", [P, P], BF16)
        causal_bf = sb("causal_bf", [P, P], BF16)
        ones = sb("ones", [P, P], F32R)
        zeros = sb("zeros", [P, P], F32)
        max_part = sb("max_part", [P, 2, CHUNKS], F32)
        row_max = sb("row_max", [P, 2], F32)
        neg_max = sb("neg_max", [P, 2], F32)
        sums = sb("sums", [P, 2, RPC, CHUNKS], F32)
        total = sb("total", [P, 2, RPC], F32)
        inv = sb("inv", [P, 2, RPC], F32)

        bank = ps("bank", [P, BANKS, CHUNK])
        turned = ps("turned", [P, TURNS, CHUNK])
        z_ps = ps("z_ps", [P, CHUNK])

        const_step = sem("const_step")
        pool_const = sem("pool_const")
        act_const = sem("act_const")
        dve_const = sem("dve_const")
        x_in = sem("x_in")
        w_in = [sem(f"w_in{n}") for n in range(2)]
        w_hi_made = sem("w_hi_made")
        w_split = sem("w_split")
        job_ready = sem("job_ready")
        proj_hi = sem("proj_hi")
        proj_lo = sem("proj_lo")
        part_done = sem("part_done")
        max_done = sem("max_done")
        bias_done = sem("bias_done")
        exp_done = sem("exp_done")
        turn_ready = sem("turn_ready")
        turn_hi = sem("turn_hi")
        turn_lo = sem("turn_lo")
        pv_done = sem("pv_done")
        sum_step = sem("sum_step")
        diag_done = sem("diag_done")
        spread_done = sem("spread_done")
        z_done = sem("z_done")
        z_out = [sem(f"z_out{n}") for n in range(2)]
        zero_out = sem("zero_out")
        block = ctx.enter_context(nc.Block())

        def ring_back(n):
            if n >= TURNS:
                return TURNS
            last = max(m for m in range(n_turns) if m % TURNS == n)
            return n + n_turns - last

        def proj_dst(part, job):
            kind, c, m = job
            if kind == "q":
                return q_sb[part][:, m, :]
            if kind == "k":
                return k_sb[part][:, m, c * CHUNK:(c + 1) * CHUNK]
            t = c * RPC + 2 * m
            return v_sb[part][:, t:t + 2, :].rearrange("p t n -> p (t n)")

        @block.gpsimd
        def _(pool):
            nc.gpsimd.memset(zeros[:], 0.0).then_inc(pool_const, 1)
            nc.gpsimd.memset(ident[:], 0.0).then_inc(const_step, 1)
            nc.gpsimd.memset(causal_bf[:], 0.0).then_inc(const_step, 1)
            pool.wait_ge(const_step, 2)
            nc.gpsimd.affine_select(out=ident[:], in_=ident[:], compare_op=ALU.not_equal, fill=1.0,
                                    base=0, pattern=[[-1, P]], channel_multiplier=1).then_inc(pool_const, 1)
            nc.gpsimd.affine_select(out=causal_bf[:], in_=causal_bf[:], compare_op=ALU.is_ge, fill=MASKED,
                                    base=0, pattern=[[-1, P]], channel_multiplier=1).then_inc(pool_const, 1)

        @block.sync
        def _(sp):
            sp.wait_ge(pool_const, 3)
            zero_src = zeros[:, :].rearrange("p (a n) -> p a n", a=1).to_broadcast([P, DM // P, P])
            for dt in range(2):
                sp.dma_start(w_raw[:, dt], w_qkv[0, dt]).then_inc(w_in[dt % 2], 16)
            for dt in range(2, DT):
                sp.wait_ge(w_split, dt - 1)
                sp.dma_start(w_raw[:, dt % 2], w_qkv[0, dt]).then_inc(w_in[dt % 2], 16)
            def load_x(c):
                sp.dma_start(x_sb[:, 0].bitcast(F32), x_parts[c, 0].rearrange("p (t n) -> p t n", t=DT)).then_inc(x_in, 16)
                sp.dma_start(x_sb[:, 1].bitcast(F32), x_parts[c, 1].rearrange("p (t n) -> p t n", t=DT)).then_inc(x_in, 16)

            load_x(0)
            with sp.Fori(0, PAIRS) as i:
                for step in plan:
                    if step[0:2] == ("job", "v") and step[3] == 1:
                        c = step[2]
                        sp.wait_ge(job_ready, after(i, n_jobs, job_at["v", c, 1] + 1))
                        load_x((c + 1) % CHUNKS)
                        for n in range(EXPERTS // PAIRS // CHUNKS):
                            e = i * (EXPERTS // PAIRS) + (c * (EXPERTS // PAIRS // CHUNKS) + n)
                            sp.dma_start(gathered_x[bass.ds(e, 1)].rearrange("a p (t n) -> (a p) t n", n=P),
                                         zero_src).then_inc(zero_out, 16)
                    if step in w_load_steps:
                        dt = w_load_steps.index(step)
                        sp.wait_ge(w_split, i * DT + (DT + dt - 1))
                        sp.dma_start(w_raw[:, dt % 2], w_qkv[bass.ds((i + 1) % PAIRS, 1), dt]
                                     .rearrange("a p n -> (a p) n")).then_inc(w_in[dt % 2], 16)
            sp.wait_ge(x_in, 32 * (CHUNKS * PAIRS + 1))
            sp.wait_ge(zero_out, 16 * EXPERTS)

        @block.scalar
        def _(act):
            act.wait_ge(pool_const, 3)
            nc.scalar.activation(ident_bf[:], ident[:], ACT.Copy).then_inc(act_const, 1)

            def split_w(base, pieces=range(DT)):
                for dt in pieces:
                    act.wait_ge(w_in[dt % 2], base * (16 // 2) + (16 * (dt // 2) + 16))
                    nc.scalar.activation(w_sb[0][:, dt], w_raw[:, dt % 2], ACT.Copy).then_inc(w_hi_made, 1)

            split_w(0)
            act.sem_inc(exp_done, n_exp)
            act.sem_inc(proj_hi, n_proj - len(early))
            act.sem_inc(spread_done, n_units)
            for n in range(2):
                act.sem_inc(z_out[n], 8 * n_units)

            def project(i, job):
                act.wait_ge(job_ready, after(i, n_jobs, job_at[job] + 1))
                nc.scalar.activation(proj_dst(0, job), bank[:, job_at[job] % BANKS], ACT.Copy).then_inc(proj_hi, 1)

            for job in early:
                project(-1, job)
            with act.Fori(0, PAIRS) as i:
                def exp(h, c, r, kc):
                    row, u = row_at[h, c, r], unit_at[h, c]
                    if kc == 0:
                        act.wait_ge(bias_done, i * n_rows + (row + 1))
                        act.wait_ge(diag_done, after(i, n_units, u - 1))
                    used, _ = widths(c, r, kc)
                    nc.scalar.activation(probs[:, u % 2, r, kc * CHUNK:kc * CHUNK + used],
                                         bank[:, job_at["s", h, c, r, kc] % BANKS, 0:used], ACT.Exp,
                                         bias=neg_max[:, row % 2:row % 2 + 1], scale=SCALE,
                                         accum_out=sums[:, u % 2, r, kc:kc + 1]).then_inc(exp_done, 1)

                def turn(s):
                    n = turn_at[s]
                    lo_col = max(0, s[3] - RPC * s[2]) * P
                    act.wait_ge(turn_ready, i * n_turns + (n + 1))
                    act.wait_ge(pv_done, after(i, n_turns, n - ring_back(n) + 1))
                    nc.scalar.activation(pT_sb[0][:, n % TURNS, lo_col:], turned[:, n % TURNS, lo_col:],
                                         ACT.Copy).then_inc(turn_hi, 1)

                def store_z(u):
                    h, c = units[u]
                    dst = z_dram[c * RPC:(c + 1) * RPC, :, bass.ds(i * 2 + h, 1), :].rearrange("t p a n -> p (t a) n")
                    act.dma_start(dst, z_sb[:, u % 2].rearrange("p (t n) -> p t n", n=P)).then_inc(z_out[u % 2], 16)

                late = []
                for step in plan:
                    straight_after_row = step[0] == "job" and step[1] == "q" and step[2] > 0 and step[3] == 0
                    if step[0] not in ("turn", "pv", "norm") and not straight_after_row:
                        for bank_of_row in late:
                            exp(*bank_of_row)
                        late = []
                    if step[0] in ("job", "norm"):
                        mine = job_at[step[1:] if step[0] == "job" else step]
                        while late and job_at["s", *late[0]] <= mine - BANKS:
                            exp(*late.pop(0))
                    if step[0] == "job":
                        project(i, step[1:])
                    if step[0] == "row":
                        late = [(*step[1:], kc) for kc in range(step[2] + 1)]
                    if step[0] == "turn":
                        turn(step)
                        if late:
                            exp(*late.pop(0))
                    if step[0] == "norm":
                        act.wait_ge(job_ready, after(i, n_jobs, job_at[step] + 1))
                        act.wait_ge(z_done, after(i, n_units, unit_at[step[1:]]))
                        if unit_at[step[1:]]:
                            store_z(unit_at[step[1:]] - 1)
                        nc.scalar.activation(spread_sb[:], bank[:, job_at[step] % BANKS],
                                             ACT.Copy).then_inc(spread_done, 1)
                    if step in w_split_steps:
                        act.wait_ge(job_ready, after(i, n_jobs, job_at["v", CHUNKS - 1, 1] + 1))
                        split_w(i * DT + DT, [w_split_steps.index(step)])
                act.wait_ge(z_done, after(i, n_units, n_units))
                store_z(n_units - 1)
            for n in range(2):
                act.wait_ge(z_out[n], 8 * n_units * (PAIRS + 1))

        @block.vector
        def _(dve):
            nc.vector.memset(spread_sb[:], 1.0).then_inc(dve_const, 1)
            dve.wait_ge(dve_const, 1)
            nc.vector.tensor_copy(ones[:], spread_sb[:, 0:P]).then_inc(dve_const, 1)
            dve.sem_inc(proj_lo, n_proj - len(early))
            dve.sem_inc(turn_lo, n_turns)
            dve.sem_inc(diag_done, n_units)
            dve.sem_inc(z_done, n_units)

            def split_w(base, pieces=range(DT)):
                for dt in pieces:
                    dve.wait_ge(w_hi_made, base + (dt + 1))
                    nc.vector.tensor_tensor(w_sb[1][:, dt], w_raw[:, dt % 2], w_sb[0][:, dt].bitcast(F32),
                                            ALU.subtract).then_inc(w_split, 1)

            split_w(0)
            dve.wait_ge(pool_const, 3)

            def project(i, job):
                dve.wait_ge(proj_hi, after(i, n_proj, proj_at[job] + 1))
                nc.vector.tensor_tensor(proj_dst(1, job), bank[:, job_at[job] % BANKS],
                                        proj_dst(0, job).bitcast(F32), ALU.subtract).then_inc(proj_lo, 1)

            for job in early:
                project(-1, job)
            with dve.Fori(0, PAIRS) as i:
                def maxima(h, c, r):
                    row = row_at[h, c, r]
                    first = exp_at["s", h, c, r, 0]
                    if row >= 2:
                        h2, c2, r2 = rows[row - 2]
                        dve.wait_ge(exp_done, after(i, n_exp, exp_at["s", h2, c2, r2, c2] + 1))
                    else:
                        dve.wait_ge(exp_done, after(i, n_exp, 0))
                    for kc in range(c + 1):
                        job = ("s", h, c, r, kc)
                        used, _ = widths(c, r, kc)
                        dve.wait_ge(job_ready, after(i, n_jobs, job_at[job] + 1))
                        dst = max_part[:, row % 2, kc:kc + 1]
                        nc.vector.reduce_max(dst, bank[:, job_at[job] % BANKS, 0:used],
                                             axis=AX_X).then_inc(part_done, 1)
                    dve.wait_ge(part_done, i * n_exp + (first + c + 1))
                    nc.vector.reduce_max(row_max[:, row % 2:row % 2 + 1], max_part[:, row % 2, 0:c + 1],
                                         axis=AX_X).then_inc(max_done, 1)
                    dve.wait_ge(max_done, i * n_rows + (row + 1))
                    nc.vector.tensor_scalar(neg_max[:, row % 2:row % 2 + 1], row_max[:, row % 2:row % 2 + 1],
                                            -SCALE, None, ALU.mult).then_inc(bias_done, 1)

                def inverse(h, c):
                    u = unit_at[h, c]
                    dve.wait_ge(exp_done, after(i, n_exp, exp_at["s", h, c, RPC - 1, c] + 1))
                    nc.vector.reduce_sum(total[:, u % 2], sums[:, u % 2, :, 0:c + 1], axis=AX_X).then_inc(sum_step, 1)
                    dve.wait_ge(sum_step, i * (3 * n_units) + (3 * u + 1))
                    nc.vector.reciprocal(inv[:, u % 2], total[:, u % 2]).then_inc(sum_step, 1)
                    dve.wait_ge(sum_step, i * (3 * n_units) + (3 * u + 2))
                    dve.wait_ge(spread_done, after(i, n_units, u))
                    for r in range(RPC):
                        mark = nc.vector.tensor_scalar(diag[0][:, r], ident[:], inv[:, u % 2, r:r + 1], None,
                                                       ALU.mult)
                    mark.then_inc(sum_step, 1)
                    dve.wait_ge(sum_step, i * (3 * n_units) + (3 * u + 3))
                    for r in range(RPC):
                        mark = nc.vector.scalar_tensor_tensor(diag[1][:, r], ident[:], inv[:, u % 2, r:r + 1],
                                                              diag[0][:, r].bitcast(F32), ALU.mult, ALU.subtract)
                    mark.then_inc(diag_done, 1)

                for step in plan:
                    if step[0] == "job":
                        project(i, step[1:])
                    if step[0] == "row":
                        maxima(*step[1:])
                    if step[0] == "turn":
                        n = turn_at[step]
                        lo_col = max(0, step[3] - RPC * step[2]) * P
                        dve.wait_ge(turn_hi, i * n_turns + (n + 1))
                        nc.vector.tensor_tensor(pT_sb[1][:, n % TURNS, lo_col:], turned[:, n % TURNS, lo_col:],
                                                pT_sb[0][:, n % TURNS, lo_col:].bitcast(F32),
                                                ALU.subtract).then_inc(turn_lo, 1)
                    if step[0] == "inverse":
                        inverse(*step[1:])
                    if step[0] == "out":
                        u = unit_at[step[1:]]
                        last = pv_at["turn", *step[1:], RPC * (step[2] + 1) - 1]
                        dve.wait_ge(pv_done, after(i, n_turns, last + 1))
                        dve.wait_ge(spread_done, after(i, n_units, u + 1))
                        dve.wait_ge(z_out[u % 2], i * (8 * n_units) + (8 * n_units + 16 * (u // 2)))
                        nc.vector.tensor_tensor(z_sb[:, u % 2], z_ps[:], spread_sb[:], ALU.mult).then_inc(z_done, 1)
                    if step in w_split_steps:
                        split_w(i * DT + DT, [w_split_steps.index(step)])

        @block.tensor
        def _(pe):
            pe.sem_inc(job_ready, n_jobs - len(early))
            pe.sem_inc(pv_done, n_turns)
            pe.wait_ge(pool_const, 3)
            pe.wait_ge(act_const, 1)
            pe.wait_ge(dve_const, 2)

            def take(i, n):
                m = n - BANKS
                old = jobs[m]
                back = 0 if m >= 0 else 1
                if old[0] == "s":
                    pe.wait_ge(exp_done, after(i, n_exp, exp_at[old] + 1 - back * n_exp))
                elif old[0] == "norm":
                    pe.wait_ge(spread_done, after(i, n_units, unit_at[old[1:]] + 1 - back * n_units))
                else:
                    pe.wait_ge(proj_lo, after(i, n_proj, proj_at[old] + 1 - back * n_proj))
                return bank[:, n % BANKS]

            def project(i, job):
                kind, c, m = job
                if job in early:
                    pe.wait_ge(x_in, i * (32 * CHUNKS) + 32 * (CHUNKS + 1))
                    pe.wait_ge(w_split, i * DT + 2 * DT)
                else:
                    pe.wait_ge(x_in, i * (32 * CHUNKS) + 32 * (c + 1))
                dst = take(i, job_at[job])
                if kind == "v":
                    for t in range(2):
                        rows_ = slice((2 * m + t) * P, (2 * m + t + 1) * P)
                        for dt in range(DT):
                            for a, b in PASSES:
                                mark = nc.tensor.matmul(dst[:, t * 2 * DH:(t + 1) * 2 * DH],
                                                        x_sb[:, a, dt, rows_], w_sb[b][:, dt, 4 * DH:],
                                                        start=(dt == 0 and (a, b) == PASSES[0]),
                                                        stop=(dt == DT - 1 and (a, b) == PASSES[-1]))
                else:
                    first = (2 * m + "qk".index(kind)) * DH
                    for dt in range(DT):
                        for a, b in PASSES:
                            mark = nc.tensor.matmul(dst, w_sb[a][:, dt, first:first + DH], x_sb[:, b, dt, :],
                                                    start=(dt == 0 and (a, b) == PASSES[0]),
                                                    stop=(dt == DT - 1 and (a, b) == PASSES[-1]))
                mark.then_inc(job_ready, 1)

            for job in early:
                project(-1, job)
            with pe.Fori(0, PAIRS) as i:
                def scores(h, c, r):
                    if r == 0:
                        later = max(proj_at["q", c, h], proj_at["k", c, h])
                        pe.wait_ge(proj_lo, after(i, n_proj, later + 1 - (0 if c else n_proj)))
                    for kc in range(c + 1):
                        n = job_at["s", h, c, r, kc]
                        dst = take(i, n)
                        used, width = widths(c, r, kc)
                        for a, b in PASSES:
                            mark = nc.tensor.matmul(dst[:, 0:width], q_sb[a][:, h, r * P:(r + 1) * P],
                                                    k_sb[b][:, h, kc * CHUNK:kc * CHUNK + width],
                                                    start=(a, b) == PASSES[0], stop=(a, b) == PASSES[-1])
                            if kc == c and (a, b) == PASSES[0]:
                                nc.tensor.matmul(dst[:, r * P:(r + 1) * P], ident_bf[:], causal_bf[:],
                                                 start=False, stop=False, skip_group_check=True)
                        mark.then_inc(job_ready, 1)

                def turn(s):
                    _, h, c, j = s
                    n, u = turn_at[s], unit_at[h, c]
                    first = max(0, j - RPC * c)
                    if j == 0:
                        pe.wait_ge(exp_done, after(i, n_exp, exp_at["s", h, c, RPC - 1, c] + 1))
                    pe.wait_ge(turn_lo, after(i, n_turns, n - ring_back(n) + 1))
                    for r in range(first, RPC):
                        mark = nc.tensor.transpose(turned[:, n % TURNS, r * P:(r + 1) * P],
                                                   probs[:, u % 2, r, j * P:(j + 1) * P], ident[:])
                    mark.then_inc(turn_ready, 1)

                def value(s):
                    _, h, c, j = s
                    n = turn_at["turn", h, c, j]
                    first = max(0, j - RPC * c)
                    if j == 0:
                        pe.wait_ge(z_done, after(i, n_units, unit_at[h, c]))
                    if j == RPC * c:
                        pe.wait_ge(proj_lo, after(i, n_proj, proj_at["v", c, 1] + 1))
                    pe.wait_ge(turn_lo, after(i, n_turns, n + 1))
                    for a, b in PASSES:
                        mark = nc.tensor.matmul(z_ps[:, first * P:], v_sb[a][:, j, h * DH:(h + 1) * DH],
                                                pT_sb[b][:, n % TURNS, first * P:],
                                                start=(j == 0 and (a, b) == PASSES[0]),
                                                stop=(j == RPC * (c + 1) - 1 and (a, b) == PASSES[-1]),
                                                skip_group_check=True)
                    mark.then_inc(pv_done, 1)

                for step in plan:
                    if step[0] == "job":
                        project(i, step[1:])
                    if step[0] == "row":
                        scores(*step[1:])
                    if step[0] == "turn":
                        turn(step)
                    if step[0] == "pv":
                        value(step)
                    if step[0] == "norm":
                        dst = take(i, job_at[step])
                        pe.wait_ge(diag_done, after(i, n_units, unit_at[step[1:]] + 1))
                        for part in range(2):
                            mark = nc.tensor.matmul(dst, ones[:], diag[part][:].rearrange("p r n -> p (r n)"),
                                                    start=part == 0, stop=part == 1)
                        mark.then_inc(job_ready, 1)


def project_and_route(nc, z_dram, w_o, gate_w, x_rows, x1_dram, x1T_parts, gathered_x, routes):
    slot_of, gate_of = routes
    BIG = 1 << 20

    with ExitStack() as ctx:
        def sb(name, shape, dt=F32):
            return ctx.enter_context(nc.sbuf_tensor(name, shape, dt))

        def ps(name, shape, dt=F32):
            return ctx.enter_context(nc.psum_tensor(name, shape, dt))

        def sem(name):
            return ctx.enter_context(nc.semaphore(name))

        NB = 2
        wo_raw = sb("wo_raw", [P, 2, DM])
        wo = [sb(f"wo_{n}", [P, HEADS, DM], F32R) for n in ("hi", "lo")]
        gw = sb("gw", [P, DT, EXPERTS])
        z_raw = sb("z_raw", [P, NB, HEADS, P])
        z = [sb(f"z_{n}", [P, NB, HEADS, P], F32R) for n in ("hi", "lo")]
        xr = sb("xr", [P, NB, DM])
        y = sb("y", [P, NB, DM])
        x1 = sb("x1", [P, NB, DM])
        x1T = sb("x1T", [P, NB, DT, P])
        xT_part = [sb(f"x1T_{n}", [P, NB, DT, P], F32R) for n in ("hi", "lo")]
        stats = sb("stats", [P, 6])
        mv = sb("mv", [P, 2])
        small = sb("small", [P, 16])
        eps = sb("eps", [P, 1])
        lg = sb("lg", [P, EXPERTS])
        lg_c = sb("lg_c", [P, EXPERTS])
        ex = sb("ex", [P, EXPERTS])
        top = sb("top", [P, 8])
        top_e = sb("top_e", [P, 8])
        gate = sb("gate", [P, TOPK])
        idx = sb("idx", [P, 8], U32)
        idx_f = sb("idx_f", [P, 8])
        pick = sb("pick", [P, TOPK, EXPERTS])
        pick_pos = sb("pick_pos", [P, TOPK, EXPERTS])
        chosen = sb("chosen", [P, EXPERTS])
        chosen_bf = sb("chosen_bf", [P, EXPERTS], BF16)
        count = sb("count", [P, EXPERTS])
        pos_all = sb("pos_all", [P, EXPERTS])
        slot = sb("slot", [P, NB, TOPK], U32)
        pos = sb("pos", [P, TOPK])
        full = sb("full", [P, TOPK])
        room = sb("room", [P, TOPK])
        place = sb("place", [P, TOPK])
        place2 = sb("place2", [P, TOPK])
        iota_i = sb("iota_i", [P, EXPERTS], I32)
        iota_f = sb("iota_f", [P, EXPERTS])
        ident = sb("ident3", [P, P])
        before_bf = sb("before_bf", [P, P], BF16)
        ones_bf = sb("ones_bf", [P, P], BF16)

        o_ps = ps("o_ps", [P, 2, DM])
        t_ps = ps("t_ps", [P, DT * P])
        l_ps = ps("l_ps", [P, EXPERTS])
        c_ps = ps("c_ps", [P, 2, EXPERTS])

        credits = sem("credits")
        waited = sem("waited3")
        pool_step = sem("pool_step")
        pool_const = sem("pool_const3")
        dve_const = sem("dve_const3")
        wo_in = [sem(f"wo_in{n}") for n in range(2)]
        wo_hi = sem("wo_hi")
        wo_split = sem("wo_split")
        gw_in = sem("gw_in")
        z_in = [sem(f"z_in{n}") for n in range(NB)]
        x_in = [sem(f"xr_in{n}") for n in range(NB)]
        z_hi = sem("z_hi")
        z_lo = sem("z_lo")
        out_ready = sem("out_ready")
        out_read = sem("out_read")
        rooted = sem("rooted")
        x1_ready = sem("x1_ready")
        x1_stored = [sem(f"x1_stored{n}") for n in range(NB)]
        t_ready = sem("t_ready")
        t_read = sem("t_read")
        t_hi = sem("t_hi")
        t_split = sem("t_split")
        t_stored = [sem(f"t_stored{n}") for n in range(NB)]
        l_ready = sem("l_ready")
        l_read = sem("l_read")
        exp_ready = sem("exp_ready")
        chosen_ready = sem("chosen_ready")
        c_ready = sem("c_ready")
        c_read = sem("c_read")
        placed = sem("placed")
        moved = sem("moved")
        rows_left = sem("rows_left")
        chain = sem("chain3")
        block = ctx.enter_context(nc.Block())
        STEPS = 27

        @block.gpsimd
        def _(pool):
            nc.gpsimd.memset(ident[:], 0.0).then_inc(pool_step, 1)
            nc.gpsimd.memset(before_bf[:], 1.0).then_inc(pool_step, 1)
            nc.gpsimd.iota(iota_i[:], pattern=[[1, EXPERTS]], base=0, channel_multiplier=0).then_inc(pool_const, 1)
            pool.wait_ge(pool_step, 2)
            nc.gpsimd.affine_select(out=ident[:], in_=ident[:], compare_op=ALU.not_equal, fill=1.0,
                                    base=0, pattern=[[-1, P]], channel_multiplier=1).then_inc(pool_const, 1)
            nc.gpsimd.affine_select(out=before_bf[:], in_=before_bf[:], compare_op=ALU.is_gt, fill=0.0,
                                    base=0, pattern=[[1, P]], channel_multiplier=-1).then_inc(pool_const, 1)
            flat = gathered_x.rearrange("e c d -> (e c) d")
            last_slot = nc.gpsimd.to_reg(SLOTS - 1)
            pool.sem_inc(rows_left, NB)
            with pool.Fori(0, TILES // NB) as i:
                for b in range(NB):
                    wait_apart(pool, waited, placed, after(i, NB, b + 1))
                    for k in range(TOPK):
                        nc.gpsimd.indirect_dma_start(
                            flat, bass.IndirectOffsetOnAxis(ap=slot[:, b, k:k + 1], axis=0), x1[:, b], None,
                            bounds_check=last_slot, oob_is_err=False).then_inc(moved, 16)
                    pool.wait_ge(moved, (i * NB + (b + 1)) * (16 * TOPK))
                    pool.sem_inc(rows_left, 1)

        @block.sync
        def _(sp):
            sp.dma_start(gw[:], gate_w).then_inc(gw_in, 16)
            for h in range(HEADS):
                if h >= 2:
                    sp.wait_ge(wo_split, h - 1)
                sp.dma_start(wo_raw[:, h % 2], w_o[:, h]).then_inc(wo_in[h % 2], 16)

            def load(i, b):
                t = i * NB + b
                sp.dma_start(z_raw[:, b], z_dram[bass.ds(t, 1)].rearrange("a p h n -> (a p) h n")
                             ).then_inc(z_in[b], 16)
                sp.dma_start(xr[:, b], x_rows[bass.ds(t * P, P)]).then_inc(x_in[b], 16)

            def tiles(i, last):
                for b in range(NB):
                    t = i * NB + b
                    sp.wait_ge(x1_ready, after(i, NB, b + 1))
                    sp.dma_start(x1_dram[bass.ds(t * P, P)], x1[:, b]).then_inc(x1_stored[b], 16)
                    sp.wait_ge(t_split, after(i, NB, b + 1))
                    for part in range(2):
                        sp.dma_start(x1T_parts[bass.ds(t, 1), part].rearrange("a p n -> (a p) n"),
                                     xT_part[part][:, b].rearrange("p t n -> p (t n)").bitcast(F32)
                                     ).then_inc(t_stored[b], 16)
                    if not last:
                        sp.wait_ge(z_lo, after(i, NB, b + 1))
                        sp.wait_ge(out_read, after(i, NB, b + 1))
                        load(i + 1, b)

            load(0, 0)
            load(0, 1)
            for b in range(NB):
                sp.sem_inc(x1_stored[b], 16)
                sp.sem_inc(t_stored[b], 32)
            with sp.Fori(0, TILES // NB - 1) as i:
                tiles(i, False)
            tiles(TILES // NB - 1, True)
            for b in range(NB):
                sp.wait_ge(x1_stored[b], 16 * TILES // NB + 16)
                sp.wait_ge(t_stored[b], 32 * TILES // NB + 32)

        @block.scalar
        def _(act):
            for h in range(HEADS):
                act.wait_ge(wo_in[h % 2], 16 * (h // 2) + 16)
                nc.scalar.activation(wo[0][:, h], wo_raw[:, h % 2], ACT.Copy).then_inc(wo_hi, 1)

            def split(i, b):
                act.wait_ge(z_in[b], i * 16 + 16)
                act.wait_ge(out_ready, after(i, NB, b - 1))
                nc.scalar.activation(z[0][:, b], z_raw[:, b], ACT.Copy).then_inc(z_hi, 1)

            def tiles(i, last):
                for b in range(NB):
                    if b + 1 < NB:
                        split(i, b + 1)
                    elif not last:
                        split(i + 1, 0)
                    act.wait_ge(chain, i * (NB * STEPS) + (b * STEPS + 3))
                    nc.scalar.activation(small[:, 0:1], mv[:, 1:2], ACT.Sqrt, bias=eps[:]).then_inc(rooted, 1)
                    act.wait_ge(t_ready, i * NB + (b + 1))
                    act.wait_ge(l_ready, after(i, NB, b - 1))
                    nc.scalar.activation(x1T[:, b].rearrange("p t n -> p (t n)"), t_ps[:], ACT.Copy
                                         ).then_inc(t_read, 1)
                    act.wait_ge(t_stored[b], after(i, 32, 0))
                    nc.scalar.activation(xT_part[0][:, b].rearrange("p t n -> p (t n)"), t_ps[:], ACT.Copy
                                         ).then_inc(t_hi, 1)
                    act.wait_ge(l_read, after(i, NB, b + 1))
                    nc.scalar.activation(ex[:], lg_c[:], ACT.Exp, accum_out=small[:, 4:5]).then_inc(exp_ready, 1)

            act.wait_ge(credits, 1)
            split(0, 0)
            with act.Fori(0, TILES // NB - 1) as i:
                tiles(i, False)
            tiles(TILES // NB - 1, True)

        @block.tensor
        def _(pe):
            pe.wait_ge(wo_split, HEADS)
            pe.wait_ge(pool_const, 3)
            pe.wait_ge(dve_const, 3)
            pe.wait_ge(gw_in, 16)
            pe.sem_inc(out_ready, NB)
            pe.sem_inc(l_ready, NB)
            pe.sem_inc(credits, 1)

            def project(i, b):
                pe.wait_ge(z_lo, after(i, NB, b + 1))
                pe.wait_ge(out_read, after(i, NB, b - 1))
                for h in range(HEADS):
                    for m, n in PASSES:
                        mark = nc.tensor.matmul(o_ps[:, b], z[m][:, b, h], wo[n][:, h],
                                                start=h == 0 and (m, n) == PASSES[0],
                                                stop=h == HEADS - 1 and (m, n) == PASSES[-1])
                mark.then_inc(out_ready, 1)

            def tiles(i, last):
                for b in range(NB):
                    if b + 1 < NB:
                        project(i, b + 1)
                    elif not last:
                        project(i + 1, 0)
                    pe.wait_ge(x1_ready, after(i, NB, b + 1))
                    pe.wait_ge(t_split, after(i, NB, b))
                    for d in range(DT):
                        mark = nc.tensor.transpose(t_ps[:, d * P:(d + 1) * P], x1[:, b, d * P:(d + 1) * P], ident[:])
                    mark.then_inc(t_ready, 1)
                    pe.wait_ge(t_read, i * NB + (b + 1))
                    pe.wait_ge(l_read, after(i, NB, b))
                    for d in range(DT):
                        mark = nc.tensor.matmul(l_ps[:], x1T[:, b, d], gw[:, d], start=d == 0, stop=d == DT - 1)
                    mark.then_inc(l_ready, 1)
                    pe.wait_ge(chosen_ready, i * NB + (b + 1))
                    pe.wait_ge(c_read, after(i, NB, b))
                    nc.tensor.matmul(c_ps[:, 0], before_bf[:], chosen_bf[:], start=True, stop=True)
                    nc.tensor.matmul(c_ps[:, 1], ones_bf[:], chosen_bf[:], start=True, stop=True).then_inc(c_ready, 1)

            project(0, 0)
            with pe.Fori(0, TILES // NB - 1) as i:
                tiles(i, False)
            tiles(TILES // NB - 1, True)

        @block.vector
        def _(dve):
            done = [0, 0]

            def step(ins, waited=None):
                done[0] += 1
                ins.then_inc(chain, 1)
                if waited:
                    wait_apart(dve, waited, chain, done[1] * (NB * STEPS) + done[0])
                else:
                    dve.wait_ge(chain, done[1] * (NB * STEPS) + done[0])

            nc.vector.memset(eps[:], EPS).then_inc(dve_const, 1)
            nc.vector.memset(ones_bf[:], 1.0).then_inc(dve_const, 1)
            nc.vector.memset(count[:], 0.0).then_inc(dve_const, 1)
            dve.wait_ge(dve_const, 3)
            for h in range(HEADS):
                dve.wait_ge(wo_hi, h + 1)
                nc.vector.tensor_tensor(wo[1][:, h], wo_raw[:, h % 2], wo[0][:, h].bitcast(F32),
                                        ALU.subtract).then_inc(wo_split, 1)
            dve.wait_ge(pool_const, 3)
            nc.vector.tensor_copy(iota_f[:], iota_i[:]).then_inc(dve_const, 1)

            for free in (z_lo, out_read, x1_ready, t_split, l_read, c_read, placed):
                dve.sem_inc(free, NB)

            def split(i, b):
                dve.wait_ge(z_hi, i * NB + (b + 1))
                nc.vector.tensor_tensor(z[1][:, b], z_raw[:, b], z[0][:, b].bitcast(F32),
                                        ALU.subtract).then_inc(z_lo, 1)

            def tile(i, b, last):
                t = i * NB + b
                if b + 1 < NB:
                    split(i, b + 1)
                elif not last:
                    split(i + 1, 0)
                dve.wait_ge(out_ready, after(i, NB, b + 1))
                dve.wait_ge(x_in[b], i * 16 + 16)
                nc.vector.tensor_tensor(y[:, b], o_ps[:, b], xr[:, b], ALU.add).then_inc(out_read, 1)
                dve.wait_ge(out_read, after(i, NB, b + 1))
                step(nc.vector.bn_stats(stats[:], y[:, b]), waited)
                step(nc.vector.bn_aggr(mv[:], stats[:]))
                step(nc.vector.tensor_scalar(small[:, 1:2], mv[:, 1:2], EPS, None, ALU.add))
                dve.wait_ge(rooted, i * NB + (b + 1))
                step(nc.vector.reciprocal(small[:, 2:3], small[:, 0:1]))
                newton(nc, step, small)
                dve.wait_ge(x1_stored[b], after(i, 16, 0))
                dve.wait_ge(rows_left, after(i, NB, b - 1))
                nc.vector.tensor_scalar(x1[:, b], y[:, b], mv[:, 0:1], small[:, 2:3], ALU.subtract,
                                        ALU.mult).then_inc(x1_ready, 1)
                dve.wait_ge(t_hi, i * NB + (b + 1))
                dve.wait_ge(t_stored[b], after(i, 32, 0))
                nc.vector.tensor_tensor(xT_part[1][:, b].rearrange("p t n -> p (t n)"), t_ps[:],
                                        xT_part[0][:, b].rearrange("p t n -> p (t n)").bitcast(F32),
                                        ALU.subtract).then_inc(t_split, 1)
                dve.wait_ge(l_ready, after(i, NB, b + 1))
                step(nc.vector.reduce_max(small[:, 3:4], l_ps[:], axis=AX_X))
                nc.vector.tensor_scalar(lg_c[:], l_ps[:], small[:, 3:4], LOG_LEAST, ALU.subtract,
                                        ALU.max).then_inc(l_read, 1)
                wait_apart(dve, waited, l_read, after(i, NB, b + 1))
                step(nc.vector.max(top[:], lg_c[:]), waited)
                step(nc.vector.max_index(idx[:], top[:], lg_c[:]))
                step(nc.vector.tensor_copy(idx_f[:], idx[:]))
                step(nc.vector.tensor_tensor(
                    pick[:], iota_f[:].rearrange("p (k e) -> p k e", k=1).to_broadcast([P, TOPK, EXPERTS]),
                    idx_f[:, 0:TOPK].rearrange("p (k e) -> p k e", e=1).to_broadcast([P, TOPK, EXPERTS]),
                    ALU.is_equal))
                step(nc.vector.reduce_sum(chosen[:], pick[:].rearrange("p k e -> p e k"), axis=AX_X))
                nc.vector.tensor_copy(chosen_bf[:], chosen[:]).then_inc(chosen_ready, 1)
                dve.wait_ge(exp_ready, i * NB + (b + 1))
                step(nc.vector.tensor_tensor(pick_pos[:], pick[:], ex[:].rearrange("p (k e) -> p k e", k=1)
                                             .to_broadcast([P, TOPK, EXPERTS]), ALU.mult))
                step(nc.vector.reduce_sum(top_e[:, 0:TOPK], pick_pos[:], axis=AX_X))
                step(nc.vector.reciprocal(small[:, 5:6], small[:, 4:5]))
                step(nc.vector.tensor_scalar(gate[:], top_e[:, 0:TOPK], small[:, 5:6], None, ALU.mult))
                dve.wait_ge(c_ready, i * NB + (b + 1))
                step(nc.vector.tensor_tensor(pos_all[:], c_ps[:, 0], count[:], ALU.add))
                nc.vector.tensor_tensor(count[:], c_ps[:, 1], count[:], ALU.add).then_inc(c_read, 1)
                dve.wait_ge(c_read, after(i, NB, b + 1))
                step(nc.vector.tensor_tensor(pick_pos[:], pick[:], pos_all[:].rearrange("p (k e) -> p k e", k=1)
                                             .to_broadcast([P, TOPK, EXPERTS]), ALU.mult))
                step(nc.vector.reduce_sum(pos[:], pick_pos[:], axis=AX_X))
                step(nc.vector.tensor_scalar(full[:], pos[:], float(CAPACITY), float(BIG), ALU.is_ge, ALU.mult))
                step(nc.vector.tensor_scalar(room[:], pos[:], float(CAPACITY), None, ALU.is_lt))
                step(nc.vector.scalar_tensor_tensor(place[:], idx_f[:, 0:TOPK], float(CAPACITY), pos[:],
                                                    ALU.mult, ALU.add))
                step(nc.vector.tensor_tensor(gate_of[:, bass.ds(t, 1)].rearrange("p a k -> p (a k)"), gate[:], room[:], ALU.mult))
                step(nc.vector.tensor_tensor(slot_of[:, bass.ds(t, 1)].rearrange("p a k -> p (a k)"), place[:], full[:],
                                             ALU.add))
                nc.vector.tensor_tensor(slot[:, b], place[:], full[:], ALU.add).then_inc(placed, 1)
                assert done[0] == STEPS * (b + 1), done

            def tiles(i, last):
                done[:] = [0, i]
                for b in range(NB):
                    tile(i, b, last)

            dve.wait_ge(dve_const, 4)
            split(0, 0)
            with dve.Fori(0, TILES // NB - 1) as i:
                tiles(i, False)
            tiles(TILES // NB - 1, True)


def newton(nc, step, s):
    step(nc.vector.tensor_tensor(s[:, 6:7], s[:, 2:3], s[:, 2:3], ALU.mult))
    step(nc.vector.scalar_tensor_tensor(s[:, 7:8], s[:, 6:7], -0.5, s[:, 1:2], ALU.mult, ALU.mult))
    step(nc.vector.tensor_scalar(s[:, 8:9], s[:, 7:8], 1.5, None, ALU.add))
    step(nc.vector.tensor_tensor(s[:, 9:10], s[:, 8:9], s[:, 2:3], ALU.mult))
    step(nc.vector.tensor_copy(s[:, 2:3], s[:, 9:10]))


def experts(nc, gathered_x, x1T_parts, w13, w2, s13, s2, y_dram, shared_dram):
    with ExitStack() as ctx:
        def sb(name, shape, dt=F32):
            return ctx.enter_context(nc.sbuf_tensor(name, shape, dt))

        def ps(name, shape, dt=F32):
            return ctx.enter_context(nc.psum_tensor(name, shape, dt))

        def sem(name):
            return ctx.enter_context(nc.semaphore(name))

        BODIES = 8
        NE = EXPERTS // BODIES
        NS = TILES * SHARED_PARTS // BODIES
        UNITS = [("s", u // 3) if u % 3 == 2 else ("e", 2 * (u // 3) + u % 3) for u in range(NE + NS)]
        NU = len(UNITS)
        unit_of = {unit: u for u, unit in enumerate(UNITS)}
        PIECES = [(2 * INTER, P)] * DT + [(DM, rows) for _, rows in INTER_TILES]
        NP = len(PIECES)
        IT = len(INTER_TILES)
        UP, DOWN = range(DT), range(DT, NP)
        pieces_of_step = []
        for e in range(0, NE, 2):
            pieces_of_step += [[(e + 1, p) for p in UP[2:]] + [(e, p) for p in DOWN],
                               [(e + 1, p) for p in DOWN] + [(e + 2, p) for p in UP[:2]],
                               [(e + 2, p) for p in UP[2:]] + [(e + 3, p) for p in UP[:2]]]
        pieces = [piece for step in pieces_of_step for piece in step]
        NQ = len(pieces)
        EARLY = [q for q in range(NQ) if pieces[q][0] >= NE]
        assert EARLY == list(range(EARLY[0], NQ)) and len(pieces_of_step) == NU
        SLOTS_RAW = 8
        assert NQ % SLOTS_RAW == 0
        PER_SLOT = 16 * NQ // SLOTS_RAW
        shared_of_step = {0: range(0, DT), 1: range(DT, NP), 3: range(NP, NP + DT), 4: range(NP + DT, 2 * NP)}

        def piece_at(n, p):
            return pieces.index((n, p)) if (n, p) in pieces else pieces.index((n + NE, p)) - NQ

        raw = sb("w_raw4", [P, SLOTS_RAW, 2 * INTER])
        s_raw = sb("s_raw", [P, 2, 2 * INTER])
        up_w = [sb(f"up_{n}", [P, 2, DT, 2 * INTER], F32R) for n in ("hi", "lo")]
        down_w = [sb(f"down_{n}", [P, 2, IT, DM], F32R) for n in ("hi", "lo")]
        s_up = [sb(f"s_up_{n}", [P, SHARED_PARTS, DT, 2 * INTER], F32R) for n in ("hi", "lo")]
        s_down = [sb(f"s_down_{n}", [P, SHARED_PARTS, IT, DM], F32R) for n in ("hi", "lo")]
        rows_in = sb("rows_in", [P, 2, DM])
        eT = [sb(f"eT_{n}", [P, 2, DT * P], F32R) for n in ("hi", "lo")]
        sT = sb("sT", [P, 2, 2, DT * P], F32R)
        act_sb = sb("act_sb", [P, 2, INTER])
        h_sb = sb("h_sb", [P, 2, INTER])
        hT = [sb(f"hT_{n}", [P, 2, IT * P], F32R) for n in ("hi", "lo")]
        y_sb = sb("y_sb", [P, 2, DM])
        ys_sb = sb("ys_sb", [P, 2, DM])
        ident = sb("ident4", [P, P])

        t_ps = ps("t4_ps", [P, 2, CHUNK])
        h_ps = ps("h_ps", [P, 2, 2, CHUNK])
        y_ps = ps("y_ps", [P, DM])
        ys_ps = ps("ys_ps", [P, DM])

        tjobs = []
        for u in range(NU):
            tjobs.append(("h", (u - 1) % NU))
            if u == 0 and UNITS[0][0] == "e":
                tjobs.append(("x", 0))
            if u + 1 < NU and UNITS[u + 1][0] == "e":
                tjobs.append(("x", u + 1))
        assert len(tjobs) % 2 == 0 and NU % 2 == 0 and NE % 2 == 0
        NT = len(tjobs)
        t_at = {job: n for n, job in enumerate(tjobs)}

        pool_step = sem("pool_step4")
        pool_const = sem("pool_const4")
        s_in = [sem(f"s_in{n}") for n in range(2)]
        s_hi = sem("s_hi")
        s_lo = sem("s_lo")
        raw_in = [sem(f"raw_in{n}") for n in range(SLOTS_RAW)]
        w_hi = sem("w_hi")
        w_lo = sem("w_lo")
        rows_loaded = [sem(f"rows_loaded{n}") for n in range(2)]
        sT_loaded = [sem(f"sT_loaded{n}") for n in range(2)]
        t_ready = sem("t4_ready")
        t_hi = sem("t4_hi")
        t_lo = sem("t4_lo")
        up_ready = sem("up_ready")
        silu_ready = sem("silu_ready")
        h_ready = sem("h_ready")
        down_ready = sem("down_ready")
        y_read = sem("y_read")
        ys_read = sem("ys_read")
        y_stored = [sem(f"y_stored{n}") for n in range(2)]
        ys_stored = [sem(f"ys_stored{n}") for n in range(2)]
        block = ctx.enter_context(nc.Block())

        def job_before(n):
            return n == 0

        def dst_of(part, n, p, up, down):
            cols, rows = PIECES[p]
            return up[part][:, n, p, :] if p < DT else down[part][0:rows, n, p - DT, :]

        def weights(up_src, down_src, p):
            cols, rows = PIECES[p]
            if p < DT:
                return up_src[:, :, p, :].rearrange("a p n -> (a p) n")
            first = INTER_TILES[p - DT][0]
            return down_src[:, first:first + rows, :].rearrange("a p n -> (a p) n")

        def raw_of(buffer, slot, p):
            cols, rows = PIECES[p]
            return buffer[0:rows, slot, 0:cols]

        @block.gpsimd
        def _(pool):
            nc.gpsimd.memset(ident[:], 0.0).then_inc(pool_step, 1)
            pool.wait_ge(pool_step, 1)
            nc.gpsimd.affine_select(out=ident[:], in_=ident[:], compare_op=ALU.not_equal, fill=1.0,
                                    base=0, pattern=[[-1, P]], channel_multiplier=1).then_inc(pool_const, 1)
            for k in range(SHARED_PARTS * NP):
                half, p = k // NP, k % NP
                if k >= 2:
                    pool.wait_ge(s_lo, k - 1)
                pool.dma_start(raw_of(s_raw, k % 2, p), weights(s13[half:half + 1], s2[half:half + 1], p)
                               ).then_inc(s_in[k % 2], 16)

        @block.sync
        def _(sp):
            for slot in range(SLOTS_RAW):
                sp.sem_inc(raw_in[slot], PER_SLOT - 16 * len([q for q in EARLY if q % SLOTS_RAW == slot]))

            def load_piece(e, q):
                p = pieces[q][1]
                sp.dma_start(raw_of(raw, q % SLOTS_RAW, p), weights(w13[bass.ds(e, 1)], w2[bass.ds(e, 1)], p)
                             ).then_inc(raw_in[q % SLOTS_RAW], 16)

            def load_rows(i, u):
                n = UNITS[u][1]
                back = t_at["x", unit_of["e", (n - 2) % NE]] - (NT if n < 2 else 0)
                sp.wait_ge(t_ready, after(i, NT, back + 1))
                sp.dma_start(rows_in[:, n % 2], gathered_x[bass.ds(i * NE + n, 1)].rearrange("a p n -> (a p) n")
                             ).then_inc(rows_loaded[n % 2], 16)

            for q in EARLY:
                load_piece(pieces[q][0] - NE, q)
            with sp.Fori(0, BODIES) as i:
                load_rows(i, 0)
                for u, (kind, n) in enumerate(UNITS):
                    if u + 1 < NU and UNITS[u + 1][0] == "e":
                        load_rows(i, u + 1)
                    if kind == "s" and n % 2 == 0:
                        s = n // 2
                        back = unit_of["s", (2 * s - 3) % NS] - (NU if s < 2 else 0)
                        sp.wait_ge(up_ready, after(i, NU, back + 1))
                        for part in range(2):
                            sp.dma_start(sT[:, s % 2, part].bitcast(F32),
                                         x1T_parts[bass.ds(i * (NS // 2) + s, 1), part].rearrange("a p n -> (a p) n")
                                         ).then_inc(sT_loaded[s % 2], 16)
                    for piece in pieces_of_step[u]:
                        q = pieces.index(piece)
                        sp.wait_ge(w_lo, after(i, NQ, q - SLOTS_RAW + 1))
                        load_piece((i * NE + piece[0]) % EXPERTS if piece[0] >= NE else i * NE + piece[0], q)
            for slot in range(SLOTS_RAW):
                sp.wait_ge(raw_in[slot], PER_SLOT * (BODIES + 1))

        @block.scalar
        def _(act):
            act.sem_inc(w_hi, NQ - len(EARLY))
            act.sem_inc(y_read, NE)
            act.sem_inc(ys_read, NS // 2)
            for n in range(2):
                act.sem_inc(y_stored[n], 16 * NE // 2)
                act.sem_inc(ys_stored[n], 16 * NS // 4)

            def split_piece(i, q):
                n, p = pieces[q]
                back = unit_of["e", (n - 2) % NE] - (NU if n < 2 else 0)
                act.wait_ge(up_ready if p < DT else down_ready, after(i, NU, back + 1))
                act.wait_ge(raw_in[q % SLOTS_RAW], after(i, PER_SLOT, 16 * (q // SLOTS_RAW) + 16))
                nc.scalar.activation(dst_of(0, n % 2, p, up_w, down_w), raw_of(raw, q % SLOTS_RAW, p),
                                     ACT.Copy).then_inc(w_hi, 1)

            def split_shared(k):
                half, p = k // NP, k % NP
                act.wait_ge(s_in[k % 2], 16 * (k // 2) + 16)
                nc.scalar.activation(dst_of(0, half, p, s_up, s_down), raw_of(s_raw, k % 2, p),
                                     ACT.Copy).then_inc(s_hi, 1)

            def turned(i, job):
                n = t_at[job]
                act.wait_ge(t_ready, after(i, NT, n + 1))
                u = job[1]
                if job[0] == "x":
                    e = UNITS[u][1]
                    back = unit_of["e", (e - 2) % NE] - (NU if e < 2 else 0)
                    act.wait_ge(up_ready, after(i, NU, back + 1))
                    nc.scalar.activation(eT[0][:, e % 2], t_ps[:, n % 2], ACT.Copy).then_inc(t_hi, 1)
                else:
                    v = (u - 2) - (NU if job_before(n) else 0)
                    act.wait_ge(down_ready, after(i, NU, v + 1))
                    nc.scalar.activation(hT[0][:, u % 2, 0:2 * P], t_ps[:, n % 2, 0:2 * P], ACT.Copy)
                    nc.scalar.activation(hT[0][0:96, u % 2, 2 * P:3 * P], t_ps[0:96, n % 2, 2 * P:3 * P],
                                         ACT.Copy).then_inc(t_hi, 1)

            def result(i, u, wrapped):
                kind, n = UNITS[u]
                if kind == "s" and n % 2 == 0:
                    return
                act.wait_ge(down_ready, after(i, NU, u + 1 - (NU if wrapped else 0)))
                if kind == "e":
                    per = 16 * NE // 2
                    act.wait_ge(y_stored[n % 2], after(i, per, 16 * (n // 2) - (per if wrapped else 0)))
                    nc.scalar.activation(y_sb[:, n % 2], y_ps[:], ACT.Copy).then_inc(y_read, 1)
                    act.wait_ge(y_read, after(i, NE, n + 1 - (NE if wrapped else 0)))
                    e = i * NE + (n - (NE if wrapped else 0))
                    act.dma_start(y_dram[bass.ds(e, 1)].rearrange("a p n -> (a p) n"), y_sb[:, n % 2]
                                  ).then_inc(y_stored[n % 2], 16)
                else:
                    s = n // 2
                    per = 16 * NS // 4
                    act.wait_ge(ys_stored[s % 2], after(i, per, 16 * (s // 2) - (per if wrapped else 0)))
                    nc.scalar.activation(ys_sb[:, s % 2], ys_ps[:], ACT.Copy).then_inc(ys_read, 1)
                    act.wait_ge(ys_read, after(i, NS // 2, s + 1 - (NS // 2 if wrapped else 0)))
                    t = i * (NS // 2) + (s - (NS // 2 if wrapped else 0))
                    act.dma_start(shared_dram[bass.ds(t * P, P)], ys_sb[:, s % 2]).then_inc(ys_stored[s % 2], 16)

            def body(i, first):
                for u, (kind, n) in enumerate(UNITS):
                    if not (first and u == 0):
                        turned(i, ("h", (u - 1) % NU))
                    if u == 0 and kind == "e":
                        turned(i, ("x", 0))
                    if not (first and u < 2):
                        result(i, (u - 2) % NU, u < 2)
                    mine = [pieces.index(piece) for piece in pieces_of_step[u]]
                    for q in mine[:3]:
                        split_piece(i, q)
                    act.wait_ge(up_ready, after(i, NU, u + 1))
                    act.wait_ge(h_ready, after(i, NU, u - 1))
                    nc.scalar.activation(act_sb[:, u % 2], h_ps[:, u % 2, 0, 0:INTER], ACT.Silu).then_inc(silu_ready, 1)
                    if u + 1 < NU and UNITS[u + 1][0] == "e":
                        turned(i, ("x", u + 1))
                    for q in mine[3:]:
                        split_piece(i, q)
                    if first:
                        for k in shared_of_step.get(u, ()):
                            split_shared(k)

            for q in EARLY:
                split_piece(-1, q)
            body(0, True)
            with act.Fori(1, BODIES) as i:
                body(i, False)
            turned(BODIES, ("h", NU - 1))
            result(BODIES, NU - 2, True)
            result(BODIES, NU - 1, True)
            for n in range(2):
                act.wait_ge(y_stored[n], (16 * NE // 2) * (BODIES + 1))
                act.wait_ge(ys_stored[n], (16 * NS // 4) * (BODIES + 1))

        @block.vector
        def _(dve):
            dve.sem_inc(w_lo, NQ - len(EARLY))
            dve.sem_inc(t_lo, NT)
            dve.sem_inc(h_ready, NU)

            def split_piece(i, q):
                n, p = pieces[q]
                dve.wait_ge(w_hi, after(i, NQ, q + 1))
                nc.vector.tensor_tensor(dst_of(1, n % 2, p, up_w, down_w), raw_of(raw, q % SLOTS_RAW, p),
                                        dst_of(0, n % 2, p, up_w, down_w).bitcast(F32),
                                        ALU.subtract).then_inc(w_lo, 1)

            def split_shared(k):
                half, p = k // NP, k % NP
                dve.wait_ge(s_hi, k + 1)
                nc.vector.tensor_tensor(dst_of(1, half, p, s_up, s_down), raw_of(s_raw, k % 2, p),
                                        dst_of(0, half, p, s_up, s_down).bitcast(F32),
                                        ALU.subtract).then_inc(s_lo, 1)

            def turned(i, job):
                n = t_at[job]
                dve.wait_ge(t_hi, i * NT + n)
                u = job[1]
                if job[0] == "x":
                    e = UNITS[u][1]
                    nc.vector.tensor_tensor(eT[1][:, e % 2], t_ps[:, n % 2], eT[0][:, e % 2].bitcast(F32),
                                            ALU.subtract).then_inc(t_lo, 1)
                else:
                    nc.vector.tensor_tensor(hT[1][:, u % 2, 0:2 * P], t_ps[:, n % 2, 0:2 * P],
                                            hT[0][:, u % 2, 0:2 * P].bitcast(F32), ALU.subtract)
                    nc.vector.tensor_tensor(hT[1][0:96, u % 2, 2 * P:3 * P], t_ps[0:96, n % 2, 2 * P:3 * P],
                                            hT[0][0:96, u % 2, 2 * P:3 * P].bitcast(F32),
                                            ALU.subtract).then_inc(t_lo, 1)

            def body(i, first):
                for u, (kind, n) in enumerate(UNITS):
                    if not (first and u == 0):
                        turned(i, ("h", (u - 1) % NU))
                    if u == 0 and kind == "e":
                        turned(i, ("x", 0))
                    mine = [pieces.index(piece) for piece in pieces_of_step[u]]
                    for q in mine[:3]:
                        split_piece(i, q)
                    dve.wait_ge(silu_ready, i * NU + (u + 1))
                    job = t_at["h", (u - 2) % NU]
                    if u >= 2:
                        dve.wait_ge(t_ready, after(i, NT, job + 1))
                    elif u == 1:
                        dve.wait_ge(t_ready, after(i, NT, 1))
                    else:
                        dve.wait_ge(t_ready, after(i, NT, t_at["h", NU - 2] + 1 - NT))
                    nc.vector.tensor_tensor(h_sb[:, u % 2], act_sb[:, u % 2], h_ps[:, u % 2, 1, 0:INTER],
                                            ALU.mult).then_inc(h_ready, 1)
                    if u + 1 < NU and UNITS[u + 1][0] == "e":
                        turned(i, ("x", u + 1))
                    for q in mine[3:]:
                        split_piece(i, q)
                    if first:
                        for k in shared_of_step.get(u, ()):
                            split_shared(k)

            for q in EARLY:
                split_piece(-1, q)
            body(0, True)
            with dve.Fori(1, BODIES) as i:
                body(i, False)
            turned(BODIES, ("h", NU - 1))

        @block.tensor
        def _(pe):
            pe.sem_inc(t_ready, NT + 1)
            pe.sem_inc(up_ready, NU)
            pe.sem_inc(down_ready, NU)
            pe.wait_ge(pool_const, 1)

            def turn(i, job):
                n = t_at[job]
                pe.wait_ge(t_lo, after(i, NT, n - 2))
                u = job[1]
                if job[0] == "x":
                    e = UNITS[u][1]
                    pe.wait_ge(rows_loaded[e % 2], i * (16 * NE // 2) + (16 * (e // 2) + 16))
                    for d in range(DT):
                        mark = nc.tensor.transpose(t_ps[:, n % 2, d * P:(d + 1) * P],
                                                   rows_in[:, e % 2, d * P:(d + 1) * P], ident[:])
                else:
                    pe.wait_ge(h_ready, after(i, NU, u + 1 - (NU if job_before(n) else 0)))
                    for k, (first, rows) in enumerate(INTER_TILES):
                        mark = nc.tensor.transpose(t_ps[0:rows, n % 2, k * P:(k + 1) * P],
                                                   h_sb[:, u % 2, first:first + rows], ident[:])
                mark.then_inc(t_ready, 1)

            def up(i, u, first_body):
                kind, n = UNITS[u]
                pe.wait_ge(h_ready, after(i, NU, u - 1))
                if kind == "e":
                    pe.wait_ge(t_lo, after(i, NT, t_at["x", u]))
                    pe.wait_ge(w_lo, after(i, NQ, piece_at(n, DT - 1) + 1))
                    lhs = [eT[m][:, n % 2] for m in range(2)]
                    rhs = [up_w[m][:, n % 2] for m in range(2)]
                else:
                    s = n // 2
                    pe.wait_ge(sT_loaded[s % 2], i * (32 * NS // 4) + (32 * (s // 2) + 32))
                    if first_body:
                        pe.wait_ge(s_lo, NP * (n % 2) + DT)
                    lhs = [sT[:, s % 2, m] for m in range(2)]
                    rhs = [s_up[m][:, n % 2] for m in range(2)]
                for k in range(2):
                    for d in range(DT):
                        for a, b in PASSES:
                            mark = nc.tensor.matmul(h_ps[:, u % 2, k, 0:INTER], lhs[a][:, d * P:(d + 1) * P],
                                                    rhs[b][:, d, k * INTER:(k + 1) * INTER],
                                                    start=d == 0 and (a, b) == PASSES[0],
                                                    stop=d == DT - 1 and (a, b) == PASSES[-1])
                mark.then_inc(up_ready, 1)

            def down(i, u, wrapped, first_body=False):
                kind, n = UNITS[u]
                pe.wait_ge(t_lo, after(i, NT, t_at["h", u]))
                if kind == "e":
                    pe.wait_ge(y_read, after(i, NE, n - (NE if wrapped else 0)))
                    pe.wait_ge(w_lo, after(i, NQ, piece_at(n, NP - 1) + 1 - (NQ if wrapped else 0)))
                    dst, rhs, opens, closes = y_ps, [down_w[m][:, n % 2] for m in range(2)], True, True
                else:
                    s = n // 2
                    pe.wait_ge(ys_read, after(i, NS // 2, s - (NS // 2 if wrapped else 0)))
                    if first_body:
                        pe.wait_ge(s_lo, NP * (n % 2 + 1))
                    dst, rhs, opens, closes = ys_ps, [s_down[m][:, n % 2] for m in range(2)], n % 2 == 0, n % 2 == 1
                for k, (first, rows) in enumerate(INTER_TILES):
                    for a, b in PASSES:
                        mark = nc.tensor.matmul(dst[:], hT[a][0:rows, u % 2, k * P:(k + 1) * P],
                                                rhs[b][0:rows, k],
                                                start=opens and k == 0 and (a, b) == PASSES[0],
                                                stop=closes and k == IT - 1 and (a, b) == PASSES[-1])
                mark.then_inc(down_ready, 1)

            def body(i, first):
                for u, (kind, n) in enumerate(UNITS):
                    if not (first and u == 0):
                        turn(i, ("h", (u - 1) % NU))
                    if u == 0 and kind == "e":
                        turn(i, ("x", 0))
                    up(i, u, first)
                    if u + 1 < NU and UNITS[u + 1][0] == "e":
                        turn(i, ("x", u + 1))
                    if not (first and u == 0):
                        down(i, (u - 1) % NU, u == 0, first)

            body(0, True)
            with pe.Fori(1, BODIES) as i:
                body(i, False)
            turn(BODIES, ("h", NU - 1))
            down(BODIES, NU - 1, True)


def combine(nc, y_dram, shared_dram, x1_dram, out_rows, routes):
    slot_of, gate_of = routes
    with ExitStack() as ctx:
        def sb(name, shape, dt=F32):
            return ctx.enter_context(nc.sbuf_tensor(name, shape, dt))

        def sem(name):
            return ctx.enter_context(nc.semaphore(name))

        NB = 2
        STEPS = TOPK + 10
        rows = sb("rows", [P, NB, TOPK, DM])
        shared = sb("shared", [P, NB, DM])
        x1 = sb("x1c", [P, NB, DM])
        acc = sb("acc", [P, 2, DM])
        y = sb("yc", [P, NB, DM])
        slot = sb("slotc", [P, NB, TOPK], U32)
        gate = sb("gatec", [P, NB, TOPK])
        stats = sb("statsc", [P, 6])
        mv = sb("mvc", [P, 2])
        small = sb("smallc", [P, 16])
        eps = sb("epsc", [P, 1])

        waited = sem("waited5")
        cleared = sem("cleared")
        slots_ready = sem("slots_ready")
        gathered = [sem(f"gathered{n}") for n in range(NB)]
        loaded = [sem(f"loaded{n}") for n in range(NB)]
        summed = sem("summed")
        chain = sem("chain5")
        rooted = sem("rooted5")
        y_ready = sem("y_ready")
        stored = [sem(f"stored{n}") for n in range(NB)]
        block = ctx.enter_context(nc.Block())

        @block.gpsimd
        def _(pool):
            flat = y_dram.rearrange("e c d -> (e c) d")
            last_slot = nc.gpsimd.to_reg(SLOTS - 1)
            pool.wait_ge(cleared, 1)
            with pool.Fori(0, TILES // NB) as i:
                for b in range(NB):
                    pool.wait_ge(summed, after(i, NB, b - 1))
                    wait_apart(pool, waited, slots_ready, i * NB + (b + 1))
                    for k in range(TOPK):
                        nc.gpsimd.indirect_dma_start(
                            rows[:, b, k], None, flat, bass.IndirectOffsetOnAxis(ap=slot[:, b, k:k + 1], axis=0),
                            bounds_check=last_slot, oob_is_err=False).then_inc(gathered[b], 16)

        @block.sync
        def _(sp):
            with sp.Fori(0, TILES // NB) as i:
                for b in range(NB):
                    t = i * NB + b
                    sp.wait_ge(summed, after(i, NB, b - 1))
                    sp.dma_start(shared[:, b], shared_dram[bass.ds(t * P, P)]).then_inc(loaded[b], 16)
                    sp.dma_start(x1[:, b], x1_dram[bass.ds(t * P, P)]).then_inc(loaded[b], 16)

        @block.scalar
        def _(act):
            for b in range(NB):
                act.sem_inc(stored[b], 16)
            with act.Fori(0, TILES // NB) as i:
                for b in range(NB):
                    t = i * NB + b
                    act.wait_ge(chain, i * (NB * STEPS) + (b * STEPS + TOPK + 4))
                    nc.scalar.activation(small[:, 0:1], mv[:, 1:2], ACT.Sqrt, bias=eps[:]).then_inc(rooted, 1)
                    act.wait_ge(y_ready, i * NB + (b + 1))
                    act.dma_start(out_rows[bass.ds(t * P, P)], y[:, b]).then_inc(stored[b], 16)
            for b in range(NB):
                act.wait_ge(stored[b], 16 * TILES // NB + 16)

        @block.vector
        def _(dve):
            done = [0, 0]

            def step(ins, waited=None):
                done[0] += 1
                ins.then_inc(chain, 1)
                if waited:
                    wait_apart(dve, waited, chain, done[1] * (NB * STEPS) + done[0])
                else:
                    dve.wait_ge(chain, done[1] * (NB * STEPS) + done[0])

            nc.vector.memset(eps[:], EPS)
            nc.vector.memset(rows[:], 0.0).then_inc(cleared, 1)
            dve.sem_inc(summed, NB)
            dve.wait_ge(cleared, 1)

            def places(i, b):
                nc.vector.tensor_copy(gate[:, b], gate_of[:, bass.ds(i * NB + b, 1)].rearrange("p a k -> p (a k)"))
                nc.vector.tensor_copy(slot[:, b], slot_of[:, bass.ds(i * NB + b, 1)].rearrange("p a k -> p (a k)")
                                      ).then_inc(slots_ready, 1)

            def body(i, last):
                done[:] = [0, i]
                for b in range(NB):
                    dve.wait_ge(slots_ready, i * NB + (b + 1))
                    dve.wait_ge(loaded[b], i * 32 + 32)
                    step(nc.vector.tensor_tensor(acc[:, 1], shared[:, b], x1[:, b], ALU.add))
                    dve.wait_ge(gathered[b], i * (16 * TOPK) + 16 * TOPK)
                    for k in range(TOPK):
                        ins = nc.vector.scalar_tensor_tensor(acc[:, k % 2], rows[:, b, k], gate[:, b, k:k + 1],
                                                             acc[:, (k + 1) % 2], ALU.mult, ALU.add)
                        step(ins)
                    a = acc[:, (TOPK - 1) % 2]
                    nc.vector.bn_stats(stats[:], a).then_inc(summed, 1)
                    if not last:
                        places(i + 1, b)
                    wait_apart(dve, waited, summed, after(i, NB, b + 1))
                    step(nc.vector.bn_aggr(mv[:], stats[:]))
                    step(nc.vector.tensor_scalar(small[:, 1:2], mv[:, 1:2], EPS, None, ALU.add))
                    step(nc.vector.tensor_copy(small[:, 10:11], small[:, 1:2]))
                    dve.wait_ge(rooted, i * NB + (b + 1))
                    step(nc.vector.reciprocal(small[:, 2:3], small[:, 0:1]))
                    newton(nc, step, small)
                    dve.wait_ge(stored[b], after(i, 16, 0))
                    nc.vector.tensor_scalar(y[:, b], a, mv[:, 0:1], small[:, 2:3], ALU.subtract,
                                            ALU.mult).then_inc(y_ready, 1)
                    dve.wait_ge(y_ready, i * NB + (b + 1))
                    assert done[0] == STEPS * (b + 1), done

            places(0, 0)
            places(0, 1)
            with dve.Fori(0, TILES // NB - 1) as i:
                body(i, False)
            body(TILES // NB - 1, True)


def post_ln_layer(nc, xT, x_rows, w_qkv, w_o, gate_w, w13, w2, s13, s2, out):
    def dram(name, shape):
        return nc.dram_tensor(name, shape, F32, kind="Internal").ap()

    x_parts = dram("x_parts", [CHUNKS, 2, P, DT * CHUNK])
    z_dram = dram("z_dram", [TILES, P, HEADS, P])
    gathered_x = dram("gathered_x", [EXPERTS, CAPACITY, DM])
    x1_dram = dram("x1_dram", [SEQ, DM])
    x1T_parts = dram("x1T_parts", [TILES, 2, P, DT * P])
    y_dram = dram("y_dram", [EXPERTS, CAPACITY, DM])
    shared_dram = dram("shared_dram", [SEQ, DM])
    with (
        nc.sbuf_tensor("slot_of", [P, TILES, TOPK], U32) as slot_of,
        nc.sbuf_tensor("gate_of", [P, TILES, TOPK], F32) as gate_of,
    ):
        split_x(nc, xT, x_parts)
        attention(nc, x_parts, w_qkv, z_dram, gathered_x)
        project_and_route(nc, z_dram, w_o, gate_w, x_rows, x1_dram, x1T_parts, gathered_x, (slot_of, gate_of))
        experts(nc, gathered_x, x1T_parts, w13, w2, s13, s2, y_dram, shared_dram)
        combine(nc, y_dram, shared_dram, x1_dram, out, (slot_of, gate_of))


def lay_out(name, a, np):
    a = {k: np.asarray(v) for k, v in a.items()}
    if name == "x_rows":
        return a["L0_attn_x"].reshape(SEQ, DM)
    if name == "xT":
        return a["L0_attn_x"].reshape(CHUNKS, CHUNK, DT, P).transpose(0, 3, 2, 1).reshape(CHUNKS, P, DT * CHUNK)
    if name == "w_qkv":
        qk = np.stack([a["L0_attn_W_Q"], a["L0_attn_W_K"]], 1).reshape(PAIRS, 4 * DH, DM)
        v = a["L0_attn_W_V"].reshape(PAIRS, 2 * DH, DM)
        return np.concatenate([qk, v], 1).transpose(0, 2, 1).reshape(PAIRS, DT, P, 6 * DH)
    if name == "w_o":
        return a["L0_attn_W_O"].reshape(DM, HEADS, DH).transpose(2, 1, 0)
    if name == "gate_w":
        return a["L0_ffn_gate_w"].reshape(EXPERTS, DT, P).transpose(2, 1, 0)
    if name == "w13":
        w = np.concatenate([a["L0_ffn_w1"], a["L0_ffn_w3"]], 1)
        return w.reshape(EXPERTS, 2 * INTER, DT, P).transpose(0, 3, 2, 1)
    if name == "w2":
        return a["L0_ffn_w2"].transpose(0, 2, 1)
    if name == "s13":
        w = np.concatenate([a[n].reshape(SHARED_PARTS, INTER, DM) for n in ("L0_ffn_sw1", "L0_ffn_sw3")], 1)
        return w.reshape(SHARED_PARTS, 2 * INTER, DT, P).transpose(0, 3, 2, 1)
    if name == "s2":
        return a["L0_ffn_sw2"].T.reshape(SHARED_PARTS, INTER, DM)


def kernel(**inputs):
    import numpy as _np
    import concourse.bacc as _bacc
    from concourse import mybir as _mybir
    from concourse.bass_utils import run_bass_kernel_spmd as _run

    nc = _bacc.Bacc("TRN2", target_bir_lowering=False, num_devices=1)
    arrays, args = {}, []
    for name in ("xT", "x_rows", "w_qkv", "w_o", "gate_w", "w13", "w2", "s13", "s2"):
        a = _np.ascontiguousarray(lay_out(name, inputs, _np))
        arrays[f"in_{name}"] = a
        args.append(nc.dram_tensor(f"in_{name}", a.shape, _mybir.dt.from_np(a.dtype), kind="ExternalInput").ap())
    out = nc.dram_tensor("out", (SEQ, DM), F32, kind="ExternalOutput").ap()
    post_ln_layer(nc, *args, out)
    r = _run(nc, [arrays], core_ids=[0])
    return r.results[0]["out"].reshape(1, SEQ, DM)
```

```python
from contextlib import ExitStack

import numpy as np

import concourse.bass as bass
from concourse import mybir

P = 128
F32 = mybir.dt.float32
F32R = mybir.dt.float32r
BF16 = mybir.dt.bfloat16
I32 = mybir.dt.int32
U32 = mybir.dt.uint32
ALU = mybir.AluOpType
ACT = mybir.ActivationFunctionType
AX_X = mybir.AxisListType.X

SEQ, DM, HEADS, DH = 2048, 512, 16, 128
EXPERTS, INTER, TOPK, CAPACITY = 64, 352, 6, 128
SHARED_PARTS = 2
EPS = 1e-5
MASKED = -1.0e10
LOG_LEAST = -87.3365

DT = DM // P
CHUNK = 512
CHUNKS = SEQ // CHUNK
RPC = CHUNK // P
TILES = SEQ // P
PAIRS = HEADS // 2
SCALE = float(1.0 / np.sqrt(np.float32(DH)))
INTER_TILES = [(0, 128), (128, 128), (256, 96)]
SLOTS = EXPERTS * CAPACITY

PASSES = ((0, 0), (0, 1), (1, 0))


def after(i, per, k):
    return i * per + (per + k)


NB = 4


def done(i, k, per=1, n=None):
    return i * (NB * per) + (k * per + (per if n is None else n))


def exists(i, k):
    return not isinstance(i, int) or 0 <= k < TILES


def wait_apart(eng, waited, sem, value):
    eng.wait_ge(sem, value)
    eng.sem_inc(waited, 1)


def attention_plan():
    units = [(h, c) for c in range(CHUNKS) for h in range(2)]
    plan = []
    AHEAD = 2

    def tiles_of(u):
        h, c = units[u]
        n = RPC * (c + 1)
        steps = [("turn", h, c, j) for j in range(min(AHEAD, n))]
        for j in range(n):
            if j + AHEAD < n:
                steps.append(("turn", h, c, j + AHEAD))
            steps.append(("pv", h, c, j))
        return steps

    def between(u, r):
        if u == len(units):
            return [], [[], [("q", 0, 0)], [("k", 0, 0)], [("q", 0, 1), ("k", 0, 1)]][r]
        h, c = units[u]
        if h == 1:
            if c + 1 == CHUNKS:
                return [], []
            return [[], [], [], [("q", c + 1, 0)]][r], [[], [], [("k", c + 1, 0)], []][r]
        if c == 0:
            return [], [[], [("v", 0, 0)], [], [("v", 0, 1)]][r]
        return [], [[("k", c, 1)], [("q", c, 1)], [("v", c, 0)], [("v", c, 1)]][r]

    for u in range(len(units) + 1):
        behind = tiles_of(u - 1) if u else []
        first_turns, behind = behind[:AHEAD], behind[AHEAD:]
        per = -(-len(behind) // RPC)
        norm_at = RPC - 1 if u < len(units) else 1
        for r in range(RPC):
            first, last = between(u, r)
            if r == 0:
                plan += first_turns
                if u == len(units):
                    plan += [("inverse", *units[u - 1]), ("diag_lo", *units[u - 1])]
            if u and r == norm_at:
                plan.append(("norm", *units[u - 1]))
            if u < len(units):
                plan.append(("row", *units[u], r))
            plan += [("job", *job) for job in first]
            tiles = behind[r * per:(r + 1) * per]
            half = len(tiles) // 2
            plan += tiles[:half]
            if 0 < u < len(units) and r < 2:
                plan.append((["inverse", "diag_lo"][r], *units[u - 1]))
            plan += tiles[half:]
            plan += [("job", *job) for job in last]
        if u:
            plan.append(("out", *units[u - 1]))
    return plan, units


def attention(nc, xT, x_parts, w_qkv, z_dram, gathered_x):
    plan, units = attention_plan()
    BANKS = 4
    TURNS = 3

    jobs = []
    for step in plan:
        if step[0] == "job":
            jobs.append(step[1:])
        if step[0] == "row":
            _, h, c, r = step
            jobs += [("s", h, c, r, kc) for kc in range(c + 1)]
        if step[0] == "norm":
            jobs.append(step)
    early = [("q", 0, 0), ("k", 0, 0), ("q", 0, 1), ("k", 0, 1)]
    assert len(jobs) % BANKS == 0 and jobs[-len(early):] == early
    job_at = {job: n for n, job in enumerate(jobs)}
    turn_at = {s: n for n, s in enumerate(s for s in plan if s[0] == "turn")}
    pv_at = {("turn", *s[1:]): n for n, s in enumerate(s for s in plan if s[0] == "pv")}
    unit_at = {unit: n for n, unit in enumerate(units)}
    turns = list(turn_at)
    n_jobs, n_turns, n_units = len(jobs), len(turns), len(unit_at)
    scores_jobs = [j for j in jobs if j[0] == "s"]
    proj_jobs = [j for j in jobs if j[0] in "qkv"]
    exp_at = {j: n for n, j in enumerate(scores_jobs)}
    proj_at = {j: n for n, j in enumerate(proj_jobs)}
    rows = [s[1:] for s in plan if s[0] == "row"]
    row_at = {s: n for n, s in enumerate(rows)}
    n_exp, n_proj, n_rows = len(scores_jobs), len(proj_jobs), len(rows)

    w_load_steps = [("row", 0, 1, 0), ("row", 0, 2, 0), ("row", 1, CHUNKS - 1, 1), ("row", 1, CHUNKS - 1, 2)]
    w_split_steps = [("row", 1, CHUNKS - 1, r) for r in range(RPC)]

    def widths(c, r, kc):
        used = CHUNK if kc < c else (r + 1) * P
        return used, max(used, 2 * P)

    with ExitStack() as ctx:
        def sb(name, shape, dt):
            return ctx.enter_context(nc.sbuf_tensor(name, shape, dt))

        def ps(name, shape, dt=F32):
            return ctx.enter_context(nc.psum_tensor(name, shape, dt))

        def sem(name):
            return ctx.enter_context(nc.semaphore(name))

        x_sb = sb("x_sb", [P, 2, DT, CHUNK], F32R)
        w_raw = sb("w_raw", [P, 2, 6 * DH], F32)
        w_sb = [sb(f"w_{n}", [P, DT, 6 * DH], F32R) for n in ("hi", "lo")]
        q_sb = [sb(f"q_{n}", [P, 2, CHUNK], F32R) for n in ("hi", "lo")]
        k_sb = [sb(f"k_{n}", [P, 2, SEQ], F32R) for n in ("hi", "lo")]
        v_sb = [sb(f"v_{n}", [P, TILES, 2 * DH], F32R) for n in ("hi", "lo")]
        probs = sb("probs", [P, 2, RPC, SEQ], F32)
        pT_sb = [sb(f"pT_{n}", [P, TURNS, CHUNK], F32R) for n in ("hi", "lo")]
        diag = [sb(f"diag_{n}", [P, RPC, P], F32R) for n in ("hi", "lo")]
        spread_sb = sb("spread_sb", [P, CHUNK], F32)
        z_sb = sb("z_sb", [P, 2, CHUNK], F32)
        ident = sb("ident", [P, P], F32)
        ident_bf = sb("ident_bf", [P, P], BF16)
        causal_bf = sb("causal_bf", [P, P], BF16)
        ones = sb("ones", [P, P], F32R)
        zeros = sb("zeros", [P, P], F32)
        max_part = sb("max_part", [P, 2, CHUNKS], F32)
        row_max = sb("row_max", [P, 2], F32)
        neg_max = sb("neg_max", [P, 2], F32)
        sums = sb("sums", [P, 2, RPC, CHUNKS], F32)
        total = sb("total", [P, 2, RPC], F32)
        inv = sb("inv", [P, 2, RPC], F32)

        bank = ps("bank", [P, BANKS, CHUNK])
        turned = ps("turned", [P, TURNS, CHUNK])
        z_ps = ps("z_ps", [P, CHUNK])

        const_step = sem("const_step")
        pool_const = sem("pool_const")
        act_const = sem("act_const")
        dve_const = sem("dve_const")
        x_raw_in = [sem(f"x_raw_in{c}") for c in range(CHUNKS)]
        x_hi = sem("x_hi")
        x_lo = sem("x_lo")
        x_stored = [sem(f"x_stored{c}") for c in range(CHUNKS)]
        x_stored_all = [16 * 2 * (DT if c else 1) for c in range(CHUNKS)]
        x_in = sem("x_in")
        w_in = [sem(f"w_in{n}") for n in range(2)]
        w_hi_made = sem("w_hi_made")
        w_split = sem("w_split")
        job_ready = sem("job_ready")
        proj_hi = sem("proj_hi")
        proj_lo = sem("proj_lo")
        part_done = sem("part_done")
        max_done = sem("max_done")
        bias_done = sem("bias_done")
        exp_done = sem("exp_done")
        turn_ready = sem("turn_ready")
        turn_hi = sem("turn_hi")
        turn_lo = sem("turn_lo")
        pv_done = sem("pv_done")
        sum_step = sem("sum_step")
        diag_done = sem("diag_done")
        spread_done = sem("spread_done")
        z_done = sem("z_done")
        z_out = [sem(f"z_out{n}") for n in range(2)]
        zero_out = sem("zero_out")
        block = ctx.enter_context(nc.Block())

        def ring_back(n):
            if n >= TURNS:
                return TURNS
            last = max(m for m in range(n_turns) if m % TURNS == n)
            return n + n_turns - last

        def x_place(part, c, dt):
            if c == 0:
                return x_sb[:, part, dt]
            n = ((c - 1) * 2 + part) * DT + dt
            row, third = n // 3, n % 3
            first = CHUNK * (1 + third)
            return probs[:, row // RPC, row % RPC, first:first + CHUNK].bitcast(F32R)

        def x_raw_place(c, dt):
            return probs[:, 1, dt, 0:CHUNK] if c == 0 else x_place(1, c, dt).bitcast(F32)

        x_pieces = [(c, dt) for c in range(CHUNKS) for dt in range(DT)]
        per_job = DT * (CHUNKS - 1) // len(early)
        pieces_after_job = {job: x_pieces[DT + n * per_job:DT + (n + 1) * per_job] for n, job in enumerate(early)}

        def proj_dst(part, job):
            kind, c, m = job
            if kind == "q":
                return q_sb[part][:, m, :]
            if kind == "k":
                return k_sb[part][:, m, c * CHUNK:(c + 1) * CHUNK]
            t = c * RPC + 2 * m
            return v_sb[part][:, t:t + 2, :].rearrange("p t n -> p (t n)")

        @block.gpsimd
        def _(pool):
            nc.gpsimd.memset(zeros[:], 0.0).then_inc(pool_const, 1)
            nc.gpsimd.memset(ident[:], 0.0).then_inc(const_step, 1)
            nc.gpsimd.memset(causal_bf[:], 0.0).then_inc(const_step, 1)
            pool.wait_ge(const_step, 2)
            nc.gpsimd.affine_select(out=ident[:], in_=ident[:], compare_op=ALU.not_equal, fill=1.0,
                                    base=0, pattern=[[-1, P]], channel_multiplier=1).then_inc(pool_const, 1)
            nc.gpsimd.affine_select(out=causal_bf[:], in_=causal_bf[:], compare_op=ALU.is_ge, fill=MASKED,
                                    base=0, pattern=[[-1, P]], channel_multiplier=1).then_inc(pool_const, 1)

        @block.sync
        def _(sp):
            zero_src = zeros[:, :].rearrange("p (a n) -> p a n", a=1).to_broadcast([P, DM // P, P])

            def load_x(c):
                sp.wait_ge(x_stored[c], x_stored_all[c])
                sp.dma_start(x_sb[:, 0].bitcast(F32), x_parts[c, 0].rearrange("p (t n) -> p t n", t=DT)).then_inc(x_in, 16)
                sp.dma_start(x_sb[:, 1].bitcast(F32), x_parts[c, 1].rearrange("p (t n) -> p t n", t=DT)).then_inc(x_in, 16)

            for dt in range(2):
                sp.dma_start(w_raw[:, dt], w_qkv[0, dt]).then_inc(w_in[dt % 2], 16)
            sp.dma_start(probs[:, 1, :, 0:CHUNK], xT[0].rearrange("p (t n) -> p t n", t=DT)).then_inc(x_raw_in[0], 16)
            for dt in range(2, DT):
                sp.wait_ge(w_split, dt - 1)
                sp.dma_start(w_raw[:, dt % 2], w_qkv[0, dt]).then_inc(w_in[dt % 2], 16)
            for c, dt in x_pieces[DT:]:
                sp.dma_start(x_raw_place(c, dt), xT[c, :, dt * CHUNK:(dt + 1) * CHUNK]
                             ).then_inc(x_raw_in[c], 16)
            sp.wait_ge(x_lo, DT)
            for part in range(2):
                sp.dma_start(x_parts[0, part].rearrange("p (t n) -> p t n", t=DT), x_sb[:, part].bitcast(F32)
                             ).then_inc(x_stored[0], 16)
            for n, (c, dt) in enumerate(x_pieces[DT:]):
                sp.wait_ge(x_lo, DT + n + 1)
                for part in range(2):
                    sp.dma_start(x_parts[c, part, :, dt * CHUNK:(dt + 1) * CHUNK], x_place(part, c, dt).bitcast(F32)
                                 ).then_inc(x_stored[c], 16)
            sp.wait_ge(pool_const, 3)
            sp.wait_ge(x_stored[0], x_stored_all[0])
            with sp.Fori(0, PAIRS) as i:
                for step in plan:
                    if step[0:2] == ("job", "v") and step[3] == 1:
                        c = step[2]
                        sp.wait_ge(job_ready, after(i, n_jobs, job_at["v", c, 1] + 1))
                        load_x((c + 1) % CHUNKS)
                        for n in range(EXPERTS // PAIRS // CHUNKS):
                            e = i * (EXPERTS // PAIRS) + (c * (EXPERTS // PAIRS // CHUNKS) + n)
                            sp.dma_start(gathered_x[bass.ds(e, 1)].rearrange("a p (t n) -> (a p) t n", n=P),
                                         zero_src).then_inc(zero_out, 16)
                    if step in w_load_steps:
                        dt = w_load_steps.index(step)
                        sp.wait_ge(w_split, i * DT + (DT + dt - 1))
                        sp.dma_start(w_raw[:, dt % 2], w_qkv[bass.ds((i + 1) % PAIRS, 1), dt]
                                     .rearrange("a p n -> (a p) n")).then_inc(w_in[dt % 2], 16)
            sp.wait_ge(x_in, 32 * CHUNKS * PAIRS)
            sp.wait_ge(zero_out, 16 * EXPERTS)

        @block.scalar
        def _(act):
            def split_w(base, pieces=range(DT)):
                for dt in pieces:
                    act.wait_ge(w_in[dt % 2], base * (16 // 2) + (16 * (dt // 2) + 16))
                    nc.scalar.activation(w_sb[0][:, dt], w_raw[:, dt % 2], ACT.Copy).then_inc(w_hi_made, 1)

            def split_x(c, dt):
                act.wait_ge(x_raw_in[c], 16 if c == 0 else 16 * DT)
                nc.scalar.activation(x_place(0, c, dt), x_raw_place(c, dt), ACT.Copy).then_inc(x_hi, 1)

            split_w(0, range(2))
            for dt in range(DT):
                split_x(0, dt)
            split_w(0, range(2, DT))
            act.wait_ge(pool_const, 3)
            nc.scalar.activation(ident_bf[:], ident[:], ACT.Copy).then_inc(act_const, 1)
            act.sem_inc(exp_done, n_exp)
            act.sem_inc(proj_hi, n_proj - len(early))
            act.sem_inc(spread_done, n_units)
            for n in range(2):
                act.sem_inc(z_out[n], 8 * n_units)

            def project(i, job):
                act.wait_ge(job_ready, after(i, n_jobs, job_at[job] + 1))
                nc.scalar.activation(proj_dst(0, job), bank[:, job_at[job] % BANKS], ACT.Copy).then_inc(proj_hi, 1)

            for job in early:
                project(-1, job)
                for c, dt in pieces_after_job[job]:
                    split_x(c, dt)
            with act.Fori(0, PAIRS) as i:
                def exp(h, c, r, kc):
                    row, u = row_at[h, c, r], unit_at[h, c]
                    if kc == 0:
                        act.wait_ge(bias_done, i * n_rows + (row + 1))
                        act.wait_ge(diag_done, after(i, n_units, u - 1))
                    if (h, c, r, kc) == (0, 1, 0, 0):
                        for n in range(1, CHUNKS):
                            act.wait_ge(x_stored[n], x_stored_all[n])
                    used, _ = widths(c, r, kc)
                    nc.scalar.activation(probs[:, u % 2, r, kc * CHUNK:kc * CHUNK + used],
                                         bank[:, job_at["s", h, c, r, kc] % BANKS, 0:used], ACT.Exp,
                                         bias=neg_max[:, row % 2:row % 2 + 1], scale=SCALE,
                                         accum_out=sums[:, u % 2, r, kc:kc + 1]).then_inc(exp_done, 1)

                def turn(s):
                    n = turn_at[s]
                    lo_col = max(0, s[3] - RPC * s[2]) * P
                    act.wait_ge(turn_ready, i * n_turns + (n + 1))
                    act.wait_ge(pv_done, after(i, n_turns, n - ring_back(n) + 1))
                    nc.scalar.activation(pT_sb[0][:, n % TURNS, lo_col:], turned[:, n % TURNS, lo_col:],
                                         ACT.Copy).then_inc(turn_hi, 1)

                def store_z(u):
                    h, c = units[u]
                    dst = z_dram[c * RPC:(c + 1) * RPC, :, bass.ds(i * 2 + h, 1), :].rearrange("t p a n -> p (t a) n")
                    act.dma_start(dst, z_sb[:, u % 2].rearrange("p (t n) -> p t n", n=P)).then_inc(z_out[u % 2], 16)

                late, fresh = [], False
                for step in plan:
                    straight_after_row = step[0] == "job" and step[1] == "q" and step[2] > 0 and step[3] == 0
                    if step[0] not in ("turn", "pv", "inverse", "diag_lo", "norm") and not straight_after_row:
                        for bank_of_row in late:
                            exp(*bank_of_row)
                        late = []
                    if step[0] == "turn" and step[3] == 0:
                        for bank_of_row in late:
                            exp(*bank_of_row)
                        late = []
                    if step[0] == "diag_lo" and unit_at[step[1:]]:
                        act.wait_ge(z_done, after(i, n_units, unit_at[step[1:]]))
                        store_z(unit_at[step[1:]] - 1)
                    if step[0] in ("job", "norm"):
                        mine = job_at[step[1:] if step[0] == "job" else step]
                        while late and job_at["s", *late[0]] <= mine - BANKS:
                            exp(*late.pop(0))
                    if step[0] == "job":
                        project(i, step[1:])
                    if step[0] == "row":
                        late = [(*step[1:], kc) for kc in range(step[2] + 1)]
                        fresh = True
                    if step[0] == "turn":
                        turn(step)
                        if late and not fresh:
                            exp(*late.pop(0))
                        fresh = False
                    if step[0] == "norm":
                        act.wait_ge(job_ready, after(i, n_jobs, job_at[step] + 1))
                        act.wait_ge(z_done, after(i, n_units, unit_at[step[1:]]))
                        nc.scalar.activation(spread_sb[:], bank[:, job_at[step] % BANKS],
                                             ACT.Copy).then_inc(spread_done, 1)
                    if step in w_split_steps:
                        act.wait_ge(job_ready, after(i, n_jobs, job_at["v", CHUNKS - 1, 1] + 1))
                        split_w(i * DT + DT, [w_split_steps.index(step)])
                act.wait_ge(z_done, after(i, n_units, n_units))
                store_z(n_units - 1)
            for n in range(2):
                act.wait_ge(z_out[n], 8 * n_units * (PAIRS + 1))

        @block.vector
        def _(dve):
            nc.vector.memset(spread_sb[:], 1.0).then_inc(dve_const, 1)
            dve.wait_ge(dve_const, 1)
            nc.vector.tensor_copy(ones[:], spread_sb[:, 0:P]).then_inc(dve_const, 1)
            dve.sem_inc(proj_lo, n_proj - len(early))
            dve.sem_inc(turn_lo, n_turns)
            dve.sem_inc(diag_done, n_units)
            dve.sem_inc(z_done, n_units)

            def split_w(base, pieces=range(DT)):
                for dt in pieces:
                    dve.wait_ge(w_hi_made, base + (dt + 1))
                    nc.vector.tensor_tensor(w_sb[1][:, dt], w_raw[:, dt % 2], w_sb[0][:, dt].bitcast(F32),
                                            ALU.subtract).then_inc(w_split, 1)

            def split_x(c, dt):
                dve.wait_ge(x_hi, x_pieces.index((c, dt)) + 1)
                nc.vector.tensor_tensor(x_place(1, c, dt), x_raw_place(c, dt),
                                        x_place(0, c, dt).bitcast(F32), ALU.subtract).then_inc(x_lo, 1)

            split_w(0, range(2))
            for dt in range(DT):
                split_x(0, dt)
            split_w(0, range(2, DT))
            dve.wait_ge(pool_const, 3)

            def project(i, job):
                dve.wait_ge(proj_hi, after(i, n_proj, proj_at[job] + 1))
                nc.vector.tensor_tensor(proj_dst(1, job), bank[:, job_at[job] % BANKS],
                                        proj_dst(0, job).bitcast(F32), ALU.subtract).then_inc(proj_lo, 1)

            for job in early:
                project(-1, job)
                for c, dt in pieces_after_job[job]:
                    split_x(c, dt)
            with dve.Fori(0, PAIRS) as i:
                def maxima(h, c, r):
                    row = row_at[h, c, r]
                    first = exp_at["s", h, c, r, 0]
                    if row >= 2:
                        h2, c2, r2 = rows[row - 2]
                        dve.wait_ge(exp_done, after(i, n_exp, exp_at["s", h2, c2, r2, c2] + 1))
                    else:
                        dve.wait_ge(exp_done, after(i, n_exp, 0))
                    for kc in range(c + 1):
                        job = ("s", h, c, r, kc)
                        used, _ = widths(c, r, kc)
                        dve.wait_ge(job_ready, after(i, n_jobs, job_at[job] + 1))
                        dst = max_part[:, row % 2, kc:kc + 1]
                        nc.vector.reduce_max(dst, bank[:, job_at[job] % BANKS, 0:used],
                                             axis=AX_X).then_inc(part_done, 1)
                    dve.wait_ge(part_done, i * n_exp + (first + c + 1))
                    nc.vector.reduce_max(row_max[:, row % 2:row % 2 + 1], max_part[:, row % 2, 0:c + 1],
                                         axis=AX_X).then_inc(max_done, 1)
                    dve.wait_ge(max_done, i * n_rows + (row + 1))
                    nc.vector.tensor_scalar(neg_max[:, row % 2:row % 2 + 1], row_max[:, row % 2:row % 2 + 1],
                                            -SCALE, None, ALU.mult).then_inc(bias_done, 1)

                def inverse(h, c):
                    u = unit_at[h, c]
                    dve.wait_ge(exp_done, after(i, n_exp, exp_at["s", h, c, RPC - 1, c] + 1))
                    nc.vector.reduce_sum(total[:, u % 2], sums[:, u % 2, :, 0:c + 1], axis=AX_X).then_inc(sum_step, 1)
                    dve.wait_ge(sum_step, i * (3 * n_units) + (3 * u + 1))
                    nc.vector.reciprocal(inv[:, u % 2], total[:, u % 2]).then_inc(sum_step, 1)
                    dve.wait_ge(sum_step, i * (3 * n_units) + (3 * u + 2))
                    dve.wait_ge(spread_done, after(i, n_units, u))
                    for r in range(RPC):
                        mark = nc.vector.tensor_scalar(diag[0][:, r], ident[:], inv[:, u % 2, r:r + 1], None,
                                                       ALU.mult)
                    mark.then_inc(sum_step, 1)

                def diag_lo(h, c):
                    u = unit_at[h, c]
                    dve.wait_ge(sum_step, i * (3 * n_units) + (3 * u + 3))
                    for r in range(RPC):
                        mark = nc.vector.scalar_tensor_tensor(diag[1][:, r], ident[:], inv[:, u % 2, r:r + 1],
                                                              diag[0][:, r].bitcast(F32), ALU.mult, ALU.subtract)
                    mark.then_inc(diag_done, 1)

                for step in plan:
                    if step[0] == "job":
                        project(i, step[1:])
                    if step[0] == "row":
                        maxima(*step[1:])
                    if step[0] == "turn":
                        n = turn_at[step]
                        lo_col = max(0, step[3] - RPC * step[2]) * P
                        dve.wait_ge(turn_hi, i * n_turns + (n + 1))
                        nc.vector.tensor_tensor(pT_sb[1][:, n % TURNS, lo_col:], turned[:, n % TURNS, lo_col:],
                                                pT_sb[0][:, n % TURNS, lo_col:].bitcast(F32),
                                                ALU.subtract).then_inc(turn_lo, 1)
                    if step[0] == "inverse":
                        inverse(*step[1:])
                    if step[0] == "diag_lo":
                        diag_lo(*step[1:])
                    if step[0] == "out":
                        u = unit_at[step[1:]]
                        last = pv_at["turn", *step[1:], RPC * (step[2] + 1) - 1]
                        dve.wait_ge(pv_done, after(i, n_turns, last + 1))
                        dve.wait_ge(spread_done, after(i, n_units, u + 1))
                        dve.wait_ge(z_out[u % 2], i * (8 * n_units) + (8 * n_units + 16 * (u // 2)))
                        nc.vector.tensor_tensor(z_sb[:, u % 2], z_ps[:], spread_sb[:], ALU.mult).then_inc(z_done, 1)
                    if step in w_split_steps:
                        split_w(i * DT + DT, [w_split_steps.index(step)])

        @block.tensor
        def _(pe):
            pe.sem_inc(job_ready, n_jobs - len(early))
            pe.sem_inc(pv_done, n_turns)
            pe.wait_ge(pool_const, 3)
            pe.wait_ge(act_const, 1)
            pe.wait_ge(dve_const, 2)

            def take(i, n):
                m = n - BANKS
                old = jobs[m]
                back = 0 if m >= 0 else 1
                if old[0] == "s":
                    pe.wait_ge(exp_done, after(i, n_exp, exp_at[old] + 1 - back * n_exp))
                elif old[0] == "norm":
                    pe.wait_ge(spread_done, after(i, n_units, unit_at[old[1:]] + 1 - back * n_units))
                else:
                    pe.wait_ge(proj_lo, after(i, n_proj, proj_at[old] + 1 - back * n_proj))
                return bank[:, n % BANKS]

            def project(i, job):
                kind, c, m = job
                if job in early:
                    if isinstance(i, int):
                        pe.wait_ge(x_lo, DT)
                    else:
                        pe.wait_ge(x_in, i * (32 * CHUNKS) + 32 * CHUNKS)
                elif c:
                    pe.wait_ge(x_in, i * (32 * CHUNKS) + 32 * c)
                dst = take(i, job_at[job])
                if kind == "v":
                    for t in range(2):
                        rows_ = slice((2 * m + t) * P, (2 * m + t + 1) * P)
                        for dt in range(DT):
                            for a, b in PASSES:
                                mark = nc.tensor.matmul(dst[:, t * 2 * DH:(t + 1) * 2 * DH],
                                                        x_sb[:, a, dt, rows_], w_sb[b][:, dt, 4 * DH:],
                                                        start=(dt == 0 and (a, b) == PASSES[0]),
                                                        stop=(dt == DT - 1 and (a, b) == PASSES[-1]))
                else:
                    first = (2 * m + "qk".index(kind)) * DH
                    for dt in range(DT):
                        if job == early[0]:
                            pe.wait_ge(w_split, i * DT + (DT + dt + 1))
                        for a, b in PASSES:
                            mark = nc.tensor.matmul(dst, w_sb[a][:, dt, first:first + DH], x_sb[:, b, dt, :],
                                                    start=(dt == 0 and (a, b) == PASSES[0]),
                                                    stop=(dt == DT - 1 and (a, b) == PASSES[-1]))
                mark.then_inc(job_ready, 1)

            for job in early:
                project(-1, job)
            with pe.Fori(0, PAIRS) as i:
                def scores(h, c, r):
                    if r == 0:
                        later = max(proj_at["q", c, h], proj_at["k", c, h])
                        pe.wait_ge(proj_lo, after(i, n_proj, later + 1 - (0 if c else n_proj)))
                    for kc in range(c + 1):
                        n = job_at["s", h, c, r, kc]
                        dst = take(i, n)
                        used, width = widths(c, r, kc)
                        for a, b in PASSES:
                            mark = nc.tensor.matmul(dst[:, 0:width], q_sb[a][:, h, r * P:(r + 1) * P],
                                                    k_sb[b][:, h, kc * CHUNK:kc * CHUNK + width],
                                                    start=(a, b) == PASSES[0], stop=(a, b) == PASSES[-1])
                            if kc == c and (a, b) == PASSES[0]:
                                nc.tensor.matmul(dst[:, r * P:(r + 1) * P], ident_bf[:], causal_bf[:],
                                                 start=False, stop=False, skip_group_check=True)
                        mark.then_inc(job_ready, 1)

                def turn(s):
                    _, h, c, j = s
                    n, u = turn_at[s], unit_at[h, c]
                    first = max(0, j - RPC * c)
                    if j == 0:
                        pe.wait_ge(exp_done, after(i, n_exp, exp_at["s", h, c, RPC - 1, c] + 1))
                    pe.wait_ge(turn_lo, after(i, n_turns, n - ring_back(n) + 1))
                    for r in range(first, RPC):
                        mark = nc.tensor.transpose(turned[:, n % TURNS, r * P:(r + 1) * P],
                                                   probs[:, u % 2, r, j * P:(j + 1) * P], ident[:])
                    mark.then_inc(turn_ready, 1)

                def value(s):
                    _, h, c, j = s
                    n = turn_at["turn", h, c, j]
                    first = max(0, j - RPC * c)
                    if j == 0:
                        pe.wait_ge(z_done, after(i, n_units, unit_at[h, c]))
                    if j == RPC * c:
                        pe.wait_ge(proj_lo, after(i, n_proj, proj_at["v", c, 1] + 1))
                    pe.wait_ge(turn_lo, after(i, n_turns, n + 1))
                    for a, b in PASSES:
                        mark = nc.tensor.matmul(z_ps[:, first * P:], v_sb[a][:, j, h * DH:(h + 1) * DH],
                                                pT_sb[b][:, n % TURNS, first * P:],
                                                start=(j == 0 and (a, b) == PASSES[0]),
                                                stop=(j == RPC * (c + 1) - 1 and (a, b) == PASSES[-1]),
                                                skip_group_check=True)
                    mark.then_inc(pv_done, 1)

                for step in plan:
                    if step[0] == "job":
                        project(i, step[1:])
                    if step[0] == "row":
                        scores(*step[1:])
                    if step[0] == "turn":
                        turn(step)
                    if step[0] == "pv":
                        value(step)
                    if step[0] == "norm":
                        dst = take(i, job_at[step])
                        pe.wait_ge(diag_done, after(i, n_units, unit_at[step[1:]] + 1))
                        for part in range(2):
                            mark = nc.tensor.matmul(dst, ones[:], diag[part][:].rearrange("p r n -> p (r n)"),
                                                    start=part == 0, stop=part == 1)
                        mark.then_inc(job_ready, 1)


def project_and_route(nc, z_dram, w_o, gate_w, x_rows, x1_dram, x1T_parts, gathered_x, routes):
    slot_of, gate_of = routes
    BIG = 1 << 20

    with ExitStack() as ctx:
        def sb(name, shape, dt=F32):
            return ctx.enter_context(nc.sbuf_tensor(name, shape, dt))

        def ps(name, shape, dt=F32):
            return ctx.enter_context(nc.psum_tensor(name, shape, dt))

        def sem(name):
            return ctx.enter_context(nc.semaphore(name))

        LOOPS = TILES // NB - 2
        GROUP = 2
        LATE = (12, 14)
        wo_raw = sb("wo_raw", [P, HEADS, DM])
        wo = [sb(f"wo_{n}", [P, HEADS, DM], F32R) for n in ("hi", "lo")]
        gw = sb("gw", [P, DT, EXPERTS])
        z_raw = sb("z_raw", [P, 2, HEADS, P])
        z = [sb(f"z_{n}", [P, 2, HEADS, P], F32R) for n in ("hi", "lo")]
        xr = sb("xr", [P, 2, DM])
        y = sb("y", [P, DM])
        x1 = sb("x1", [P, NB, DM])
        x1T = sb("x1T", [P, 2, DT, P])
        xT_part = [sb(f"x1T_{n}", [P, 2, DT, P], F32R) for n in ("hi", "lo")]
        stats = sb("stats", [P, 6])
        mv = sb("mv", [P, 2])
        small = sb("small", [P, 16])
        eps = sb("eps", [P, 1])
        lg_c = sb("lg_c", [P, EXPERTS])
        ex = sb("ex", [P, EXPERTS])
        top = sb("top", [P, 8])
        top_e = sb("top_e", [P, 8])
        gate = sb("gate", [P, TOPK])
        idx = sb("idx", [P, 8], U32)
        idx_f = sb("idx_f", [P, 8])
        pick = sb("pick", [P, TOPK, EXPERTS])
        pick_pos = sb("pick_pos", [P, TOPK, EXPERTS])
        chosen = sb("chosen", [P, EXPERTS])
        chosen_bf = sb("chosen_bf", [P, EXPERTS], BF16)
        count = sb("count", [P, EXPERTS])
        pos_all = sb("pos_all", [P, EXPERTS])
        slot = sb("slot", [P, 2, TOPK], U32)
        pos = sb("pos", [P, TOPK])
        full = sb("full", [P, TOPK])
        room = sb("room", [P, TOPK])
        place = sb("place", [P, TOPK])
        iota_i = sb("iota_i", [P, EXPERTS], I32)
        iota_f = sb("iota_f", [P, EXPERTS])
        ident = sb("ident3", [P, P])
        before_bf = sb("before_bf", [P, P], BF16)
        ones_bf = sb("ones_bf", [P, P], BF16)

        o_ps = ps("o_ps", [P, 2, DM])
        t_ps = ps("t_ps", [P, DT * P])
        l_ps = ps("l_ps", [P, EXPERTS])
        c_ps = ps("c_ps", [P, 2, EXPERTS])

        waited = sem("waited3")
        pool_step = sem("pool_step")
        pool_const = sem("pool_const3")
        dve_const = sem("dve_const3")
        wo_in = [sem(f"wo_in{n}") for n in range(HEADS // GROUP)]
        wo_hi = sem("wo_hi")
        wo_split = sem("wo_split")
        gw_in = sem("gw_in")
        z_in = [sem(f"z_in{n}") for n in range(2)]
        x_in = [sem(f"xr_in{n}") for n in range(2)]
        z_hi = sem("z_hi")
        z_lo = sem("z_lo")
        out_ready = sem("out_ready")
        out_read = sem("out_read")
        rooted = sem("rooted")
        x1_ready = sem("x1_ready")
        x1_stored = [sem(f"x1_stored{n}") for n in range(NB)]
        t_ready = sem("t_ready")
        t_read = sem("t_read")
        t_hi = sem("t_hi")
        t_split = sem("t_split")
        t_stored = [sem(f"t_stored{n}") for n in range(2)]
        l_ready = sem("l_ready")
        l_read = sem("l_read")
        exp_ready = sem("exp_ready")
        chosen_ready = sem("chosen_ready")
        c_ready = sem("c_ready")
        c_read = sem("c_read")
        placed = sem("placed")
        moved = sem("moved")
        rows_left = sem("rows_left")
        ln_chain = sem("ln_chain3")
        route_chain = sem("route_chain")
        block = ctx.enter_context(nc.Block())
        LN_STEPS = 9
        CHOOSE_STEPS, GATE_STEPS = 6, 4
        ROUTE_STEPS = CHOOSE_STEPS + GATE_STEPS + 5

        @block.gpsimd
        def _(pool):
            nc.gpsimd.memset(ident[:], 0.0).then_inc(pool_step, 1)
            nc.gpsimd.memset(before_bf[:], 1.0).then_inc(pool_step, 1)
            nc.gpsimd.iota(iota_i[:], pattern=[[1, EXPERTS]], base=0, channel_multiplier=0).then_inc(pool_const, 1)
            pool.wait_ge(pool_step, 2)
            nc.gpsimd.affine_select(out=ident[:], in_=ident[:], compare_op=ALU.not_equal, fill=1.0,
                                    base=0, pattern=[[-1, P]], channel_multiplier=1).then_inc(pool_const, 1)
            nc.gpsimd.affine_select(out=before_bf[:], in_=before_bf[:], compare_op=ALU.is_gt, fill=0.0,
                                    base=0, pattern=[[1, P]], channel_multiplier=-1).then_inc(pool_const, 1)
            flat = gathered_x.rearrange("e c d -> (e c) d")
            last_slot = nc.gpsimd.to_reg(SLOTS - 1)
            with pool.Fori(0, TILES // NB) as i:
                for k in range(NB):
                    wait_apart(pool, waited, placed, done(i, k))
                    for n in range(TOPK):
                        nc.gpsimd.indirect_dma_start(
                            flat, bass.IndirectOffsetOnAxis(ap=slot[:, k % 2, n:n + 1], axis=0), x1[:, k], None,
                            bounds_check=last_slot, oob_is_err=False).then_inc(moved, 16)
                    pool.wait_ge(moved, done(i, k, 16 * TOPK))
                    pool.sem_inc(rows_left, 1)

        @block.sync
        def _(sp):
            def load_z(i, k):
                sp.dma_start(z_raw[:, k % 2], z_dram[bass.ds(i * NB + k, 1)].rearrange("a p h n -> (a p) h n")
                             ).then_inc(z_in[k % 2], 16)

            def load_x(i, k):
                sp.dma_start(xr[:, k % 2], x_rows[bass.ds((i * NB + k) * P, P)]).then_inc(x_in[k % 2], 16)

            load_z(0, 0)
            sp.dma_start(gw[:], gate_w).then_inc(gw_in, 16)
            for g in range(HEADS // GROUP):
                sp.dma_start(wo_raw[:, g * GROUP:(g + 1) * GROUP], w_o[:, g * GROUP:(g + 1) * GROUP]
                             ).then_inc(wo_in[g], 16)
            load_z(0, 1)
            load_x(0, 0)
            load_x(0, 1)

            def step(i, k):
                if exists(i, k - 1):
                    t = i * NB + (k - 1)
                    if exists(i, k + 1):
                        sp.wait_ge(out_read, done(i, k - 1))
                        load_x(i, k + 1)
                    sp.wait_ge(x1_ready, done(i, k - 1))
                    sp.dma_start(x1_dram[bass.ds(t * P, P)], x1[:, (k - 1) % NB]).then_inc(x1_stored[(k - 1) % NB], 16)
                if exists(i, k + 2):
                    sp.wait_ge(z_lo, done(i, k))
                    load_z(i, k + 2)
                if exists(i, k - 1):
                    sp.wait_ge(t_split, done(i, k - 1))
                    for part in range(2):
                        sp.dma_start(x1T_parts[bass.ds(t, 1), part].rearrange("a p n -> (a p) n"),
                                     xT_part[part][:, (k - 1) % 2].rearrange("p t n -> p (t n)").bitcast(F32)
                                     ).then_inc(t_stored[(k - 1) % 2], 16)

            for k in range(NB):
                step(0, k)
            with sp.Fori(0, LOOPS) as i:
                for k in range(NB, 2 * NB):
                    step(i, k)
            for k in range(TILES - NB, TILES + 2):
                step(0, k)
            for n in range(NB):
                sp.wait_ge(x1_stored[n], 16 * TILES // NB)
            for n in range(2):
                sp.wait_ge(t_stored[n], 32 * TILES // 2)

        @block.scalar
        def _(act):
            def split_wo(g):
                act.wait_ge(wo_in[g], 16)
                nc.scalar.activation(wo[0][:, g * GROUP:(g + 1) * GROUP], wo_raw[:, g * GROUP:(g + 1) * GROUP],
                                     ACT.Copy).then_inc(wo_hi, 1)

            def split_z(i, k):
                act.wait_ge(z_in[k % 2], i * (16 * NB // 2) + 16 * (k // 2 + 1))
                if exists(i, k - 2):
                    act.wait_ge(out_ready, done(i, k - 2))
                nc.scalar.activation(z[0][:, k % 2], z_raw[:, k % 2], ACT.Copy).then_inc(z_hi, 1)

            def root(i, k):
                act.wait_ge(ln_chain, done(i, k, LN_STEPS, 3))
                nc.scalar.activation(small[:, 0:1], mv[:, 1:2], ACT.Sqrt, bias=eps[:]).then_inc(rooted, 1)

            def exponentials(i, k):
                act.wait_ge(l_read, done(i, k))
                nc.scalar.activation(ex[:], lg_c[:], ACT.Exp, accum_out=small[:, 4:5]).then_inc(exp_ready, 1)

            def turned(i, k):
                act.wait_ge(t_ready, done(i, k))
                if exists(i, k - 2):
                    act.wait_ge(l_ready, done(i, k - 2))
                nc.scalar.activation(x1T[:, k % 2].rearrange("p t n -> p (t n)"), t_ps[:], ACT.Copy
                                     ).then_inc(t_read, 1)
                if exists(i, k - 2):
                    act.wait_ge(t_stored[k % 2], i * (32 * NB // 2) + 32 * (k // 2))
                nc.scalar.activation(xT_part[0][:, k % 2].rearrange("p t n -> p (t n)"), t_ps[:], ACT.Copy
                                     ).then_inc(t_hi, 1)

            def step(i, k):
                if exists(i, k - 1):
                    root(i, k - 1)
                if exists(i, k - 2):
                    exponentials(i, k - 2)
                if exists(i, k + 1):
                    split_z(i, k + 1)
                if exists(i, k - 1):
                    turned(i, k - 1)

            split_z(0, 0)
            for g in range(HEADS // GROUP):
                split_wo(g)
            act.wait_ge(dve_const, 3)
            for k in range(NB):
                step(0, k)
            with act.Fori(0, LOOPS) as i:
                for k in range(NB, 2 * NB):
                    step(i, k)
            for k in range(TILES - NB, TILES + 2):
                step(0, k)

        @block.tensor
        def _(pe):
            def project(i, k, heads):
                if heads[0] == 0:
                    pe.wait_ge(z_lo, done(i, k))
                    if exists(i, k - 2):
                        pe.wait_ge(out_read, done(i, k - 2))
                for h in heads:
                    if isinstance(i, int) and k == 0 and h % GROUP == 0:
                        pe.wait_ge(wo_split, h // GROUP + 1)
                    for m, n in PASSES:
                        mark = nc.tensor.matmul(o_ps[:, k % 2], z[m][:, k % 2, h], wo[n][:, h],
                                                start=h == 0 and (m, n) == PASSES[0],
                                                stop=h == HEADS - 1 and (m, n) == PASSES[-1])
                if heads[-1] == HEADS - 1:
                    mark.then_inc(out_ready, 1)

            def turn(i, k):
                pe.wait_ge(x1_ready, done(i, k))
                if exists(i, k - 1):
                    pe.wait_ge(t_split, done(i, k - 1))
                for d in range(DT):
                    mark = nc.tensor.transpose(t_ps[:, d * P:(d + 1) * P], x1[:, k % NB, d * P:(d + 1) * P], ident[:])
                mark.then_inc(t_ready, 1)

            def counts(i, k):
                pe.wait_ge(chosen_ready, done(i, k))
                if exists(i, k - 1):
                    pe.wait_ge(c_read, done(i, k - 1))
                nc.tensor.matmul(c_ps[:, 0], before_bf[:], chosen_bf[:], start=True, stop=True)
                nc.tensor.matmul(c_ps[:, 1], ones_bf[:], chosen_bf[:], start=True, stop=True).then_inc(c_ready, 1)

            def logits(i, k):
                pe.wait_ge(t_read, done(i, k))
                if exists(i, k - 1):
                    pe.wait_ge(l_read, done(i, k - 1))
                for d in range(DT):
                    mark = nc.tensor.matmul(l_ps[:], x1T[:, k % 2, d], gw[:, d], start=d == 0, stop=d == DT - 1)
                mark.then_inc(l_ready, 1)

            def step(i, k):
                if exists(i, k):
                    project(i, k, range(0, LATE[0]))
                if exists(i, k - 1):
                    turn(i, k - 1)
                if exists(i, k):
                    project(i, k, range(LATE[0], LATE[1]))
                if exists(i, k - 2):
                    counts(i, k - 2)
                if exists(i, k):
                    project(i, k, range(LATE[1], HEADS))
                if exists(i, k - 1):
                    logits(i, k - 1)

            pe.wait_ge(pool_const, 3)
            pe.wait_ge(dve_const, 3)
            pe.wait_ge(gw_in, 16)
            for k in range(NB):
                step(0, k)
            with pe.Fori(0, LOOPS) as i:
                for k in range(NB, 2 * NB):
                    step(i, k)
            for k in range(TILES - NB, TILES + 2):
                step(0, k)

        @block.vector
        def _(dve):
            made = {}

            def chained(sem, i, k, per, start):
                made[sem] = start

                def link(ins, apart=False):
                    made[sem] += 1
                    ins.then_inc(sem, 1)
                    if apart:
                        wait_apart(dve, waited, sem, done(i, k, per, made[sem]))
                    else:
                        dve.wait_ge(sem, done(i, k, per, made[sem]))
                return link

            def split_wo(g):
                dve.wait_ge(wo_hi, g + 1)
                part = slice(g * GROUP, (g + 1) * GROUP)
                nc.vector.tensor_tensor(wo[1][:, part], wo_raw[:, part], wo[0][:, part].bitcast(F32),
                                        ALU.subtract).then_inc(wo_split, 1)

            def split_z(i, k):
                dve.wait_ge(z_hi, done(i, k))
                nc.vector.tensor_tensor(z[1][:, k % 2], z_raw[:, k % 2], z[0][:, k % 2].bitcast(F32),
                                        ALU.subtract).then_inc(z_lo, 1)

            def normalise(i, k):
                link = chained(ln_chain, i, k, LN_STEPS, 0)
                dve.wait_ge(out_ready, done(i, k))
                dve.wait_ge(x_in[k % 2], i * (16 * NB // 2) + 16 * (k // 2 + 1))
                nc.vector.tensor_tensor(y[:], o_ps[:, k % 2], xr[:, k % 2], ALU.add).then_inc(out_read, 1)
                dve.wait_ge(out_read, done(i, k))
                link(nc.vector.bn_stats(stats[:], y[:]), apart=True)
                link(nc.vector.bn_aggr(mv[:], stats[:]))
                link(nc.vector.tensor_scalar(small[:, 1:2], mv[:, 1:2], EPS, None, ALU.add))
                dve.wait_ge(rooted, done(i, k))
                link(nc.vector.reciprocal(small[:, 2:3], small[:, 0:1]))
                newton(nc, link, small)
                assert made[ln_chain] == LN_STEPS, made[ln_chain]
                if exists(i, k - NB):
                    dve.wait_ge(x1_stored[k % NB], i * 16 + 16 * (k // NB))
                    dve.wait_ge(rows_left, done(i, k - NB))
                nc.vector.tensor_scalar(x1[:, k % NB], y[:], mv[:, 0:1], small[:, 2:3], ALU.subtract,
                                        ALU.mult).then_inc(x1_ready, 1)

            def split_x1T(i, k):
                dve.wait_ge(t_hi, done(i, k))
                if exists(i, k - 2):
                    dve.wait_ge(t_stored[k % 2], i * (32 * NB // 2) + 32 * (k // 2))
                nc.vector.tensor_tensor(xT_part[1][:, k % 2].rearrange("p t n -> p (t n)"), t_ps[:],
                                        xT_part[0][:, k % 2].rearrange("p t n -> p (t n)").bitcast(F32),
                                        ALU.subtract).then_inc(t_split, 1)

            def choose(i, k):
                link = chained(route_chain, i, k, ROUTE_STEPS, 0)
                dve.wait_ge(l_ready, done(i, k))
                link(nc.vector.reduce_max(small[:, 3:4], l_ps[:], axis=AX_X))
                nc.vector.tensor_scalar(lg_c[:], l_ps[:], small[:, 3:4], LOG_LEAST, ALU.subtract,
                                        ALU.max).then_inc(l_read, 1)
                wait_apart(dve, waited, l_read, done(i, k))
                link(nc.vector.max(top[:], lg_c[:]), apart=True)
                link(nc.vector.max_index(idx[:], top[:], lg_c[:]))
                link(nc.vector.tensor_copy(idx_f[:], idx[:]))
                link(nc.vector.tensor_tensor(
                    pick[:], iota_f[:].rearrange("p (k e) -> p k e", k=1).to_broadcast([P, TOPK, EXPERTS]),
                    idx_f[:, 0:TOPK].rearrange("p (k e) -> p k e", e=1).to_broadcast([P, TOPK, EXPERTS]),
                    ALU.is_equal))
                link(nc.vector.reduce_sum(chosen[:], pick[:].rearrange("p k e -> p e k"), axis=AX_X))
                nc.vector.tensor_copy(chosen_bf[:], chosen[:]).then_inc(chosen_ready, 1)
                assert made[route_chain] == CHOOSE_STEPS, made[route_chain]

            def gates(i, k):
                link = chained(route_chain, i, k, ROUTE_STEPS, CHOOSE_STEPS)
                dve.wait_ge(exp_ready, done(i, k))
                link(nc.vector.tensor_tensor(pick_pos[:], pick[:], ex[:].rearrange("p (k e) -> p k e", k=1)
                                             .to_broadcast([P, TOPK, EXPERTS]), ALU.mult))
                link(nc.vector.reduce_sum(top_e[:, 0:TOPK], pick_pos[:], axis=AX_X))
                link(nc.vector.reciprocal(small[:, 5:6], small[:, 4:5]))
                link(nc.vector.tensor_scalar(gate[:], top_e[:, 0:TOPK], small[:, 5:6], None, ALU.mult))
                assert made[route_chain] == CHOOSE_STEPS + GATE_STEPS, made[route_chain]

            def places(i, k):
                link = chained(route_chain, i, k, ROUTE_STEPS, CHOOSE_STEPS + GATE_STEPS)
                t = i * NB + k
                dve.wait_ge(c_ready, done(i, k))
                link(nc.vector.tensor_tensor(pos_all[:], c_ps[:, 0], count[:], ALU.add))
                nc.vector.tensor_tensor(count[:], c_ps[:, 1], count[:], ALU.add).then_inc(c_read, 1)
                link(nc.vector.tensor_tensor(pick_pos[:], pick[:], pos_all[:].rearrange("p (k e) -> p k e", k=1)
                                             .to_broadcast([P, TOPK, EXPERTS]), ALU.mult))
                link(nc.vector.reduce_sum(pos[:], pick_pos[:], axis=AX_X))
                nc.vector.tensor_scalar(full[:], pos[:], float(CAPACITY), float(BIG), ALU.is_ge, ALU.mult)
                nc.vector.tensor_scalar(room[:], pos[:], float(CAPACITY), None, ALU.is_lt)
                link(nc.vector.scalar_tensor_tensor(place[:], idx_f[:, 0:TOPK], float(CAPACITY), pos[:],
                                                    ALU.mult, ALU.add))
                nc.vector.tensor_tensor(gate_of[:, bass.ds(t, 1)].rearrange("p a k -> p (a k)"), gate[:], room[:],
                                        ALU.mult)
                nc.vector.tensor_tensor(slot_of[:, bass.ds(t, 1)].rearrange("p a k -> p (a k)"), place[:], full[:],
                                        ALU.add)
                if exists(i, k - 2):
                    dve.wait_ge(rows_left, done(i, k - 2))
                link(nc.vector.tensor_tensor(slot[:, k % 2], place[:], full[:], ALU.add))
                dve.sem_inc(placed, 1)
                dve.wait_ge(c_read, done(i, k))
                assert made[route_chain] == ROUTE_STEPS, made[route_chain]

            def step(i, k):
                if exists(i, k - 1):
                    normalise(i, k - 1)
                if exists(i, k - 2):
                    choose(i, k - 2)
                if exists(i, k + 1):
                    split_z(i, k + 1)
                if exists(i, k - 2):
                    gates(i, k - 2)
                if exists(i, k - 1):
                    split_x1T(i, k - 1)
                if exists(i, k - 2):
                    places(i, k - 2)

            nc.vector.memset(eps[:], EPS).then_inc(dve_const, 1)
            nc.vector.memset(ones_bf[:], 1.0).then_inc(dve_const, 1)
            nc.vector.memset(count[:], 0.0).then_inc(dve_const, 1)
            dve.wait_ge(dve_const, 3)
            split_z(0, 0)
            for g in range(HEADS // GROUP):
                split_wo(g)
            dve.wait_ge(pool_const, 3)
            nc.vector.tensor_copy(iota_f[:], iota_i[:]).then_inc(dve_const, 1)
            dve.wait_ge(dve_const, 4)
            for k in range(NB):
                step(0, k)
            with dve.Fori(0, LOOPS) as i:
                for k in range(NB, 2 * NB):
                    step(i, k)
            for k in range(TILES - NB, TILES + 2):
                step(0, k)


def newton(nc, step, s):
    step(nc.vector.tensor_tensor(s[:, 6:7], s[:, 2:3], s[:, 2:3], ALU.mult))
    step(nc.vector.scalar_tensor_tensor(s[:, 7:8], s[:, 6:7], -0.5, s[:, 1:2], ALU.mult, ALU.mult))
    step(nc.vector.tensor_scalar(s[:, 8:9], s[:, 7:8], 1.5, None, ALU.add))
    step(nc.vector.tensor_tensor(s[:, 9:10], s[:, 8:9], s[:, 2:3], ALU.mult))
    step(nc.vector.tensor_copy(s[:, 2:3], s[:, 9:10]))


def experts(nc, gathered_x, x1_dram, x1T_parts, w13, w2, s13, s2, y_dram, base_dram):
    with ExitStack() as ctx:
        def sb(name, shape, dt=F32):
            return ctx.enter_context(nc.sbuf_tensor(name, shape, dt))

        def ps(name, shape, dt=F32):
            return ctx.enter_context(nc.psum_tensor(name, shape, dt))

        def sem(name):
            return ctx.enter_context(nc.semaphore(name))

        BODIES = 8
        NE = EXPERTS // BODIES
        NS = TILES * SHARED_PARTS // BODIES
        UNITS = [("s", u // 3) if u % 3 == 2 else ("e", 2 * (u // 3) + u % 3) for u in range(NE + NS)]
        NU = len(UNITS)
        unit_of = {unit: u for u, unit in enumerate(UNITS)}
        PIECES = [(2 * INTER, P)] * DT + [(DM, rows) for _, rows in INTER_TILES]
        NP = len(PIECES)
        IT = len(INTER_TILES)
        UP, DOWN = range(DT), range(DT, NP)
        pieces_of_step = []
        for e in range(0, NE, 2):
            pieces_of_step += [[(e + 1, p) for p in UP[2:]] + [(e, p) for p in DOWN],
                               [(e + 1, p) for p in DOWN] + [(e + 2, p) for p in UP[:2]],
                               [(e + 2, p) for p in UP[2:]] + [(e + 3, p) for p in UP[:2]]]
        pieces = [piece for step in pieces_of_step for piece in step]
        NQ = len(pieces)
        EARLY = [q for q in range(NQ) if pieces[q][0] >= NE]
        assert EARLY == list(range(EARLY[0], NQ)) and len(pieces_of_step) == NU
        SLOTS_RAW = 8
        assert NQ % SLOTS_RAW == 0
        PER_SLOT = 16 * NQ // SLOTS_RAW
        shared_of_step = {0: range(0, DT), 1: range(DT, NP), 3: range(NP, NP + DT), 4: range(NP + DT, 2 * NP)}

        def piece_at(n, p):
            return pieces.index((n, p)) if (n, p) in pieces else pieces.index((n + NE, p)) - NQ

        raw = sb("w_raw4", [P, SLOTS_RAW, 2 * INTER])
        s_raw = sb("s_raw", [P, 2, 2 * INTER])
        up_w = [sb(f"up_{n}", [P, 2, DT, 2 * INTER], F32R) for n in ("hi", "lo")]
        down_w = [sb(f"down_{n}", [P, 2, IT, DM], F32R) for n in ("hi", "lo")]
        s_up = [sb(f"s_up_{n}", [P, SHARED_PARTS, DT, 2 * INTER], F32R) for n in ("hi", "lo")]
        s_down = [sb(f"s_down_{n}", [P, SHARED_PARTS, IT, DM], F32R) for n in ("hi", "lo")]
        rows_in = sb("rows_in", [P, 2, DM])
        eT = [sb(f"eT_{n}", [P, 2, DT * P], F32R) for n in ("hi", "lo")]
        sT = sb("sT", [P, 2, 2, DT * P], F32R)
        act_sb = sb("act_sb", [P, 2, INTER])
        h_sb = sb("h_sb", [P, 2, INTER])
        hT = [sb(f"hT_{n}", [P, 2, IT * P], F32R) for n in ("hi", "lo")]
        y_sb = sb("y_sb", [P, 2, DM])
        ys_sb = sb("ys_sb", [P, 2, DM])
        ident = sb("ident4", [P, P])

        t_ps = ps("t4_ps", [P, 2, CHUNK])
        h_ps = ps("h_ps", [P, 2, 2, CHUNK])
        y_ps = ps("y_ps", [P, DM])
        ys_ps = ps("ys_ps", [P, DM])

        tjobs = []
        for u in range(NU):
            tjobs.append(("h", (u - 1) % NU))
            if u == 0 and UNITS[0][0] == "e":
                tjobs.append(("x", 0))
            if u + 1 < NU and UNITS[u + 1][0] == "e":
                tjobs.append(("x", u + 1))
        assert len(tjobs) % 2 == 0 and NU % 2 == 0 and NE % 2 == 0
        NT = len(tjobs)
        t_at = {job: n for n, job in enumerate(tjobs)}

        pool_step = sem("pool_step4")
        pool_const = sem("pool_const4")
        s_in = [sem(f"s_in{n}") for n in range(2)]
        s_hi = sem("s_hi")
        s_lo = sem("s_lo")
        raw_in = [sem(f"raw_in{n}") for n in range(SLOTS_RAW)]
        w_hi = sem("w_hi")
        w_lo = sem("w_lo")
        rows_loaded = [sem(f"rows_loaded{n}") for n in range(2)]
        sT_loaded = [sem(f"sT_loaded{n}") for n in range(2)]
        t_ready = sem("t4_ready")
        t_hi = sem("t4_hi")
        t_lo = sem("t4_lo")
        up_ready = sem("up_ready")
        silu_ready = sem("silu_ready")
        h_ready = sem("h_ready")
        down_ready = sem("down_ready")
        y_read = sem("y_read")
        x1_loaded = [sem(f"x1_loaded{n}") for n in range(2)]
        ys_read = sem("ys_read")
        y_stored = [sem(f"y_stored{n}") for n in range(2)]
        ys_stored = [sem(f"ys_stored{n}") for n in range(2)]
        block = ctx.enter_context(nc.Block())

        def job_before(n):
            return n == 0

        def dst_of(part, n, p, up, down):
            rows = PIECES[p][1]
            return up[part][:, n, p, :] if p < DT else down[part][0:rows, n, p - DT, :]

        def weights(up_src, down_src, p):
            rows = PIECES[p][1]
            if p < DT:
                return up_src[:, :, p, :].rearrange("a p n -> (a p) n")
            first = INTER_TILES[p - DT][0]
            return down_src[:, first:first + rows, :].rearrange("a p n -> (a p) n")

        def raw_of(buffer, slot, p):
            cols, rows = PIECES[p]
            return buffer[0:rows, slot, 0:cols]

        @block.gpsimd
        def _(pool):
            nc.gpsimd.memset(ident[:], 0.0).then_inc(pool_step, 1)
            pool.wait_ge(pool_step, 1)
            nc.gpsimd.affine_select(out=ident[:], in_=ident[:], compare_op=ALU.not_equal, fill=1.0,
                                    base=0, pattern=[[-1, P]], channel_multiplier=1).then_inc(pool_const, 1)
            for k in range(SHARED_PARTS * NP):
                half, p = k // NP, k % NP
                if k >= 2:
                    pool.wait_ge(s_lo, k - 1)
                pool.dma_start(raw_of(s_raw, k % 2, p), weights(s13[half:half + 1], s2[half:half + 1], p)
                               ).then_inc(s_in[k % 2], 16)

        @block.sync
        def _(sp):
            for slot in range(SLOTS_RAW):
                sp.sem_inc(raw_in[slot], PER_SLOT - 16 * len([q for q in EARLY if q % SLOTS_RAW == slot]))

            def load_piece(e, q):
                p = pieces[q][1]
                sp.dma_start(raw_of(raw, q % SLOTS_RAW, p), weights(w13[bass.ds(e, 1)], w2[bass.ds(e, 1)], p)
                             ).then_inc(raw_in[q % SLOTS_RAW], 16)

            def load_rows(i, n):
                back = t_at["x", unit_of["e", (n - 2) % NE]] - (NT if n < 2 else 0)
                sp.wait_ge(t_ready, after(i, NT, back + 1))
                e = (i * NE + n) % EXPERTS if n == NE else i * NE + n
                sp.dma_start(rows_in[:, n % 2], gathered_x[bass.ds(e, 1)].rearrange("a p n -> (a p) n")
                             ).then_inc(rows_loaded[n % 2], 16)

            sp.dma_start(rows_in[:, 0], gathered_x[0]).then_inc(rows_loaded[0], 16)
            for q in EARLY:
                load_piece(pieces[q][0] - NE, q)
            with sp.Fori(0, BODIES) as i:
                for u, (kind, n) in enumerate(UNITS):
                    if u + 1 == NU or UNITS[u + 1][0] == "e":
                        load_rows(i, NE if u + 1 == NU else UNITS[u + 1][1])
                    if kind == "s" and n % 2 == 0:
                        s = n // 2
                        back = unit_of["s", (2 * s - 3) % NS] - (NU if s < 2 else 0)
                        sp.wait_ge(up_ready, after(i, NU, back + 1))
                        for part in range(2):
                            sp.dma_start(sT[:, s % 2, part].bitcast(F32),
                                         x1T_parts[bass.ds(i * (NS // 2) + s, 1), part].rearrange("a p n -> (a p) n")
                                         ).then_inc(sT_loaded[s % 2], 16)
                        sp.wait_ge(ys_stored[s % 2], after(i, 16 * NS // 4, 16 * (s // 2)))
                        t = i * (NS // 2) + s
                        sp.dma_start(ys_sb[:, s % 2], x1_dram[bass.ds(t * P, P)]).then_inc(x1_loaded[s % 2], 16)
                    for piece in pieces_of_step[u]:
                        q = pieces.index(piece)
                        sp.wait_ge(w_lo, after(i, NQ, q - SLOTS_RAW + 1))
                        load_piece((i * NE + piece[0]) % EXPERTS if piece[0] >= NE else i * NE + piece[0], q)
            for slot in range(SLOTS_RAW):
                sp.wait_ge(raw_in[slot], PER_SLOT * (BODIES + 1))
            sp.wait_ge(rows_loaded[0], 16 * (EXPERTS // 2 + 1))

        @block.scalar
        def _(act):
            act.sem_inc(w_hi, NQ - len(EARLY))
            act.sem_inc(y_read, NE)
            for n in range(2):
                act.sem_inc(y_stored[n], 16 * NE // 2)
                act.sem_inc(ys_stored[n], 16 * NS // 4)

            def split_piece(i, q):
                n, p = pieces[q]
                back = unit_of["e", (n - 2) % NE] - (NU if n < 2 else 0)
                act.wait_ge(up_ready if p < DT else down_ready, after(i, NU, back + 1))
                act.wait_ge(raw_in[q % SLOTS_RAW], after(i, PER_SLOT, 16 * (q // SLOTS_RAW) + 16))
                nc.scalar.activation(dst_of(0, n % 2, p, up_w, down_w), raw_of(raw, q % SLOTS_RAW, p),
                                     ACT.Copy).then_inc(w_hi, 1)

            def split_shared(k):
                half, p = k // NP, k % NP
                act.wait_ge(s_in[k % 2], 16 * (k // 2) + 16)
                nc.scalar.activation(dst_of(0, half, p, s_up, s_down), raw_of(s_raw, k % 2, p),
                                     ACT.Copy).then_inc(s_hi, 1)

            def turned(i, job):
                n = t_at[job]
                act.wait_ge(t_ready, after(i, NT, n + 1))
                u = job[1]
                if job[0] == "x":
                    e = UNITS[u][1]
                    back = unit_of["e", (e - 2) % NE] - (NU if e < 2 else 0)
                    act.wait_ge(up_ready, after(i, NU, back + 1))
                    nc.scalar.activation(eT[0][:, e % 2], t_ps[:, n % 2], ACT.Copy).then_inc(t_hi, 1)
                else:
                    v = (u - 2) - (NU if job_before(n) else 0)
                    act.wait_ge(down_ready, after(i, NU, v + 1))
                    nc.scalar.activation(hT[0][:, u % 2, 0:2 * P], t_ps[:, n % 2, 0:2 * P], ACT.Copy)
                    nc.scalar.activation(hT[0][0:96, u % 2, 2 * P:3 * P], t_ps[0:96, n % 2, 2 * P:3 * P],
                                         ACT.Copy).then_inc(t_hi, 1)

            def result(i, u, wrapped):
                kind, n = UNITS[u]
                if kind == "s" and n % 2 == 0:
                    return
                if kind == "e":
                    act.wait_ge(down_ready, after(i, NU, u + 1 - (NU if wrapped else 0)))
                    per = 16 * NE // 2
                    act.wait_ge(y_stored[n % 2], after(i, per, 16 * (n // 2) - (per if wrapped else 0)))
                    nc.scalar.activation(y_sb[:, n % 2], y_ps[:], ACT.Copy).then_inc(y_read, 1)
                    act.wait_ge(y_read, after(i, NE, n + 1 - (NE if wrapped else 0)))
                    e = i * NE + (n - (NE if wrapped else 0))
                    act.dma_start(y_dram[bass.ds(e, 1)].rearrange("a p n -> (a p) n"), y_sb[:, n % 2]
                                  ).then_inc(y_stored[n % 2], 16)
                else:
                    s = n // 2
                    act.wait_ge(ys_read, after(i, NS // 2, s + 1 - (NS // 2 if wrapped else 0)))
                    t = i * (NS // 2) + (s - (NS // 2 if wrapped else 0))
                    act.dma_start(base_dram[bass.ds(t * P, P)], ys_sb[:, s % 2]).then_inc(ys_stored[s % 2], 16)

            def body(i, first):
                for u, (kind, n) in enumerate(UNITS):
                    if not (first and u == 0):
                        turned(i, ("h", (u - 1) % NU))
                    if u == 0 and kind == "e":
                        turned(i, ("x", 0))
                    if first and u == 0:
                        for q in EARLY[DT:]:
                            split_piece(-1, q)
                    if not (first and u < 2):
                        result(i, (u - 2) % NU, u < 2)
                    mine = [pieces.index(piece) for piece in pieces_of_step[u]]
                    for q in mine[:3]:
                        split_piece(i, q)
                    act.wait_ge(up_ready, after(i, NU, u + 1))
                    act.wait_ge(h_ready, after(i, NU, u - 1))
                    nc.scalar.activation(act_sb[:, u % 2], h_ps[:, u % 2, 0, 0:INTER], ACT.Silu).then_inc(silu_ready, 1)
                    if u + 1 < NU and UNITS[u + 1][0] == "e":
                        turned(i, ("x", u + 1))
                    for q in mine[3:]:
                        split_piece(i, q)
                    if first:
                        for k in shared_of_step.get(u, ()):
                            split_shared(k)

            for q in EARLY[:DT]:
                split_piece(-1, q)
            body(0, True)
            with act.Fori(1, BODIES) as i:
                body(i, False)
            turned(BODIES, ("h", NU - 1))
            result(BODIES, NU - 2, True)
            result(BODIES, NU - 1, True)
            for n in range(2):
                act.wait_ge(y_stored[n], (16 * NE // 2) * (BODIES + 1))
                act.wait_ge(ys_stored[n], (16 * NS // 4) * (BODIES + 1))

        @block.vector
        def _(dve):
            dve.sem_inc(w_lo, NQ - len(EARLY))
            dve.sem_inc(t_lo, NT)
            dve.sem_inc(h_ready, NU)
            dve.sem_inc(ys_read, NS // 2)

            def shared_result(i, u, wrapped):
                kind, n = UNITS[u]
                if kind == "e" or n % 2 == 0:
                    return
                s = n // 2
                per = 16 * NS // 4
                back = per if wrapped else 0
                dve.wait_ge(down_ready, after(i, NU, u + 1 - (NU if wrapped else 0)))
                dve.wait_ge(x1_loaded[s % 2], i * per + (16 * (s // 2) + 16 - back))
                nc.vector.tensor_tensor(ys_sb[:, s % 2], ys_ps[:], ys_sb[:, s % 2], ALU.add).then_inc(ys_read, 1)

            def split_piece(i, q):
                n, p = pieces[q]
                dve.wait_ge(w_hi, after(i, NQ, q + 1))
                nc.vector.tensor_tensor(dst_of(1, n % 2, p, up_w, down_w), raw_of(raw, q % SLOTS_RAW, p),
                                        dst_of(0, n % 2, p, up_w, down_w).bitcast(F32),
                                        ALU.subtract).then_inc(w_lo, 1)

            def split_shared(k):
                half, p = k // NP, k % NP
                dve.wait_ge(s_hi, k + 1)
                nc.vector.tensor_tensor(dst_of(1, half, p, s_up, s_down), raw_of(s_raw, k % 2, p),
                                        dst_of(0, half, p, s_up, s_down).bitcast(F32),
                                        ALU.subtract).then_inc(s_lo, 1)

            def turned(i, job):
                n = t_at[job]
                dve.wait_ge(t_hi, i * NT + n)
                u = job[1]
                if job[0] == "x":
                    e = UNITS[u][1]
                    nc.vector.tensor_tensor(eT[1][:, e % 2], t_ps[:, n % 2], eT[0][:, e % 2].bitcast(F32),
                                            ALU.subtract).then_inc(t_lo, 1)
                else:
                    nc.vector.tensor_tensor(hT[1][:, u % 2, 0:2 * P], t_ps[:, n % 2, 0:2 * P],
                                            hT[0][:, u % 2, 0:2 * P].bitcast(F32), ALU.subtract)
                    nc.vector.tensor_tensor(hT[1][0:96, u % 2, 2 * P:3 * P], t_ps[0:96, n % 2, 2 * P:3 * P],
                                            hT[0][0:96, u % 2, 2 * P:3 * P].bitcast(F32),
                                            ALU.subtract).then_inc(t_lo, 1)

            def body(i, first):
                for u, (kind, n) in enumerate(UNITS):
                    if not (first and u == 0):
                        turned(i, ("h", (u - 1) % NU))
                    if u == 0 and kind == "e":
                        turned(i, ("x", 0))
                    if first and u == 0:
                        for q in EARLY[DT:]:
                            split_piece(-1, q)
                    if not (first and u < 2):
                        shared_result(i, (u - 2) % NU, u < 2)
                    mine = [pieces.index(piece) for piece in pieces_of_step[u]]
                    for q in mine[:3]:
                        split_piece(i, q)
                    dve.wait_ge(silu_ready, i * NU + (u + 1))
                    job = t_at["h", (u - 2) % NU]
                    if u >= 2:
                        dve.wait_ge(t_ready, after(i, NT, job + 1))
                    elif u == 1:
                        dve.wait_ge(t_ready, after(i, NT, 1))
                    else:
                        dve.wait_ge(t_ready, after(i, NT, t_at["h", NU - 2] + 1 - NT))
                    nc.vector.tensor_tensor(h_sb[:, u % 2], act_sb[:, u % 2], h_ps[:, u % 2, 1, 0:INTER],
                                            ALU.mult).then_inc(h_ready, 1)
                    if u + 1 < NU and UNITS[u + 1][0] == "e":
                        turned(i, ("x", u + 1))
                    for q in mine[3:]:
                        split_piece(i, q)
                    if first:
                        for k in shared_of_step.get(u, ()):
                            split_shared(k)

            for q in EARLY[:DT]:
                split_piece(-1, q)
            body(0, True)
            with dve.Fori(1, BODIES) as i:
                body(i, False)
            turned(BODIES, ("h", NU - 1))
            shared_result(BODIES, NU - 1, True)

        @block.tensor
        def _(pe):
            pe.sem_inc(t_ready, NT + 1)
            pe.sem_inc(up_ready, NU)
            pe.sem_inc(down_ready, NU)
            pe.wait_ge(pool_const, 1)

            def turn(i, job):
                n = t_at[job]
                pe.wait_ge(t_lo, after(i, NT, n - 2))
                u = job[1]
                if job[0] == "x":
                    e = UNITS[u][1]
                    pe.wait_ge(rows_loaded[e % 2], i * (16 * NE // 2) + (16 * (e // 2) + 16))
                    for d in range(DT):
                        mark = nc.tensor.transpose(t_ps[:, n % 2, d * P:(d + 1) * P],
                                                   rows_in[:, e % 2, d * P:(d + 1) * P], ident[:])
                else:
                    pe.wait_ge(h_ready, after(i, NU, u + 1 - (NU if job_before(n) else 0)))
                    for k, (first, rows) in enumerate(INTER_TILES):
                        mark = nc.tensor.transpose(t_ps[0:rows, n % 2, k * P:(k + 1) * P],
                                                   h_sb[:, u % 2, first:first + rows], ident[:])
                mark.then_inc(t_ready, 1)

            def up(i, u, first_body):
                kind, n = UNITS[u]
                pe.wait_ge(h_ready, after(i, NU, u - 1))
                if kind == "e":
                    pe.wait_ge(t_lo, after(i, NT, t_at["x", u]))
                    pe.wait_ge(w_lo, after(i, NQ, piece_at(n, DT - 1) + 1))
                    lhs = [eT[m][:, n % 2] for m in range(2)]
                    rhs = [up_w[m][:, n % 2] for m in range(2)]
                else:
                    s = n // 2
                    pe.wait_ge(sT_loaded[s % 2], i * (32 * NS // 4) + (32 * (s // 2) + 32))
                    if first_body:
                        pe.wait_ge(s_lo, NP * (n % 2) + DT)
                    lhs = [sT[:, s % 2, m] for m in range(2)]
                    rhs = [s_up[m][:, n % 2] for m in range(2)]
                for k in range(2):
                    for d in range(DT):
                        for a, b in PASSES:
                            mark = nc.tensor.matmul(h_ps[:, u % 2, k, 0:INTER], lhs[a][:, d * P:(d + 1) * P],
                                                    rhs[b][:, d, k * INTER:(k + 1) * INTER],
                                                    start=d == 0 and (a, b) == PASSES[0],
                                                    stop=d == DT - 1 and (a, b) == PASSES[-1])
                mark.then_inc(up_ready, 1)

            def down(i, u, wrapped, first_body=False):
                kind, n = UNITS[u]
                pe.wait_ge(t_lo, after(i, NT, t_at["h", u]))
                if kind == "e":
                    pe.wait_ge(y_read, after(i, NE, n - (NE if wrapped else 0)))
                    pe.wait_ge(w_lo, after(i, NQ, piece_at(n, NP - 1) + 1 - (NQ if wrapped else 0)))
                    dst, rhs, opens, closes = y_ps, [down_w[m][:, n % 2] for m in range(2)], True, True
                else:
                    s = n // 2
                    pe.wait_ge(ys_read, after(i, NS // 2, s - (NS // 2 if wrapped else 0)))
                    if first_body:
                        pe.wait_ge(s_lo, NP * (n % 2 + 1))
                    dst, rhs, opens, closes = ys_ps, [s_down[m][:, n % 2] for m in range(2)], n % 2 == 0, n % 2 == 1
                for k, (first, rows) in enumerate(INTER_TILES):
                    for a, b in PASSES:
                        mark = nc.tensor.matmul(dst[:], hT[a][0:rows, u % 2, k * P:(k + 1) * P],
                                                rhs[b][0:rows, k],
                                                start=opens and k == 0 and (a, b) == PASSES[0],
                                                stop=closes and k == IT - 1 and (a, b) == PASSES[-1])
                mark.then_inc(down_ready, 1)

            def body(i, first):
                for u, (kind, n) in enumerate(UNITS):
                    if not (first and u == 0):
                        turn(i, ("h", (u - 1) % NU))
                    if u == 0 and kind == "e":
                        turn(i, ("x", 0))
                    up(i, u, first)
                    if u + 1 < NU and UNITS[u + 1][0] == "e":
                        turn(i, ("x", u + 1))
                    if not (first and u == 0):
                        down(i, (u - 1) % NU, u == 0, first)

            body(0, True)
            with pe.Fori(1, BODIES) as i:
                body(i, False)
            turn(BODIES, ("h", NU - 1))
            down(BODIES, NU - 1, True)


def combine(nc, y_dram, base_dram, out_rows, routes):
    slot_of, gate_of = routes
    with ExitStack() as ctx:
        def sb(name, shape, dt=F32):
            return ctx.enter_context(nc.sbuf_tensor(name, shape, dt))

        def sem(name):
            return ctx.enter_context(nc.semaphore(name))

        LOOPS = TILES // NB - 2
        LN_STEPS = 9
        rows = sb("rows", [P, NB, TOPK, DM])
        base = sb("base", [P, NB, DM])
        acc = sb("acc", [P, 2, 2, DM])
        centred = sb("centred", [P, DM])
        y = sb("yc", [P, NB, DM])
        slot = sb("slotc", [P, NB, TOPK], U32)
        gate = sb("gatec", [P, NB, TOPK])
        stats = sb("statsc", [P, 6])
        mv = sb("mvc", [P, 2, 2])
        neg_mean = sb("neg_meanc", [P, 2])
        var = sb("varc", [P, 2])
        root = sb("rootc", [P, 2])
        guess = sb("guessc", [P, 2])
        newton_part = sb("newton_partc", [P, 3])
        inverse = sb("inversec", [P, 2])
        eps = sb("epsc", [P, 1])

        waited = sem("waited5")
        eps_ready = sem("eps_ready")
        cleared = sem("cleared")
        slots_ready = sem("slots_ready")
        gathered = [sem(f"gathered{n}") for n in range(NB)]
        loaded = [sem(f"loaded{n}") for n in range(NB)]
        sum_chain = sem("sum_chain")
        ln_chain = sem("ln_chain5")
        rooted = sem("rooted5")
        centred_ready = sem("centred_ready")
        y_ready = sem("y_ready")
        stored = [sem(f"stored{n}") for n in range(NB)]
        block = ctx.enter_context(nc.Block())

        @block.gpsimd
        def _(pool):
            flat = y_dram.rearrange("e c d -> (e c) d")
            last_slot = nc.gpsimd.to_reg(SLOTS - 1)
            def gather(i, k):
                if exists(i, k - NB):
                    pool.wait_ge(sum_chain, done(i, k - NB, TOPK))
                wait_apart(pool, waited, slots_ready, done(i, k))
                for n in range(TOPK):
                    nc.gpsimd.indirect_dma_start(
                        rows[:, k % NB, n], None, flat,
                        bass.IndirectOffsetOnAxis(ap=slot[:, k % NB, n:n + 1], axis=0),
                        bounds_check=last_slot, oob_is_err=False).then_inc(gathered[k % NB], 16)

            for k in range(NB):
                pool.wait_ge(cleared, k + 1)
                gather(0, k)
            with pool.Fori(0, TILES // NB - 1) as i:
                for k in range(NB, 2 * NB):
                    gather(i, k)

        @block.sync
        def _(sp):
            def load(i, k):
                if exists(i, k - NB):
                    sp.wait_ge(sum_chain, done(i, k - NB, TOPK))
                sp.dma_start(base[:, k % NB], base_dram[bass.ds((i * NB + k) * P, P)]).then_inc(loaded[k % NB], 16)

            for k in range(NB):
                load(0, k)
            with sp.Fori(0, TILES // NB - 1) as i:
                for k in range(NB, 2 * NB):
                    load(i, k)

        @block.scalar
        def _(act):
            act.wait_ge(eps_ready, 1)

            def step(i, k):
                t = i * NB + k
                b = k % 2
                act.wait_ge(ln_chain, done(i, k, LN_STEPS, 2))
                nc.scalar.activation(root[:, b:b + 1], mv[:, b, 1:2], ACT.Sqrt, bias=eps[:]).then_inc(rooted, 1)
                act.wait_ge(ln_chain, done(i, k, LN_STEPS, 4))
                nc.scalar.activation(centred[:], acc[:, b, (TOPK - 1) % 2], ACT.Identity,
                                     bias=neg_mean[:, b:b + 1]).then_inc(centred_ready, 1)
                act.wait_ge(ln_chain, done(i, k, LN_STEPS))
                act.wait_ge(centred_ready, done(i, k))
                if exists(i, k - NB):
                    act.wait_ge(stored[k % NB], i * 16 + 16 * (k // NB))
                nc.scalar.activation(y[:, k % NB], centred[:], ACT.Copy, scale=inverse[:, b:b + 1]).then_inc(y_ready, 1)
                act.wait_ge(y_ready, done(i, k))
                act.dma_start(out_rows[bass.ds(t * P, P)], y[:, k % NB]).then_inc(stored[k % NB], 16)

            for k in range(NB):
                step(0, k)
            with act.Fori(0, TILES // NB - 1) as i:
                for k in range(NB, 2 * NB):
                    step(i, k)
            for n in range(NB):
                act.wait_ge(stored[n], 16 * TILES // NB)

        @block.vector
        def _(dve):
            nc.vector.memset(eps[:], EPS).then_inc(eps_ready, 1)

            def places(i, k):
                t = i * NB + k
                nc.vector.tensor_copy(gate[:, k % NB], gate_of[:, bass.ds(t, 1)].rearrange("p a k -> p (a k)"))
                nc.vector.tensor_copy(slot[:, k % NB], slot_of[:, bass.ds(t, 1)].rearrange("p a k -> p (a k)")
                                      ).then_inc(slots_ready, 1)

            def add(i, k, n):
                dst = acc[:, k % 2, n % 2]
                if n == 0:
                    dve.wait_ge(slots_ready, done(i, k))
                    dve.wait_ge(loaded[k % NB], i * 16 + 16 * (k // NB + 1))
                    dve.wait_ge(gathered[k % NB], i * (16 * TOPK) + 16 * TOPK * (k // NB + 1))
                    if exists(i, k - 2):
                        dve.wait_ge(y_ready, done(i, k - 2))
                    before = base[:, k % NB]
                else:
                    dve.wait_ge(sum_chain, done(i, k, TOPK, n))
                    before = acc[:, k % 2, (n - 1) % 2]
                nc.vector.scalar_tensor_tensor(dst, rows[:, k % NB, n], gate[:, k % NB, n:n + 1], before,
                                               ALU.mult, ALU.add).then_inc(sum_chain, 1)

            def normalise(i, k, part):
                b = k % 2

                def after_step(n):
                    dve.wait_ge(ln_chain, done(i, k, LN_STEPS, n))

                if part == 0:
                    wait_apart(dve, waited, sum_chain, done(i, k, TOPK))
                    nc.vector.bn_stats(stats[:], acc[:, b, (TOPK - 1) % 2]).then_inc(ln_chain, 1)
                if part == 1:
                    wait_apart(dve, waited, ln_chain, done(i, k, LN_STEPS, 1))
                    nc.vector.bn_aggr(mv[:, b], stats[:]).then_inc(ln_chain, 1)
                if part == 2:
                    after_step(2)
                    nc.vector.tensor_scalar(neg_mean[:, b:b + 1], mv[:, b, 0:1], -1.0, None, ALU.mult
                                            ).then_inc(ln_chain, 1)
                    nc.vector.tensor_scalar(var[:, b:b + 1], mv[:, b, 1:2], EPS, None, ALU.add
                                            ).then_inc(ln_chain, 1)
                if part == 3:
                    dve.wait_ge(rooted, done(i, k))
                    nc.vector.reciprocal(guess[:, b:b + 1], root[:, b:b + 1]).then_inc(ln_chain, 1)
                    after_step(5)
                    nc.vector.tensor_tensor(newton_part[:, 0:1], guess[:, b:b + 1], guess[:, b:b + 1], ALU.mult
                                            ).then_inc(ln_chain, 1)
                if part == 4:
                    after_step(6)
                    nc.vector.scalar_tensor_tensor(newton_part[:, 1:2], newton_part[:, 0:1], -0.5, var[:, b:b + 1],
                                                   ALU.mult, ALU.mult).then_inc(ln_chain, 1)
                    after_step(7)
                    nc.vector.tensor_scalar(newton_part[:, 2:3], newton_part[:, 1:2], 1.5, None, ALU.add
                                            ).then_inc(ln_chain, 1)
                if part == 5:
                    after_step(8)
                    nc.vector.tensor_tensor(inverse[:, b:b + 1], newton_part[:, 2:3], guess[:, b:b + 1], ALU.mult
                                            ).then_inc(ln_chain, 1)

            def step(i, k):
                for n in range(TOPK):
                    if exists(i, k):
                        add(i, k, n)
                    if exists(i, k - 1):
                        normalise(i, k - 1, n)
                    if n == 0 and exists(i, k - 1) and exists(i, k + NB - 1):
                        places(i, k + NB - 1)

            for k in range(NB):
                places(0, k)
                nc.vector.memset(rows[:, k], 0.0).then_inc(cleared, 1)
            for k in range(NB):
                step(0, k)
            with dve.Fori(0, LOOPS) as i:
                for k in range(NB, 2 * NB):
                    step(i, k)
            for k in range(TILES - NB, TILES + 1):
                step(0, k)


def post_ln_layer(nc, xT, x_rows, w_qkv, w_o, gate_w, w13, w2, s13, s2, out):
    def dram(name, shape):
        return nc.dram_tensor(name, shape, F32, kind="Internal").ap()

    x_parts = dram("x_parts", [CHUNKS, 2, P, DT * CHUNK])
    z_dram = dram("z_dram", [TILES, P, HEADS, P])
    gathered_x = dram("gathered_x", [EXPERTS, CAPACITY, DM])
    x1_dram = dram("x1_dram", [SEQ, DM])
    x1T_parts = dram("x1T_parts", [TILES, 2, P, DT * P])
    y_dram = dram("y_dram", [EXPERTS, CAPACITY, DM])
    base_dram = dram("base_dram", [SEQ, DM])
    with (
        nc.sbuf_tensor("slot_of", [P, TILES, TOPK], U32) as slot_of,
        nc.sbuf_tensor("gate_of", [P, TILES, TOPK], F32) as gate_of,
    ):
        attention(nc, xT, x_parts, w_qkv, z_dram, gathered_x)
        project_and_route(nc, z_dram, w_o, gate_w, x_rows, x1_dram, x1T_parts, gathered_x, (slot_of, gate_of))
        experts(nc, gathered_x, x1_dram, x1T_parts, w13, w2, s13, s2, y_dram, base_dram)
        combine(nc, y_dram, base_dram, out, (slot_of, gate_of))


def lay_out(name, a, np):
    a = {k: np.asarray(v) for k, v in a.items()}
    if name == "x_rows":
        return a["L0_attn_x"].reshape(SEQ, DM)
    if name == "xT":
        return a["L0_attn_x"].reshape(CHUNKS, CHUNK, DT, P).transpose(0, 3, 2, 1).reshape(CHUNKS, P, DT * CHUNK)
    if name == "w_qkv":
        qk = np.stack([a["L0_attn_W_Q"], a["L0_attn_W_K"]], 1).reshape(PAIRS, 4 * DH, DM)
        v = a["L0_attn_W_V"].reshape(PAIRS, 2 * DH, DM)
        return np.concatenate([qk, v], 1).transpose(0, 2, 1).reshape(PAIRS, DT, P, 6 * DH)
    if name == "w_o":
        return a["L0_attn_W_O"].reshape(DM, HEADS, DH).transpose(2, 1, 0)
    if name == "gate_w":
        return a["L0_ffn_gate_w"].reshape(EXPERTS, DT, P).transpose(2, 1, 0)
    if name == "w13":
        w = np.concatenate([a["L0_ffn_w1"], a["L0_ffn_w3"]], 1)
        return w.reshape(EXPERTS, 2 * INTER, DT, P).transpose(0, 3, 2, 1)
    if name == "w2":
        return a["L0_ffn_w2"].transpose(0, 2, 1)
    if name == "s13":
        w = np.concatenate([a[n].reshape(SHARED_PARTS, INTER, DM) for n in ("L0_ffn_sw1", "L0_ffn_sw3")], 1)
        return w.reshape(SHARED_PARTS, 2 * INTER, DT, P).transpose(0, 3, 2, 1)
    if name == "s2":
        return a["L0_ffn_sw2"].T.reshape(SHARED_PARTS, INTER, DM)


def kernel(**inputs):
    import numpy as _np
    import concourse.bacc as _bacc
    from concourse import mybir as _mybir
    from concourse.bass_utils import run_bass_kernel_spmd as _run

    nc = _bacc.Bacc("TRN2", target_bir_lowering=False, num_devices=1)
    arrays, args = {}, []
    for name in ("xT", "x_rows", "w_qkv", "w_o", "gate_w", "w13", "w2", "s13", "s2"):
        a = _np.ascontiguousarray(lay_out(name, inputs, _np))
        arrays[f"in_{name}"] = a
        args.append(nc.dram_tensor(f"in_{name}", a.shape, _mybir.dt.from_np(a.dtype), kind="ExternalInput").ap())
    out = nc.dram_tensor("out", (SEQ, DM), F32, kind="ExternalOutput").ap()
    post_ln_layer(nc, *args, out)
    r = _run(nc, [arrays], core_ids=[0])
    return r.results[0]["out"].reshape(1, SEQ, DM)
```
